# Optimizing a Trainium2 kernel written in Bass

```python
import numpy as np
import jax
import jax.numpy as jnp

def _softmax(x, axis=-1):
    return jax.nn.softmax(x, axis=axis)

def _gelu(x):
    return jax.nn.gelu(x, approximate=True)

def _silu(x):
    return jax.nn.silu(x)

def _sigmoid(x):
    return jax.nn.sigmoid(x)

def _layernorm(x, axis=-1, eps=1e-05):
    m = jnp.mean(x, axis=axis, keepdims=True)
    v = jnp.var(x, axis=axis, keepdims=True)
    return (x - m) / jnp.sqrt(v + eps)

def _scatter_add(tgt, idx, src, axis=0):
    return tgt.at[idx].add(src)

def _segment_sum(src, seg, n):
    return jax.ops.segment_sum(src, seg, n)
kernel_name = 'mk_prb_d2_jaxref_r8_6c1112'

def setup_inputs(seed: int=0):
    np.random.seed(seed)
    _w = jnp.asarray

    def _L0_attn_setup():
        import jax, jax.numpy as jnp
        import numpy as np
        B, L, D, H = (8, 256, 128, 16)
        HD = D // H
        K = 4
        EPS = 1e-06

        def _short_conv(x, w, b):
            xp = jnp.pad(x, ((0, 0), (K - 1, 0), (0, 0)))
            y = b
            for i in range(K):
                y = y + w[:, i] * xp[:, i:i + x.shape[1], :]
            return y

        def _delta_rule(q, k, v, beta):
            qT = jnp.moveaxis(q, 1, 0)
            kT = jnp.moveaxis(k, 1, 0)
            vT = jnp.moveaxis(v, 1, 0)
            bT = jnp.moveaxis(beta, 1, 0)

            def step(S, inp):
                q_t, k_t, v_t, b_t = inp
                pred = jnp.einsum('bhk,bhkv->bhv', k_t, S)
                S = S + b_t[..., None, None] * (k_t[..., None] * (v_t - pred)[..., None, :])
                o_t = jnp.einsum('bhk,bhkv->bhv', q_t, S)
                return (S, o_t)
            S0 = jnp.zeros((q.shape[0], H, HD, HD), q.dtype)
            _, o = jax.lax.scan(step, S0, (qT, kT, vT, bT))
            return jnp.moveaxis(o, 0, 1)

        def _rmsnorm(x, w):
            return x * jax.lax.rsqrt(jnp.mean(x * x, axis=-1, keepdims=True) + EPS) * w
        key = jax.random.key(seed)
        ks = jax.random.split(key, 12)
        s = 0.02
        inp = {'x': jax.random.normal(ks[0], (B, L, D), jnp.float32), 'Wq': jax.random.normal(ks[1], (D, D), jnp.float32) * s, 'bq': jnp.zeros((D,), jnp.float32), 'Wk': jax.random.normal(ks[2], (D, D), jnp.float32) * s, 'bk': jnp.zeros((D,), jnp.float32), 'Wv': jax.random.normal(ks[3], (D, D), jnp.float32) * s, 'bv': jnp.zeros((D,), jnp.float32), 'Wbeta': jax.random.normal(ks[4], (H, D), jnp.float32) * s, 'bbeta': jnp.zeros((H,), jnp.float32), 'Wo': jax.random.normal(ks[5], (D, D), jnp.float32) * s, 'bo': jnp.zeros((D,), jnp.float32), 'wq_conv': jax.random.normal(ks[6], (D, K), jnp.float32) * 0.2, 'bq_conv': jnp.zeros((D,), jnp.float32), 'wk_conv': jax.random.normal(ks[7], (D, K), jnp.float32) * 0.2, 'bk_conv': jnp.zeros((D,), jnp.float32), 'wv_conv': jax.random.normal(ks[8], (D, K), jnp.float32) * 0.2, 'bv_conv': jnp.zeros((D,), jnp.float32), 'norm_w': jnp.ones((HD,), jnp.float32)}
        return inp
    _L0_attn_in = _L0_attn_setup()

    def _L0_ffn_setup():
        import jax, jax.numpy as jnp
        import numpy as np
        B, S, D, F, E = (4, 256, 128, 512, 8)
        LN_EPS = 1e-05
        key = jax.random.key(seed)
        ks = jax.random.split(key, 6)
        sc = 0.02
        return {'x': jax.random.normal(ks[0], (B, S, D), dtype=jnp.float32), 'Wr': jax.random.normal(ks[1], (D, E), dtype=jnp.float32) * sc, 'br': jnp.zeros((E,), jnp.float32), 'ln_g': jnp.ones((D,), jnp.float32), 'ln_b': jnp.zeros((D,), jnp.float32), 'W1': jax.random.normal(ks[2], (E, D, F), dtype=jnp.float32) * sc, 'b1': jnp.zeros((E, F), jnp.float32), 'W2': jax.random.normal(ks[3], (E, F, D), dtype=jnp.float32) * sc, 'b2': jnp.zeros((E, D), jnp.float32)}
    _L0_ffn_in = _L0_ffn_setup()

    def _L1_attn_setup():
        import jax, jax.numpy as jnp
        import numpy as np
        B, L, D, S, K, FF = (2, 512, 128, 16, 3, 336)
        EPS = 1e-06

        def rmsnorm(x, w):
            var = jnp.mean(x * x, axis=-1, keepdims=True)
            return x * jax.lax.rsqrt(var + EPS) * w
        key = jax.random.key(seed)
        ks = jax.random.split(key, 12)
        return {'u': jax.random.normal(ks[0], (B, L, D), jnp.float32), 'pre_norm_w': jnp.ones((D,), jnp.float32), 'in_proj_w': jax.random.normal(ks[1], (3 * D, D), jnp.float32) * D ** (-0.5), 'short_w': jax.random.normal(ks[2], (3 * D, 1, K), jnp.float32) * 0.3, 'short_b': jax.random.normal(ks[3], (3 * D,), jnp.float32) * 0.02, 'log_poles': -(jax.random.uniform(ks[4], (D, S, 1), jnp.float32) * 0.3 + 0.001), 'residues': jax.random.normal(ks[5], (D, S), jnp.float32) * S ** (-0.5), 'D_skip': jax.random.normal(ks[6], (D,), jnp.float32) * 0.02, 'out_proj_w': jax.random.normal(ks[7], (D, D), jnp.float32) * D ** (-0.5), 'post_norm_w': jnp.ones((D,), jnp.float32), 'l1_w': jax.random.normal(ks[8], (FF, D), jnp.float32) * D ** (-0.5), 'l2_w': jax.random.normal(ks[9], (FF, D), jnp.float32) * D ** (-0.5), 'l3_w': jax.random.normal(ks[10], (D, FF), jnp.float32) * FF ** (-0.5)}
    _L1_attn_in = _L1_attn_setup()

    def _L1_ffn_setup():
        import jax, jax.numpy as jnp
        import numpy as np
        B, S, D_MODEL, D_FF, E, R, TOP_K = (4, 256, 128, 512, 8, 16, 2)
        key = jax.random.key(seed)
        ks = jax.random.split(key, 9)
        sd = 1.0 / np.sqrt(D_MODEL)
        return {'hidden_states': jax.random.normal(ks[0], (B, S, D_MODEL), jnp.float32), 'wi': jax.random.normal(ks[1], (D_FF, D_MODEL), jnp.float32) * sd, 'bi': jax.random.normal(ks[2], (D_FF,), jnp.float32) * 0.01, 'wo': jax.random.normal(ks[3], (D_MODEL, D_FF), jnp.float32) * (1.0 / np.sqrt(D_FF)), 'bo': jax.random.normal(ks[4], (D_MODEL,), jnp.float32) * 0.01, 'lora_A': jax.random.normal(ks[5], (E, R, D_MODEL), jnp.float32) * sd, 'lora_B': jax.random.normal(ks[6], (E, D_FF, R), jnp.float32) * 0.02, 'gate_w': jax.random.normal(ks[7], (E, D_MODEL), jnp.float32) * sd, 'gate_b': jax.random.normal(ks[8], (E,), jnp.float32) * 0.01}
    _L1_ffn_in = _L1_ffn_setup()
    _d = {'L0_attn_x': _L0_attn_in['x'], 'L0_attn_Wq': _L0_attn_in['Wq'], 'L0_attn_bq': _L0_attn_in['bq'], 'L0_attn_Wk': _L0_attn_in['Wk'], 'L0_attn_bk': _L0_attn_in['bk'], 'L0_attn_Wv': _L0_attn_in['Wv'], 'L0_attn_bv': _L0_attn_in['bv'], 'L0_attn_Wbeta': _L0_attn_in['Wbeta'], 'L0_attn_bbeta': _L0_attn_in['bbeta'], 'L0_attn_Wo': _L0_attn_in['Wo'], 'L0_attn_bo': _L0_attn_in['bo'], 'L0_attn_wq_conv': _L0_attn_in['wq_conv'], 'L0_attn_bq_conv': _L0_attn_in['bq_conv'], 'L0_attn_wk_conv': _L0_attn_in['wk_conv'], 'L0_attn_bk_conv': _L0_attn_in['bk_conv'], 'L0_attn_wv_conv': _L0_attn_in['wv_conv'], 'L0_attn_bv_conv': _L0_attn_in['bv_conv'], 'L0_attn_norm_w': _L0_attn_in['norm_w'], 'L0_ffn_Wr': _L0_ffn_in['Wr'], 'L0_ffn_br': _L0_ffn_in['br'], 'L0_ffn_ln_g': _L0_ffn_in['ln_g'], 'L0_ffn_ln_b': _L0_ffn_in['ln_b'], 'L0_ffn_W1': _L0_ffn_in['W1'], 'L0_ffn_b1': _L0_ffn_in['b1'], 'L0_ffn_W2': _L0_ffn_in['W2'], 'L0_ffn_b2': _L0_ffn_in['b2'], 'L1_attn_pre_norm_w': _L1_attn_in['pre_norm_w'], 'L1_attn_in_proj_w': _L1_attn_in['in_proj_w'], 'L1_attn_short_w': _L1_attn_in['short_w'], 'L1_attn_short_b': _L1_attn_in['short_b'], 'L1_attn_log_poles': _L1_attn_in['log_poles'], 'L1_attn_residues': _L1_attn_in['residues'], 'L1_attn_D_skip': _L1_attn_in['D_skip'], 'L1_attn_out_proj_w': _L1_attn_in['out_proj_w'], 'L1_attn_post_norm_w': _L1_attn_in['post_norm_w'], 'L1_attn_l1_w': _L1_attn_in['l1_w'], 'L1_attn_l2_w': _L1_attn_in['l2_w'], 'L1_attn_l3_w': _L1_attn_in['l3_w'], 'L1_ffn_wi': _L1_ffn_in['wi'], 'L1_ffn_bi': _L1_ffn_in['bi'], 'L1_ffn_wo': _L1_ffn_in['wo'], 'L1_ffn_bo': _L1_ffn_in['bo'], 'L1_ffn_lora_A': _L1_ffn_in['lora_A'], 'L1_ffn_lora_B': _L1_ffn_in['lora_B'], 'L1_ffn_gate_w': _L1_ffn_in['gate_w'], 'L1_ffn_gate_b': _L1_ffn_in['gate_b']}
    _x0 = _d['L0_attn_x']
    _d['L0_attn_x'] = jax.random.normal(jax.random.fold_in(jax.random.key(seed), 1), (4, 1024, 128), dtype=_x0.dtype)
    del _x0
    return _d

def reference(L0_attn_x, L0_attn_Wq, L0_attn_bq, L0_attn_Wk, L0_attn_bk, L0_attn_Wv, L0_attn_bv, L0_attn_Wbeta, L0_attn_bbeta, L0_attn_Wo, L0_attn_bo, L0_attn_wq_conv, L0_attn_bq_conv, L0_attn_wk_conv, L0_attn_bk_conv, L0_attn_wv_conv, L0_attn_bv_conv, L0_attn_norm_w, L0_ffn_Wr, L0_ffn_br, L0_ffn_ln_g, L0_ffn_ln_b, L0_ffn_W1, L0_ffn_b1, L0_ffn_W2, L0_ffn_b2, L1_attn_pre_norm_w, L1_attn_in_proj_w, L1_attn_short_w, L1_attn_short_b, L1_attn_log_poles, L1_attn_residues, L1_attn_D_skip, L1_attn_out_proj_w, L1_attn_post_norm_w, L1_attn_l1_w, L1_attn_l2_w, L1_attn_l3_w, L1_ffn_wi, L1_ffn_bi, L1_ffn_wo, L1_ffn_bo, L1_ffn_lora_A, L1_ffn_lora_B, L1_ffn_gate_w, L1_ffn_gate_b):

    def _L0_attn_ref(x, Wq, bq, Wk, bk, Wv, bv, Wbeta, bbeta, Wo, bo, wq_conv, bq_conv, wk_conv, bk_conv, wv_conv, bv_conv, norm_w):
        import jax, jax.numpy as jnp
        import numpy as np
        B, L, D, H = (8, 256, 128, 16)
        HD = D // H
        K = 4
        EPS = 1e-06

        def _short_conv(x, w, b):
            xp = jnp.pad(x, ((0, 0), (K - 1, 0), (0, 0)))
            y = b
            for i in range(K):
                y = y + w[:, i] * xp[:, i:i + x.shape[1], :]
            return y

        def _delta_rule(q, k, v, beta):
            qT = jnp.moveaxis(q, 1, 0)
            kT = jnp.moveaxis(k, 1, 0)
            vT = jnp.moveaxis(v, 1, 0)
            bT = jnp.moveaxis(beta, 1, 0)

            def step(S, inp):
                q_t, k_t, v_t, b_t = inp
                pred = jnp.einsum('bhk,bhkv->bhv', k_t, S)
                S = S + b_t[..., None, None] * (k_t[..., None] * (v_t - pred)[..., None, :])
                o_t = jnp.einsum('bhk,bhkv->bhv', q_t, S)
                return (S, o_t)
            S0 = jnp.zeros((q.shape[0], H, HD, HD), q.dtype)
            _, o = jax.lax.scan(step, S0, (qT, kT, vT, bT))
            return jnp.moveaxis(o, 0, 1)

        def _rmsnorm(x, w):
            return x * jax.lax.rsqrt(jnp.mean(x * x, axis=-1, keepdims=True) + EPS) * w
        Bx, Lx, Dx = x.shape
        k = _short_conv(x @ Wk.T + bk, wk_conv, bk_conv)
        q = _short_conv(x @ Wq.T + bq, wq_conv, bq_conv)
        v = _short_conv(x @ Wv.T + bv, wv_conv, bv_conv)
        beta = jax.nn.sigmoid(x @ Wbeta.T + bbeta)
        k = k.reshape(Bx, Lx, H, HD)
        q = q.reshape(Bx, Lx, H, HD)
        v = v.reshape(Bx, Lx, H, HD)
        v = jax.nn.silu(v)
        knorm = jnp.linalg.norm(k, axis=-1, keepdims=True)
        qnorm = jnp.linalg.norm(q, axis=-1, keepdims=True)
        k = k / (knorm + EPS)
        v = v / (knorm + EPS)
        q = q / (qnorm + EPS)
        o = _delta_rule(q, k, v, beta)
        o = _rmsnorm(o, norm_w)
        o = o.reshape(Bx, Lx, Dx)
        return o @ Wo.T + bo

    def _L0_ffn_ref(x, Wr, br, ln_g, ln_b, W1, b1, W2, b2):
        import jax, jax.numpy as jnp
        import numpy as np
        B, S, D, F, E = (4, 256, 128, 512, 8)
        LN_EPS = 1e-05
        tokens_shape = x.shape[:-1]
        xt = x.reshape(-1, x.shape[-1])
        router_logits = xt @ Wr + br
        router_probs = jax.nn.softmax(router_logits, axis=-1)
        gates = jnp.max(router_probs, axis=-1, keepdims=True)
        idx = jnp.argmax(router_probs, axis=-1)
        onehot = jax.nn.one_hot(idx, E, dtype=xt.dtype)
        mu = jnp.mean(xt, axis=-1, keepdims=True)
        var = jnp.mean(jnp.square(xt - mu), axis=-1, keepdims=True)
        xn = (xt - mu) * jax.lax.rsqrt(var + LN_EPS) * ln_g + ln_b
        h = jnp.einsum('te,td,edf->tf', onehot, xn, W1) + b1[idx]
        h = jax.nn.relu(h)
        y = jnp.einsum('te,tf,efd->td', onehot, h, W2) + b2[idx]
        y = y * gates
        return y.reshape(tokens_shape + (y.shape[-1],))

    def _L1_attn_ref(u, pre_norm_w, in_proj_w, short_w, short_b, log_poles, residues, D_skip, out_proj_w, post_norm_w, l1_w, l2_w, l3_w):
        import jax, jax.numpy as jnp
        import numpy as np
        B, L, D, S, K, FF = (2, 512, 128, 16, 3, 336)
        EPS = 1e-06

        def rmsnorm(x, w):
            var = jnp.mean(x * x, axis=-1, keepdims=True)
            return x * jax.lax.rsqrt(var + EPS) * w
        Lc = u.shape[1]
        z = rmsnorm(u, pre_norm_w) @ in_proj_w.T
        zc = z.transpose(0, 2, 1)
        z_pre = jax.lax.conv_general_dilated(zc, short_w, window_strides=(1,), padding=[(K - 1, 0)], dimension_numbers=('NCH', 'OIH', 'NCH'), feature_group_count=3 * D)
        z_pre = z_pre + short_b[None, :, None]
        x2, x1, v = jnp.split(z_pre, 3, axis=1)
        t = jnp.arange(Lc, dtype=jnp.float32)
        h = jnp.sum(residues[:, :, None] * jnp.exp(log_poles * t[None, None, :]), axis=1)
        xv = x1 * v
        n = 2 * Lc
        Xf = jnp.fft.rfft(xv, n=n)
        Hf = jnp.fft.rfft(h, n=n)
        yconv = jnp.fft.irfft(Xf * Hf[None], n=n)[..., :Lc]
        y = (yconv + xv * D_skip[None, :, None]) * x2
        y = y.transpose(0, 2, 1)
        y = y @ out_proj_w.T + u
        zm = rmsnorm(y, post_norm_w)
        mlp = jax.nn.gelu(zm @ l1_w.T) * (zm @ l2_w.T) @ l3_w.T
        return y + mlp

    def _L1_ffn_ref(hidden_states, wi, bi, wo, bo, lora_A, lora_B, gate_w, gate_b):
        import jax, jax.numpy as jnp
        import numpy as np
        B, S, D_MODEL, D_FF, E, R, TOP_K = (4, 256, 128, 512, 8, 16, 2)
        logits = jnp.einsum('bsd,ed->bse', hidden_states, gate_w) + gate_b
        scores = jax.nn.softmax(logits, axis=-1)
        top_v, top_i = jax.lax.top_k(scores, TOP_K)
        val_sum = top_v.sum(axis=-1)
        out = jnp.zeros_like(hidden_states)
        for e in range(E):
            count = (top_i == e).sum(axis=-1).astype(hidden_states.dtype)
            gate = count * val_sum
            inter = jnp.einsum('bsd,fd->bsf', hidden_states, wi) + bi + jnp.einsum('bsr,fr->bsf', jnp.einsum('bsd,rd->bsr', hidden_states, lora_A[e]), lora_B[e])
            h = jax.nn.relu(inter)
            expert_out = jnp.einsum('bsf,df->bsd', h, wo) + bo
            out = out + gate[..., None] * expert_out
        return out
    x = L0_attn_x
    xn = _layernorm(x, axis=-1)
    x = x + _L0_attn_ref(xn, L0_attn_Wq, L0_attn_bq, L0_attn_Wk, L0_attn_bk, L0_attn_Wv, L0_attn_bv, L0_attn_Wbeta, L0_attn_bbeta, L0_attn_Wo, L0_attn_bo, L0_attn_wq_conv, L0_attn_bq_conv, L0_attn_wk_conv, L0_attn_bk_conv, L0_attn_wv_conv, L0_attn_bv_conv, L0_attn_norm_w) + _L0_ffn_ref(xn, L0_ffn_Wr, L0_ffn_br, L0_ffn_ln_g, L0_ffn_ln_b, L0_ffn_W1, L0_ffn_b1, L0_ffn_W2, L0_ffn_b2)
    xn = _layernorm(x, axis=-1)
    x = x + _L1_attn_ref(xn, L1_attn_pre_norm_w, L1_attn_in_proj_w, L1_attn_short_w, L1_attn_short_b, L1_attn_log_poles, L1_attn_residues, L1_attn_D_skip, L1_attn_out_proj_w, L1_attn_post_norm_w, L1_attn_l1_w, L1_attn_l2_w, L1_attn_l3_w) + _L1_ffn_ref(xn, L1_ffn_wi, L1_ffn_bi, L1_ffn_wo, L1_ffn_bo, L1_ffn_lora_A, L1_ffn_lora_B, L1_ffn_gate_w, L1_ffn_gate_b)
    return x

_drawn_inputs = setup_inputs


def setup_inputs(seed=0):
    import zlib

    import numpy as np

    out = dict(_drawn_inputs(seed))
    spreads = {'L0_attn_bq': (0.0, 0.1),
     'L0_attn_bk': (0.0, 0.1),
     'L0_attn_bv': (0.0, 0.1),
     'L0_attn_bbeta': (0.0, 0.8),
     'L0_attn_bo': (0.0, 0.1),
     'L0_attn_bq_conv': (0.0, 0.1),
     'L0_attn_bk_conv': (0.0, 0.1),
     'L0_attn_bv_conv': (0.0, 0.1),
     'L0_attn_norm_w': (1.0, 0.2),
     'L0_ffn_br': (0.0, 0.34),
     'L0_ffn_ln_g': (1.0, 0.6),
     'L0_ffn_ln_b': (0.0, 0.8),
     'L0_ffn_b1': (0.0, 0.8),
     'L0_ffn_b2': (0.0, 0.417),
     'L1_attn_pre_norm_w': (1.0, 0.2),
     'L1_attn_post_norm_w': (1.0, 0.2)}
    factors = {'L0_ffn_W1': 4.329,
     'L0_ffn_W2': 3.296,
     'L1_attn_D_skip': 36.177,
     'L1_ffn_bi': 8.0,
     'L1_ffn_bo': 8.0,
     'L1_ffn_lora_A': 3.086,
     'L1_ffn_lora_B': 3.077,
     'L1_ffn_gate_b': 8.0}
    for name, (base, spread) in spreads.items():
        noise = np.random.default_rng([zlib.crc32(name.encode()), seed]).standard_normal(out[name].shape)
        drawn = base * np.exp(spread * noise) if base else spread * noise
        out[name] = jnp.asarray(drawn.astype(out[name].dtype))
    for name, factor in factors.items():
        out[name] = (out[name] * factor).astype(out[name].dtype)
    return out
```

```python
import concourse.bass as bass
from concourse import mybir
from contextlib import ExitStack

B, L, D = 4, 1024, 128
P = 128
C = 32
T = L // C
N = B * L
H, HD = 16, 8
J = 2 * HD
K0, K1 = 4, 3
E0, F0 = 8, 512
FS = F0 // P
E1, RK = 8, 16
NP1 = 16
FF, FT = 336, 112
ST = 4
SC = ST * P
NS = T // ST

FIXED = [("ident", P), ("headmask", H), ("headmean", P), ("first", 1), ("descend", E0), ("woT", P),
         ("norm_w", 1), ("ln_g", 1), ("ln_b", 1), ("b1", E0 * FS), ("b2", P)]
EARLY = [("wqkvT", 3 * P), ("conv", K0 * 3 * P), ("brow", 3 * P), ("wbrT", H + E0), ("taps", 3 * K0),
         ("bqkv", 3), ("bconv", 3), ("bbr", 1)]
LATE = [("bo", P), ("inT", 3 * P), ("shortb", 3), ("poles", NP1), ("res", NP1), ("skip", 1),
        ("outT", P), ("pre_w", 1), ("post_w", 1), ("l1T", FF), ("l2T", FF), ("l3T", 3 * P),
        ("bi", FS), ("loraAT", P), ("gateT", E1), ("gateb", 1), ("bo1", P)]
LAST = [("short", K1 * 3 * P), ("wiT", F0), ("wo1T", FS * P), ("loraBT", F0)]


def width(pack):
    return sum(n for _, n in pack)


def columns(tile, pack):
    at, out = 0, {}
    for name, n in pack:
        out[name] = tile[:, at:at + n]
        at += n
    return out


class Count:

    def __init__(self, eng, sem):
        self.eng, self.sem, self.base, self.n = eng, sem, 0, 0

    def link(self, ins):
        ins.then_inc(self.sem, 1)
        self.n += 1
        self.eng.wait_ge(self.sem, self.base + self.n)

    def enter(self, i, per):
        self.outer, self.per = self.base + self.n, per
        self.base, self.n = self.outer + i * per, 0

    def leave(self, times):
        assert self.n == self.per, (self.n, self.per)
        self.base, self.n = self.outer + times * self.per, 0


def two_layers(nc, x_d, fixed_d, early_d, late_d, last_d, w1_d, w2_d, out_d, stop=None):
    fp32 = mybir.dt.float32
    ALU = mybir.AluOpType
    ACT = mybir.ActivationFunctionType
    AX = mybir.AxisListType
    ds = bass.ds
    ctx = ExitStack()
    with ctx:
        def sb(name, cols):
            return ctx.enter_context(nc.sbuf_tensor(name, [P, cols], fp32))

        def sem(name):
            return ctx.enter_context(nc.semaphore(name))

        tA = sb("tA", N)
        tB = sb("tB", N)
        tC = sb("tC", N + (K0 - 1) * P)
        tDE = sb("tDE", 2 * N)
        tF = sb("tF", N)
        tG = sb("tG", N)
        tH = sb("tH", N)
        tI = sb("tI", N)
        tJ = sb("tJ", N)
        tK = sb("tK", N)
        wt = sb("wt", max(width(EARLY), width(LATE)))
        fx = sb("fx", width(FIXED))
        stage = sb("stage", 4 * SC)
        small = sb("small", 12 * T)
        brt = sb("brt", T * (H + E0))
        gates = sb("gates", 4 * T * E0)
        stats = sb("stats", 6 * T)
        pred = sb("pred", H * J)
        biasq = sb("biasq", 4)
        ps = [ctx.enter_context(nc.psum_tensor(f"ps{n}", [P, SC], fp32)) for n in range(8)]

        F = columns(fx, FIXED)
        W = columns(wt, EARLY)
        V = columns(wt, LATE)
        V.update(columns(tH[:, N - width(LAST):N], LAST))
        ident = F["ident"]

        x_in, fixed_in, early_in, late_in = sem("x_in"), sem("fixed_in"), sem("early_in"), sem("late_in")
        last_in = sem("last_in")
        w1_in, w2_in, x_again, out_sent = sem("w1_in"), sem("w2_in"), sem("x_again"), sem("out_sent")
        dve_steps, act_steps, pool_steps = sem("dve_steps"), sem("act_steps"), sem("pool_steps")
        S = {}

        def s(name):
            if name not in S:
                S[name] = sem(name)
            return S[name]

        block = ctx.enter_context(nc.Block())

        xnT0 = tC[:, (K0 - 1) * P:]
        qv = tDE[:]
        k_tm, kb_tm = tF, tG
        fold0 = tK[:, 0:K0 * 3 * P]
        corr = tK[:, 1536:1536 + 3 * 384]
        mean, var, rstd, tmp1, tmp2 = (small[:, n * T:(n + 1) * T] for n in range(5))
        mask0 = gates[:, 0:T * E0]
        R = [tJ[:, 0:2048], tJ[:, 2048:4096]]

        znT, fold1 = tDE[:, 0:N + (K1 - 1) * P], tH[:, 0:K1 * 3 * P]
        scan = [tDE[:, 4352 + n * L:4352 + (n + 1) * L] for n in range(2)]
        picks = tDE[:, 6400:6400 + 2 * SC]
        axs = tK[:, 4 * SC:5 * SC]
        axm = [tK[:, (5 + n) * SC:(6 + n) * SC] for n in range(2)]
        m_prob = gates[:, 2 * T * E0:3 * T * E0]

        @block.sync
        def _(sp):
            sp.dma_start(tA[:], x_d).then_inc(x_in, 16)
            sp.dma_start(fx[:], fixed_d).then_inc(fixed_in, 16)
            sp.dma_start(wt[:, 0:width(EARLY)], early_d).then_inc(early_in, 16)
            sp.dma_start(tH[:], w1_d).then_inc(w1_in, 16)
            sp.dma_start(tI[:], w2_d).then_inc(w2_in, 16)
            if stop == "A2":
                sp.wait_ge(s("xnT_ready"), NS)
                sp.wait_ge(s("xeT_ready"), NS)
                sp.dma_start(out_d, tB[:]).then_inc(out_sent, 16)
                sp.wait_ge(out_sent, 16)
                return
            if stop == "A4":
                sp.wait_ge(s("prepared"), 1)
                sp.wait_ge(s("v_scaled"), 1)
                sp.dma_start(out_d, tG[:]).then_inc(out_sent, 16)
                sp.wait_ge(out_sent, 16)
                return
            sp.wait_ge(s("qkv_in"), NS + 1)
            sp.wait_ge(s("corrected"), 1)
            sp.dma_start(wt[:, 0:width(LATE)], late_d).then_inc(late_in, 16)
            sp.wait_ge(s("y0_ready"), NS * E0 + 2)
            sp.dma_start(tI[:], x_d).then_inc(x_again, 16)
            if stop == "B":
                sp.wait_ge(s("y0_used"), NS * E0 + 2)
                sp.wait_ge(s("out_done"), T + 2)
                sp.dma_start(out_d, tDE[:, 0:N]).then_inc(out_sent, 16)
                sp.wait_ge(out_sent, 16)
                return
            if stop == "C":
                sp.wait_ge(s("x1_ready"), NS)
                sp.dma_start(out_d, tA[:]).then_inc(out_sent, 16)
                sp.wait_ge(out_sent, 16)
                return
            sp.wait_ge(s("inter_done"), NS + 2)
            sp.dma_start(tH[:, N - width(LAST):N], last_d).then_inc(last_in, 16)
            with sp.Fori(0, NS) as i:
                sp.wait_ge(s("result_ready"), i + 2)
                sp.dma_start(out_d[:, ds(i * SC, SC)], tA[:, ds(i * SC, SC)]).then_inc(out_sent, 16)
            sp.wait_ge(out_sent, 16 * NS)

        @block.vector
        def _(dve):
            ch = Count(dve, dve_steps)
            link = ch.link
            v = nc.vector

            def row_stats(x, mean_o, var_o):
                with dve.Fori(0, NS) as i:
                    for j in range(ST):
                        last = v.bn_stats(stats[:, ds(i * 6 * ST + 6 * j, 6)], x[:, ds(i * SC + j * P, P)])
                    ch.enter(i, 1)
                    link(last)
                ch.leave(NS)
                st = stats[:].rearrange("p (t s) -> p t s", s=6)
                link(v.tensor_tensor(mean_o, st[:, :, 1], st[:, :, 4], ALU.add))
                link(v.tensor_scalar(mean_o, mean_o, 0.5, None, ALU.mult))
                link(v.tensor_tensor(tmp1, st[:, :, 1], mean_o, ALU.subtract))
                link(v.tensor_tensor(tmp1, tmp1, tmp1, ALU.mult))
                link(v.tensor_tensor(tmp2, st[:, :, 2], st[:, :, 5], ALU.add))
                link(v.tensor_scalar(tmp2, tmp2, 1.0 / P, None, ALU.mult))
                return v.tensor_tensor(var_o, tmp1, tmp2, ALU.add)

            def normalise(x, y):
                with dve.Fori(0, NS) as i:
                    for j in range(ST):
                        c = i * SC + j * P
                        last = v.tensor_scalar(y[:, ds(c, P)], x[:, ds(c, P)], mean[:, ds(i * ST + j, 1)],
                                               rstd[:, ds(i * ST + j, 1)], ALU.subtract, ALU.mult)
                    ch.enter(i, 1)
                    link(last)
                ch.leave(NS)

            dve.wait_ge(x_in, 16)
            row_stats(tA, mean, var).then_inc(s("var_ready"), 1)
            dve.wait_ge(s("std_ready"), 1)
            link(v.reciprocal(rstd, rstd))
            normalise(tA, tA)
            row_stats(tA, mean, var).then_inc(s("var_ready"), 1)
            dve.wait_ge(early_in, 16)
            wb = W["wqkvT"].unsqueeze(1).broadcast_to([P, K0, 3 * P])
            v.tensor_tensor(fold0.rearrange("p (i n) -> p i n", i=K0), wb,
                            W["conv"].rearrange("p (i n) -> p i n", i=K0), ALU.mult).then_inc(s("fold0_ready"), 1)
            link(v.tensor_reduce(biasq[:, 0:3], W["taps"].rearrange("p (a i) -> p a i", i=K0), AX.X, ALU.add))
            link(v.tensor_tensor(biasq[:, 0:3], biasq[:, 0:3], W["bqkv"], ALU.mult))
            v.tensor_tensor(biasq[:, 0:3], biasq[:, 0:3], W["bconv"], ALU.add).then_inc(s("biasq_ready"), 1)
            cb = W["conv"].rearrange("p (i n) -> p i n", i=K0)
            cr = corr.rearrange("p (t n) -> p t n", t=3)
            link(v.tensor_tensor(cr, cb[:, 0:3, :], W["brow"].unsqueeze(1).broadcast_to([P, 3, 384]), ALU.mult))
            link(v.tensor_tensor(cr[:, 1, :], cr[:, 0, :], cr[:, 1, :], ALU.add))
            link(v.tensor_tensor(cr[:, 2, :], cr[:, 1, :], cr[:, 2, :], ALU.add))
            dve.wait_ge(s("std_ready"), 2)
            link(v.reciprocal(rstd, rstd))
            with dve.Fori(0, NS) as i:
                dve.wait_ge(s("xe_turned"), i + 1)
                for j in range(ST):
                    last = v.tensor_scalar(stage[:, SC + j * P:SC + (j + 1) * P], tA[:, ds(i * SC + j * P, P)],
                                           mean[:, ds(i * ST + j, 1)], rstd[:, ds(i * ST + j, 1)],
                                           ALU.subtract, ALU.mult)
                last.then_inc(s("xe_staged"), 1)
                dve.wait_ge(s("xe_turned"), i + 2)
                v.tensor_scalar(tB[:, ds(i * SC, SC)], ps[1][:], F["ln_g"], F["ln_b"],
                                ALU.mult, ALU.add).then_inc(s("xeT_ready"), 1)
            link(v.memset(tC[:, 0:(K0 - 1) * P], 0.0))
            dve.wait_ge(s("xnT_ready"), NS)
            halo = tC[:, 0:(K0 - 1) * P].rearrange("p (t b c) -> p t b c", b=B, c=C)
            src = xnT0[:, (T - K0 + 1) * P:T * P].rearrange("p (t b c) -> p t b c", b=B, c=C)
            for t in range(K0 - 1):
                last = v.tensor_copy(halo[:, t, :, 1:C], src[:, t, :, 0:C - 1])
            last.then_inc(s("halo0_ready"), 1)
            if stop == "A2":
                return

            dve.sem_inc(s("qkv_in"), 1)
            with dve.Fori(0, NS) as i:
                dve.wait_ge(s("qkv_turned"), i + 2)
                qvi = qv[:, ds(i * 2 * SC, 2 * SC)].rearrange("p (t n) -> p t n", t=ST)
                v.tensor_copy(qvi[:, :, 0:P], ps[4][:].rearrange("p (t n) -> p t n", t=ST))
                v.tensor_copy(k_tm[:, ds(i * SC, SC)], ps[5][:])
                v.tensor_copy(qvi[:, :, P:2 * P], ps[6][:].rearrange("p (t n) -> p t n", t=ST))
                v.tensor_copy(brt[:, ds(i * ST * (H + E0), ST * (H + E0))],
                              ps[7][:, 0:ST * (H + E0)]).then_inc(s("qkv_in"), 1)
            dve.wait_ge(s("qkv_in"), NS + 1)
            qvt = qv.rearrange("p (t n) -> p t n", t=T)
            kt = k_tm[:].rearrange("p (t n) -> p t n", t=T)
            for t in range(3):
                row = cr[:, 2 - t, :]
                for dst, o in ((qvt[:, t, 0:P], 0), (kt[:, t, :], P), (qvt[:, t, P:2 * P], 2 * P)):
                    last = v.scalar_tensor_tensor(out=dst, in0=row[:, o:o + P], scalar=F["first"], in1=dst,
                                                  op0=ALU.mult, op1=ALU.add)
            last.then_inc(s("corrected"), 1)
            dve.wait_ge(s("corrected"), 1)

            bt = brt[:].rearrange("p (t n) -> p t n", t=T)
            logit = bt[:, :, H:H + E0]
            m3 = [gates[:, n * T * E0:(n + 1) * T * E0].rearrange("p (t e) -> p t e", e=E0) for n in range(4)]

            def over_e(col):
                return col.unsqueeze(2).broadcast_to([P, T, E0])

            desc = F["descend"].unsqueeze(1).broadcast_to([P, T, E0])
            top = small[:, 5 * T:6 * T]
            link(v.tensor_reduce(top, logit, AX.X, ALU.max))
            v.tensor_tensor(m3[1], logit, over_e(top), ALU.subtract).then_inc(s("shifted0"), 1)
            link(v.tensor_tensor(m3[0], logit, over_e(top), ALU.is_equal))
            link(v.tensor_tensor(m3[0], m3[0], desc, ALU.mult))
            link(v.tensor_reduce(top, m3[0], AX.X, ALU.max))
            link(v.tensor_tensor(m3[0], m3[0], over_e(top), ALU.is_equal))
            dve.wait_ge(s("exp0_ready"), 1)
            link(v.tensor_reduce(top, m3[1], AX.X, ALU.add))
            link(v.reciprocal(top, top))
            v.tensor_tensor(m3[0], m3[0], over_e(top), ALU.mult).then_inc(s("mask0_ready"), 1)

            q2 = tJ[:].rearrange("p (n d) -> p n d", d=HD)
            norms = tK[:, 3072:4096]
            dve.wait_ge(s("q_squared"), 1)
            v.tensor_reduce(norms[:, 0:T * H], q2, AX.X, ALU.add).then_inc(s("q2_summed"), 1)
            dve.wait_ge(s("k_squared"), 1)
            v.tensor_reduce(norms[:, T * H:2 * T * H], q2, AX.X, ALU.add).then_inc(s("norms_summed"), 1)
            dve.wait_ge(s("norms_ready"), 1)
            link(v.tensor_scalar(norms, norms, 1e-6, None, ALU.add))
            v.reciprocal(norms, norms).then_inc(s("scales_ready"), 1)
            dve.wait_ge(s("scales_ready"), 1)

            def by_head(cols):
                return cols.rearrange("p (t h) -> p t h", h=H).unsqueeze(3).broadcast_to([P, T, H, HD])

            q4 = qvt[:, :, 0:P].rearrange("p t (h d) -> p t h d", d=HD)
            k4 = kt.rearrange("p t (h d) -> p t h d", d=HD)
            kb4 = kb_tm[:].rearrange("p (t h d) -> p t h d", h=H, d=HD)
            link(v.tensor_tensor(k4, k4, by_head(norms[:, T * H:2 * T * H]), ALU.mult))
            dve.wait_ge(s("beta_ready"), 1)
            v.tensor_tensor(kb4, k4, bt[:, :, 0:H].unsqueeze(3).broadcast_to([P, T, H, HD]), ALU.mult)
            link(v.tensor_tensor(q4, q4, by_head(norms[:, 0:T * H]), ALU.mult))
            link(v.memset(R[0], 0.0))
            link(v.memset(R[0].rearrange("p (h n) -> p h n", h=H)[:, :, 0:64:9], 1.0))
            v.memset(tA[:], 0.0).then_inc(s("prepared"), 1)
            dve.wait_ge(s("prepared"), 1)
            dve.wait_ge(s("v_scaled"), 1)
            if stop == "A4":
                return

            prod = tK[:, 0:2048]
            prod4 = prod.rearrange("p (h j k) -> p h j k", h=H, j=J)
            pr3 = pred[:].rearrange("p (h j) -> p h j", h=H)
            dve.sem_inc(s("y0_used"), 2)

            def heads(tile, col):
                return tile[:, ds(col, P)].rearrange("p (h k) -> p h k", k=HD).unsqueeze(2).broadcast_to([P, H, J, HD])

            with dve.Fori(0, NS) as i:
                ch.enter(i, 4 * ST)
                for e in range(E0):
                    t = e // 2
                    cur, nxt = R[t % 2], R[(t + 1) % 2]
                    cur4 = cur.rearrange("p (h j k) -> p h j k", h=H, j=J)
                    nxt4 = nxt.rearrange("p (h j k) -> p h j k", h=H, j=J)
                    if e % 2 == 0:
                        link(v.tensor_tensor(prod4, cur4, heads(k_tm, i * SC + t * P), ALU.mult))
                        link(v.tensor_reduce(pr3, prod4, AX.X, ALU.add))
                        link(v.tensor_tensor(pr3[:, :, HD:J], pr3[:, :, HD:J],
                                             qv[:, ds(i * 2 * SC + t * 2 * P + P, P)].rearrange(
                                                 "p (h k) -> p h k", k=HD), ALU.subtract))
                    else:
                        link(v.tensor_tensor(prod4, heads(kb_tm, i * SC + t * P),
                                             pr3.unsqueeze(3).broadcast_to([P, H, J, HD]), ALU.mult))
                        dve.wait_ge(s("out_done"), i * ST + t + 1)
                        v.tensor_tensor(nxt4, cur4, prod4, ALU.subtract).then_inc(s("state_ready"), 1)
                        dve.wait_ge(s("state_ready"), i * ST + t + 1)
                    dve.wait_ge(s("y0_ready"), i * E0 + e + 3)
                    dve.wait_ge(s("y0_used"), i * E0 + e + 2)
                    for j in range(ST):
                        yj = tA[:, ds(i * SC + j * P, P)]
                        last = v.scalar_tensor_tensor(out=yj, in0=ps[4 + e % 2][:, j * P:(j + 1) * P],
                                                      scalar=mask0[:, ds(i * ST * E0 + j * E0 + e, 1)],
                                                      in1=yj, op0=ALU.mult, op1=ALU.add)
                    last.then_inc(s("y0_used"), 1)
            ch.leave(NS)
            if stop == "B":
                return

            Mt = tC[:, 0:1024]
            Nt = tC[:, 1024:2048]
            Sst = tC[:, 2048:2048 + (C + 1) * B * HD]
            Mexp = [tK[:, 0:512], tK[:, 512:1024]]
            hm = F["headmask"]
            final4 = R[0].rearrange("p (h j k) -> p h j k", h=H, j=J)
            sorted_ = tK[:, 2048:4096]
            dve.wait_ge(s("out_done"), T + 2)
            v.tensor_copy(sorted_[:, 0:1024].rearrange("p (k h j) -> p h j k", k=HD, h=H), final4[:, :, 0:HD, :])
            v.tensor_copy(sorted_[:, 1024:2048].rearrange("p (j h k) -> p h j k", j=HD, h=H),
                          final4[:, :, HD:J, :]).then_inc(s("maps_sorted"), 1)
            dve.wait_ge(s("maps_turned"), 1)
            v.tensor_copy(Mt[:, 0:512], ps[0][:])
            v.tensor_copy(Mt[:, 512:1024], ps[1][:])
            v.tensor_copy(Nt[:, 0:512], ps[2][:])
            link(v.tensor_copy(Nt[:, 512:1024], ps[3][:]))
            v.memset(Sst[:, 0:B * HD], 0.0).then_inc(s("carry_ready"), 1)
            Mt4 = Mt.rearrange("p (k b c) -> p k b c", k=HD, b=B)
            Nt4 = Nt.rearrange("p (k b c) -> p k b c", k=HD, b=B)
            hm4 = hm.unsqueeze(1).unsqueeze(3).broadcast_to([P, B, H, HD])
            with dve.Fori(0, C // 2) as i:
                for u in range(2):
                    dve.wait_ge(s("carried"), i * 2 + u + 1)
                    v.tensor_tensor(
                        Mexp[u].rearrange("p (b h k) -> p b h k", b=B, h=H),
                        Mt4[:, :, :, ds(2 * i + u, 1)].rearrange("p k b o -> p b o k").broadcast_to([P, B, H, HD]),
                        hm4, ALU.mult).then_inc(s("map_wide"), 1)
                    dve.wait_ge(s("carried"), i * 2 + u + 3)
                    v.tensor_tensor(Sst[:, ds((2 * i + u + 1) * B * HD, B * HD)].rearrange("p (b v) -> p v b", b=B),
                                    ps[6 + u][:, 0:B * HD].rearrange("p (b v) -> p v b", b=B),
                                    Nt4[:, :, :, ds(2 * i + u, 1)].rearrange("p v b o -> p v (b o)"),
                                    ALU.add).then_inc(s("carry_ready"), 1)
            dve.sem_inc(s("oT_ready"), 2)

            def by_chunk(tile):
                return tile[:].rearrange("p (t b c) -> p c b t", b=B, c=C)

            with dve.Fori(0, NS // 2) as i:
                for u in range(2):
                    dve.wait_ge(s("inter_done"), i * 2 + u + 1)
                    v.tensor_tensor(
                        tH[:, u * 2048:(u + 1) * 2048].rearrange("p (n h v) -> p n h v", n=ST * B, h=H),
                        Sst[:, ds((2 * i + u) * ST * B * HD, ST * B * HD)].rearrange(
                            "p (n v) -> p n v", n=ST * B).unsqueeze(2).broadcast_to([P, ST * B, H, HD]),
                        hm.unsqueeze(1).unsqueeze(3).broadcast_to([P, ST * B, H, HD]),
                        ALU.mult).then_inc(s("state_wide"), 1)
                    dve.wait_ge(s("inter_done"), i * 2 + u + 3)
                    dve.wait_ge(s("outs_in"), NS)
                    v.tensor_tensor(
                        by_chunk(tB)[:, ds((2 * i + u) * ST, ST), :, :],
                        ps[u][:].rearrange("p (c b t) -> p c b t", c=ST, b=B),
                        by_chunk(tG)[:, ds((2 * i + u) * ST, ST), :, :], ALU.add).then_inc(s("oT_ready"), 1)
            nr = tK[:, 2048:2048 + SC]
            onT = stage[:, SC:2 * SC]
            dve.wait_ge(s("oT_ready"), NS + 2)
            dve.wait_ge(x_again, 16)
            dve.wait_ge(late_in, 16)
            with dve.Fori(0, NS) as i:
                ch.enter(i, 3)
                dve.wait_ge(s("oroot_ready"), i + 1)
                link(v.reciprocal(nr, stage[:, 2 * SC:3 * SC]))
                dve.wait_ge(s("wo0_done"), i + 1)
                v.scalar_tensor_tensor(out=onT, in0=tB[:, ds(i * SC, SC)], scalar=F["norm_w"], in1=nr,
                                       op0=ALU.mult, op1=ALU.mult).then_inc(s("onT_ready"), 1)
                dve.wait_ge(s("wo0_done"), i + 2)
                xi = tA[:, ds(i * SC, SC)]
                link(v.tensor_tensor(xi, ps[2][:], xi, ALU.add))
                link(v.tensor_tensor(xi, xi, tI[:, ds(i * SC, SC)], ALU.add))
                v.tensor_tensor(xi.rearrange("p (t n) -> p t n", t=ST), xi.rearrange("p (t n) -> p t n", t=ST),
                                V["bo"].unsqueeze(1).broadcast_to([P, ST, P]), ALU.add).then_inc(s("x1_ready"), 1)
            ch.leave(NS)
            if stop == "C":
                return

            dve.wait_ge(s("x1_ready"), NS)
            row_stats(tA, mean, var).then_inc(s("var_ready"), 1)
            dve.wait_ge(s("std_ready"), 3)
            link(v.reciprocal(rstd, rstd))
            normalise(tA, tG)
            link(row_stats(tG, mean, var))
            link(v.tensor_tensor(mean, mean, mean, ALU.mult))
            v.tensor_tensor(var, var, mean, ALU.add).then_inc(s("var_ready"), 1)
            dve.wait_ge(last_in, 16)
            v.tensor_tensor(fold1.rearrange("p (i n) -> p i n", i=K1),
                            V["inT"].unsqueeze(1).broadcast_to([P, K1, 3 * P]),
                            V["short"].rearrange("p (i n) -> p i n", i=K1), ALU.mult).then_inc(s("fold1_ready"), 1)
            dve.wait_ge(s("std_ready"), 4)
            link(v.reciprocal(rstd, rstd))
            with dve.Fori(0, NS) as i:
                dve.wait_ge(s("zn_turned"), i + 1)
                v.tensor_tensor(stage[:, SC:2 * SC].rearrange("p (t n) -> p t n", t=ST),
                                tG[:, ds(i * SC, SC)].rearrange("p (t n) -> p t n", t=ST),
                                rstd[:, ds(i * ST, ST)].unsqueeze(2).broadcast_to([P, ST, P]),
                                ALU.mult).then_inc(s("zn_staged"), 1)
                dve.wait_ge(s("zn_turned"), i + 2)
                v.tensor_scalar(znT[:, ds((K1 - 1) * P + i * SC, SC)], ps[1][:], V["pre_w"], None,
                                ALU.mult).then_inc(s("znT_ready"), 1)
            link(v.memset(znT[:, 0:(K1 - 1) * P], 0.0))
            dve.wait_ge(s("znT_ready"), NS)
            halo1 = znT[:, 0:(K1 - 1) * P].rearrange("p (t b c) -> p t b c", b=B, c=C)
            src1 = znT[:, T * P:(T + K1 - 1) * P].rearrange("p (t b c) -> p t b c", b=B, c=C)
            for t in range(K1 - 1):
                last = v.tensor_copy(halo1[:, t, :, 1:C], src1[:, t, :, 0:C - 1])
            last.then_inc(s("halo1_ready"), 1)
            dve.sem_inc(s("xv_ready"), 1)
            dve.sem_inc(s("gate1_in"), 1)
            with dve.Fori(0, NS) as i:
                dve.wait_ge(s("z_out"), i + 2)
                dve.wait_ge(s("z_done"), i + 1)
                v.scalar_tensor_tensor(
                    out=tF[:].rearrange("p (n t) -> p t n", t=T)[:, ds(i * ST, ST), :],
                    in0=ps[2][:].rearrange("p (t n) -> p t n", t=ST), scalar=V["shortb"][:, 2:3],
                    in1=stage[:, 0:SC].rearrange("p (t n) -> p t n", t=ST),
                    op0=ALU.add, op1=ALU.mult).then_inc(s("xv_ready"), 1)
                dve.wait_ge(s("gate1_turned"), i + 1)
                v.tensor_copy(brt[:, ds(i * ST * E1, ST * E1)], ps[4][:, 0:ST * E1]).then_inc(s("gate1_in"), 1)
            dve.wait_ge(s("gate1_in"), NS + 1)
            lg = brt[:, 0:T * E1].rearrange("p (t e) -> p t e", e=E1)
            one, two, prob, work = m3
            link(v.tensor_reduce(top, lg, AX.X, ALU.max))
            v.tensor_tensor(prob, lg, over_e(top), ALU.subtract).then_inc(s("shifted1"), 1)
            dve.wait_ge(s("exp1_ready"), 1)
            link(v.tensor_reduce(top, prob, AX.X, ALU.add))
            link(v.reciprocal(top, top))
            link(v.tensor_tensor(prob, prob, over_e(top), ALU.mult))
            for n, pick in ((0, one), (1, two)):
                best = small[:, (6 + n) * T:(7 + n) * T]
                link(v.tensor_reduce(best, prob, AX.X, ALU.max))
                link(v.tensor_tensor(pick, prob, over_e(best), ALU.is_equal))
                link(v.tensor_tensor(pick, pick, desc, ALU.mult))
                link(v.tensor_reduce(top, pick, AX.X, ALU.max))
                link(v.tensor_tensor(pick, pick, over_e(top), ALU.is_equal))
                if n == 0:
                    link(v.scalar_tensor_tensor(out=prob, in0=pick, scalar=-4.0, in1=prob, op0=ALU.mult, op1=ALU.add))
            weight = small[:, 6 * T:7 * T]
            link(v.tensor_tensor(weight, weight, small[:, 7 * T:8 * T], ALU.add))
            v.memset(pred[0:1, P:2 * P], 1.0)
            v.tensor_scalar(pred[0:1, 0:P], V["bo1"][0:1, :], 2.0, None, ALU.mult).then_inc(s("picks_ready"), 1)
            dve.wait_ge(s("decay_ready"), 1)
            dve.wait_ge(s("xv_ready"), NS + 1)
            dve.sem_inc(s("ffn1_in"), 1)
            with dve.Fori(0, B) as b:
                ch.enter(b, 1 + NP1 + NP1)
                xb = tF[:, ds(b * L, L)]
                yb = tH[:, 0:L]
                link(v.tensor_scalar(yb, xb, V["skip"], None, ALU.mult))
                for n in range(NP1):
                    if n % 8 == 2:
                        u = n // 8
                        dve.wait_ge(s("pick_turned"), 2 * b + u + 1)
                        dve.wait_ge(s("axs_ready"), 2 * b + u + 2)
                        v.tensor_tensor(axm[0], ps[5][:], axs, ALU.mult)
                        v.tensor_tensor(axm[1], ps[7][:], axs, ALU.mult).then_inc(s("axm_ready"), 1)
                    sn = scan[n % 2]
                    link(v.tensor_tensor_scan(sn, V["poles"][:, n:n + 1].broadcast_to([P, L]), xb, 0.0,
                                              ALU.mult, ALU.add))
                    link(v.scalar_tensor_tensor(out=yb, in0=sn, scalar=V["res"][:, n:n + 1], in1=yb,
                                                op0=ALU.mult, op1=ALU.add))
                    if n % 8 == 7:
                        u = n // 8
                        dve.wait_ge(s("y1_done"), 2 * b + u + 2)
                        v.tensor_tensor(tI[:, ds((2 * b + u) * SC, SC)].rearrange("p (t n) -> p t n", t=ST),
                                        ps[4][:].rearrange("p (t n) -> p t n", t=ST),
                                        weight[:, ds((2 * b + u) * ST, ST)].unsqueeze(2).broadcast_to([P, ST, P]),
                                        ALU.mult).then_inc(s("ffn1_in"), 1)
                x2b = tB[:].rearrange("p (t n) -> p t n", t=T)[:, :, ds(b * C, C)]
                last = v.tensor_tensor(x2b, x2b, yb.rearrange("p (c t) -> p t c", t=T), ALU.mult)
                last.then_inc(s("yT_ready"), 1)
                dve.wait_ge(s("yT_ready"), b + 1)
            ch.leave(B)
            dve.wait_ge(s("ffn1_in"), NS + 1)
            ys, rms = stage[:, SC:2 * SC], small[:, 8 * T:8 * T + ST]
            dve.sem_inc(s("result_ready"), 1)
            with dve.Fori(0, NS) as i:
                ch.enter(i, 3)
                dve.wait_ge(s("yo_done"), i + 2)
                v.tensor_tensor(ys, ps[0][:], tG[:, ds(i * SC, SC)], ALU.add).then_inc(s("ys_ready"), 1)
                dve.wait_ge(s("ys_squared"), i + 1)
                v.tensor_reduce(rms, stage[:, 2 * SC:3 * SC].rearrange("p (t n) -> p t n", t=ST), AX.X,
                                ALU.add).then_inc(s("ms_ready"), 1)
                dve.wait_ge(s("rms_ready"), i + 1)
                link(v.reciprocal(rms, rms))
                v.tensor_tensor(stage[:, 3 * SC:4 * SC].rearrange("p (t n) -> p t n", t=ST),
                                ys.rearrange("p (t n) -> p t n", t=ST),
                                rms.unsqueeze(2).broadcast_to([P, ST, P]), ALU.mult).then_inc(s("zs_staged"), 1)
                for f in range(3):
                    dve.wait_ge(s("gelu_ready"), i * 3 + f + 1)
                    dve.wait_ge(s("l2_done"), i * 3 + f + 1)
                    v.tensor_tensor(tK[0:FT, f * SC:(f + 1) * SC], tJ[0:FT, f * SC:(f + 1) * SC],
                                    ps[5 + f][0:FT, :], ALU.mult).then_inc(s("gated_ready"), 1)
                dve.wait_ge(s("mlp_done"), i + 1)
                xi = tA[:, ds(i * SC, SC)]
                link(v.tensor_tensor(ys, ps[0][:], ys, ALU.add))
                link(v.tensor_tensor(xi, xi, ys, ALU.add))
                v.tensor_tensor(xi, xi, tI[:, ds(i * SC, SC)], ALU.add).then_inc(s("result_ready"), 1)
            ch.leave(NS)

        @block.scalar
        def _(act):
            ch = Count(act, act_steps)
            link = ch.link
            a = nc.scalar

            def root(out, in_, eps, need, done):
                act.wait_ge(*need)
                a.activation(out, in_, ACT.Sqrt, bias=eps).then_inc(done, 1)

            eps5 = small[:, 11 * T:11 * T + 1]
            eps6 = small[:, 11 * T + 1:11 * T + 2]
            act.wait_ge(s("eps_set"), 1)
            root(rstd, var, eps5, (s("var_ready"), 1), s("std_ready"))
            root(rstd, var, eps5, (s("var_ready"), 2), s("std_ready"))
            act.wait_ge(s("var_ready"), 2)
            with act.Fori(0, NS) as i:
                act.wait_ge(s("xn_turned"), i + 1)
                a.activation(stage[:, 0:SC], tA[:, ds(i * SC, SC)], ACT.Copy).then_inc(s("xn_staged"), 1)
                act.wait_ge(s("xn_turned"), i + 2)
                a.activation(xnT0[:, ds(i * SC, SC)], ps[0][:], ACT.Copy).then_inc(s("xnT_ready"), 1)
            if stop == "A2":
                return
            act.wait_ge(s("biasq_ready"), 1)
            act.wait_ge(s("xe_turned"), NS + 1)
            act.wait_ge(s("xn_turned"), NS + 1)
            with act.Fori(0, NS) as i:
                act.wait_ge(s("qkv_turned"), i + 1)
                for n in range(3):
                    act.wait_ge(s("qkv_done"), i * 4 + n + 1)
                    a.activation(stage[:, n * SC:(n + 1) * SC], ps[n][:], ACT.Identity,
                                 bias=biasq[:, n:n + 1]).then_inc(s("qkv_staged"), 1)
                act.wait_ge(s("qkv_done"), i * 4 + 4)
                a.activation(stage[0:H + E0, 3 * SC:4 * SC], ps[3][0:H + E0, :], ACT.Identity,
                             bias=W["bbr"][0:H + E0, :]).then_inc(s("qkv_staged"), 1)
            qvt = qv.rearrange("p (t n) -> p t n", t=T)
            bt = brt[:].rearrange("p (t n) -> p t n", t=T)
            act.wait_ge(s("shifted0"), 1)
            g1 = gates[:, T * E0:2 * T * E0]
            a.activation(g1, g1, ACT.Exp).then_inc(s("exp0_ready"), 1)
            a.activation(bt[:, :, 0:H], bt[:, :, 0:H], ACT.Sigmoid).then_inc(s("beta_ready"), 1)
            a.activation(qvt[:, :, P:2 * P], qvt[:, :, P:2 * P], ACT.Silu).then_inc(s("silu_done"), 1)
            a.activation(tJ[:].rearrange("p (t n) -> p t n", t=T), qvt[:, :, 0:P],
                         ACT.Square).then_inc(s("q_squared"), 1)
            act.wait_ge(s("q2_summed"), 1)
            a.activation(tJ[:], k_tm[:], ACT.Square).then_inc(s("k_squared"), 1)
            act.wait_ge(s("norms_summed"), 1)
            a.activation(tK[:, 3072:4096], tK[:, 3072:4096], ACT.Sqrt).then_inc(s("norms_ready"), 1)
            if stop == "A4":
                return
            act.wait_ge(s("qkv_done"), 4 * NS)
            act.sem_inc(s("hid_ready"), FS)
            with act.Fori(0, NS) as i:
                for e in range(E0):
                    act.wait_ge(s("y0_ready"), i * E0 + e + 1)
                    for f in range(FS):
                        act.wait_ge(s("hid_done"), i * E0 * FS + e * FS + f + 1)
                        a.activation(tC[:, (e % 2) * 2048 + f * SC:(e % 2) * 2048 + (f + 1) * SC], ps[f][:],
                                     ACT.Relu, bias=F["b1"][:, e * FS + f:e * FS + f + 1]).then_inc(s("hid_ready"), 1)
            if stop == "B":
                return
            act.wait_ge(s("out_done"), T + 2)
            with act.Fori(0, NS) as i:
                act.wait_ge(s("outs_turned"), i + 1)
                sr = tDE[:, ds(i * 2 * SC, 2 * SC)].rearrange("p (th j) -> p th j", j=J)
                a.activation(tJ[:, 2048:2048 + SC].rearrange("p (th k) -> p th k", k=HD), sr[:, :, 0:HD], ACT.Copy)
                a.activation(tJ[:, 3072:3072 + SC].rearrange("p (th k) -> p th k", k=HD), sr[:, :, HD:J],
                             ACT.Copy).then_inc(s("outs_staged"), 1)
                act.wait_ge(s("outs_turned"), i + 2)
                a.activation(tF[:, ds(i * SC, SC)], ps[4][:], ACT.Copy)
                a.activation(tG[:, ds(i * SC, SC)], ps[5][:], ACT.Copy).then_inc(s("outs_in"), 1)
            act.wait_ge(s("oT_ready"), NS + 2)
            with act.Fori(0, NS) as i:
                act.wait_ge(s("wo0_done"), i + 1)
                a.activation(stage[:, 3 * SC:3 * SC + ST * E0], mask0[:, ds(i * ST * E0, ST * E0)],
                             ACT.Copy).then_inc(s("mask_staged"), 1)
                a.activation(stage[:, 0:SC], tB[:, ds(i * SC, SC)], ACT.Square).then_inc(s("o_squared"), 1)
                act.wait_ge(s("mask_turned"), i + 1)
                a.activation(tK[0:E0, 1024:1024 + SC], ps[1][0:E0, :], ACT.Copy).then_inc(s("maskT_ready"), 1)
                act.wait_ge(s("o_meaned"), i + 1)
                a.activation(stage[:, 2 * SC:3 * SC], ps[0][:], ACT.Sqrt, bias=eps6).then_inc(s("oroot_ready"), 1)
            if stop == "C":
                return

            root(rstd, var, eps5, (s("var_ready"), 3), s("std_ready"))
            root(rstd, var, eps6, (s("var_ready"), 4), s("std_ready"))
            a.activation(V["poles"], V["poles"], ACT.Exp).then_inc(s("decay_ready"), 1)
            act.wait_ge(s("wo0_done"), NS + 1)
            with act.Fori(0, NS) as i:
                act.wait_ge(s("xn1_turned"), i + 1)
                a.activation(stage[:, 0:SC], tG[:, ds(i * SC, SC)], ACT.Copy).then_inc(s("xn1_staged"), 1)
                act.wait_ge(s("xn1_turned"), i + 2)
                a.activation(tC[:, ds(i * SC, SC)], ps[0][:], ACT.Copy).then_inc(s("xn1T_ready"), 1)
            act.wait_ge(s("zn_turned"), NS + 1)
            act.sem_inc(s("z_out"), 1)
            with act.Fori(0, NS) as i:
                act.wait_ge(s("xv_ready"), i + 1)
                act.wait_ge(s("z_done"), i + 1)
                a.activation(tB[:, ds(i * SC, SC)], ps[0][:], ACT.Identity, bias=V["shortb"][:, 0:1])
                a.activation(stage[:, 0:SC], ps[1][:], ACT.Identity, bias=V["shortb"][:, 1:2])
                a.activation(stage[0:E1, 3 * SC:4 * SC], ps[3][0:E1, :], ACT.Identity,
                             bias=V["gateb"][0:E1, :]).then_inc(s("z_out"), 1)
            act.wait_ge(s("shifted1"), 1)
            a.activation(m_prob, m_prob, ACT.Exp).then_inc(s("exp1_ready"), 1)
            act.sem_inc(s("h1_ready"), FS)
            act.sem_inc(s("axs_ready"), 1)
            act.wait_ge(s("picks_ready"), 1)
            with act.Fori(0, NS) as i:
                act.wait_ge(s("axm_ready"), i + 1)
                for n in range(2):
                    a.activation(picks[:, n * SC:(n + 1) * SC].rearrange("p (te r) -> p te r", r=RK),
                                 gates[:, ds(n * T * E1 + i * ST * E1, ST * E1)].unsqueeze(2).broadcast_to(
                                     [P, ST * E1, RK]), ACT.Copy).then_inc(s("pick_staged"), 1)
                act.wait_ge(s("ax_done"), i + 1)
                a.activation(axs, ps[6][:], ACT.Copy).then_inc(s("axs_ready"), 1)
                for n in range(2):
                    for f in range(FS):
                        act.wait_ge(s("h1_done"), i * 2 * FS + n * FS + f + 1)
                        if n == 0:
                            act.wait_ge(s("hsum_ready"), i * FS + f + 1)
                        c = (n * FS + f) * SC
                        a.activation(tJ[:, c:c + SC], ps[f][:], ACT.Relu,
                                     bias=V["bi"][:, f:f + 1]).then_inc(s("h1_ready"), 1)
            act.wait_ge(s("yT_ready"), B)
            act.wait_ge(s("hsum_ready"), NS * FS + FS)
            with act.Fori(0, NS) as i:
                act.wait_ge(s("yo_done"), i + 1)
                a.activation(stage[:, 0:SC], tB[:, ds(i * SC, SC)], ACT.Copy).then_inc(s("yT_staged"), 1)
                act.wait_ge(s("ys_ready"), i + 1)
                a.activation(stage[:, 2 * SC:3 * SC], stage[:, SC:2 * SC], ACT.Square).then_inc(s("ys_squared"), 1)
                act.wait_ge(s("ms_ready"), i + 1)
                a.activation(small[:, 8 * T:8 * T + ST], small[:, 8 * T:8 * T + ST], ACT.Sqrt, bias=eps6,
                             scale=1.0 / P).then_inc(s("rms_ready"), 1)
                act.wait_ge(s("zm_turned"), i + 1)
                a.activation(stage[:, 2 * SC:3 * SC], ps[1][:], ACT.Copy,
                             scale=V["post_w"]).then_inc(s("zmT_ready"), 1)
                for f in range(3):
                    act.wait_ge(s("l1_done"), i * 3 + f + 1)
                    a.activation(tJ[0:FT, f * SC:(f + 1) * SC], ps[2 + f][0:FT, :],
                                 ACT.Gelu_apprx_tanh).then_inc(s("gelu_ready"), 1)

        @block.tensor
        def _(pe):
            t_ = nc.tensor

            def turn_pairs(one, other):
                pe.sem_inc(s(one + "_turned"), 1)
                pe.sem_inc(s(other + "_turned"), 1)
                with pe.Fori(0, NS) as i:
                    for n, name in ((0, one), (1, other)):
                        pe.wait_ge(s(name + "_staged"), i + 1)
                        for j in range(ST):
                            c = n * SC + j * P
                            last = t_.transpose(ps[n][:, j * P:(j + 1) * P], stage[:, c:c + P], ident)
                        last.then_inc(s(name + "_turned"), 1)

            pe.wait_ge(fixed_in, 16)
            turn_pairs("xn", "xe")
            if stop == "A2":
                return

            pe.sem_inc(s("qkv_staged"), 4)
            pe.sem_inc(s("qkv_turned"), 1)
            pe.wait_ge(s("xnT_ready"), NS)
            pe.wait_ge(s("xeT_ready"), NS)
            pe.wait_ge(s("halo0_ready"), 1)
            pe.wait_ge(s("fold0_ready"), 1)

            def project0(i):
                for n in range(3):
                    pe.wait_ge(s("qkv_staged"), i * 4 + n + (2 if n == 2 else 1))
                    for tap in range(K0):
                        last = t_.matmul(ps[n][:], lhsT=fold0[:, tap * 3 * P + n * P:tap * 3 * P + (n + 1) * P],
                                         rhs=tC[:, ds(i * SC + tap * P, SC)], start=tap == 0, stop=tap == K0 - 1)
                    last.then_inc(s("qkv_done"), 1)
                t_.matmul(ps[3][0:H + E0, :], lhsT=W["wbrT"], rhs=tC[:, ds(i * SC + 3 * P, SC)],
                          start=True, stop=True).then_inc(s("qkv_done"), 1)

            def turn0(i):
                pe.wait_ge(s("qkv_staged"), i * 4 + 8)
                pe.wait_ge(s("qkv_in"), i + 1)
                for n in range(3):
                    for j in range(ST):
                        c = n * SC + j * P
                        t_.transpose(ps[4 + n][:, j * P:(j + 1) * P], stage[:, c:c + P], ident)
                for j in range(ST):
                    last = t_.transpose(ps[7][:, j * (H + E0):(j + 1) * (H + E0)],
                                        stage[0:H + E0, 3 * SC + j * P:3 * SC + (j + 1) * P],
                                        ident[0:H + E0, 0:H + E0])
                last.then_inc(s("qkv_turned"), 1)

            project0(0)
            with pe.Fori(0, NS - 1) as i:
                project0(i + 1)
                turn0(i)
            turn0(NS - 1)
            if stop == "A4":
                return

            pe.sem_inc(s("y0_ready"), 2)
            pe.wait_ge(w1_in, 16)
            pe.wait_ge(w2_in, 16)
            pe.wait_ge(s("qkv_in"), NS + 1)
            pe.wait_ge(s("qkv_staged"), 4 * NS + 4)

            def up(i, e):
                for f in range(FS):
                    pe.wait_ge(s("hid_ready"), i * E0 * FS + e * FS + f + 1)
                    t_.matmul(ps[f][:], lhsT=tH[:, (e * FS + f) * P:(e * FS + f + 1) * P],
                              rhs=tB[:, ds(i * SC, SC)], start=True, stop=True).then_inc(s("hid_done"), 1)

            def down(i, e):
                pe.wait_ge(s("y0_used"), i * E0 + e + 1)
                pe.wait_ge(s("hid_ready"), i * E0 * FS + e * FS + 2 * FS)
                for j in range(ST):
                    for f in range(FS):
                        c = (e % 2) * 2048 + f * SC + j * P
                        last = t_.matmul(ps[4 + e % 2][:, j * P:(j + 1) * P], lhsT=tC[:, c:c + P],
                                         rhs=tI[:, (e * FS + f) * P:(e * FS + f + 1) * P],
                                         start=f == 0, stop=f == FS - 1)
                last.then_inc(s("y0_ready"), 1)

            with pe.Fori(0, NS) as i:
                for e in range(E0):
                    up(i, e)
                    if e:
                        down(i, e - 1)
                down(i, E0 - 1)
            if stop == "B":
                return

            pe.sem_inc(s("outs_turned"), 1)
            pe.wait_ge(s("y0_used"), NS * E0 + 2)
            with pe.Fori(0, NS) as i:
                pe.wait_ge(s("outs_staged"), i + 1)
                for n in range(2):
                    for j in range(ST):
                        c = 2048 + n * 1024 + j * P
                        last = t_.transpose(ps[4 + n][:, j * P:(j + 1) * P], tJ[:, c:c + P], ident)
                last.then_inc(s("outs_turned"), 1)
            pe.wait_ge(s("maps_sorted"), 1)
            pe.wait_ge(s("hid_ready"), NS * E0 * FS + FS)
            for n in range(2 * HD):
                last = t_.transpose(ps[n // 4][:, (n % 4) * P:(n % 4 + 1) * P],
                                    tK[:, 2048 + n * P:2048 + (n + 1) * P], ident)
            last.then_inc(s("maps_turned"), 1)
            Sst = tC[:, 2048:2048 + (C + 1) * B * HD]
            pe.sem_inc(s("carried"), 2)
            with pe.Fori(0, C // 2) as i:
                for u in range(2):
                    pe.wait_ge(s("map_wide"), 2 * i + u + 1)
                    pe.wait_ge(s("carry_ready"), 2 * i + u + 1)
                    for b in range(B):
                        last = t_.matmul(ps[6 + u][:, b * HD:(b + 1) * HD],
                                         lhsT=tK[:, u * 512 + b * P:u * 512 + (b + 1) * P],
                                         rhs=Sst[:, ds((2 * i + u) * B * HD + b * HD, HD)], start=True, stop=True)
                    last.then_inc(s("carried"), 1)
            pe.sem_inc(s("inter_done"), 2)
            pe.wait_ge(s("outs_in"), NS)
            with pe.Fori(0, NS // 2) as i:
                for u in range(2):
                    pe.wait_ge(s("state_wide"), 2 * i + u + 1)
                    pe.wait_ge(s("oT_ready"), 2 * i + u + 1)
                    for a in range(ST):
                        for b in range(B):
                            n = a * B + b
                            qmt = tF[:].rearrange("p (t n) -> p n t", t=T)
                            last = t_.matmul(ps[u][:, n * T:(n + 1) * T],
                                             lhsT=tH[:, u * 2048 + n * P:u * 2048 + (n + 1) * P],
                                             rhs=qmt[:, ds((2 * i + u) * ST + a + b * C, 1), :],
                                             start=True, stop=True)
                    last.then_inc(s("inter_done"), 1)
            pe.sem_inc(s("wo0_done"), 1)
            pe.wait_ge(s("oT_ready"), NS + 2)
            with pe.Fori(0, NS) as i:
                pe.wait_ge(s("mask_staged"), i + 1)
                for j in range(ST):
                    last = t_.transpose(ps[1][0:E0, j * P:(j + 1) * P],
                                        stage[:, 3 * SC + j * E0:3 * SC + (j + 1) * E0], ident)
                last.then_inc(s("mask_turned"), 1)
                pe.wait_ge(s("o_squared"), i + 1)
                t_.matmul(ps[0][:], lhsT=F["headmean"], rhs=stage[:, 0:SC],
                          start=True, stop=True).then_inc(s("o_meaned"), 1)
                pe.wait_ge(s("onT_ready"), i + 1)
                pe.wait_ge(s("maskT_ready"), i + 1)
                for j in range(ST):
                    t_.matmul(ps[2][:, j * P:(j + 1) * P], lhsT=stage[:, SC + j * P:SC + (j + 1) * P],
                              rhs=F["woT"], start=True, stop=False)
                    last = t_.matmul(ps[2][:, j * P:(j + 1) * P], lhsT=tK[0:E0, 1024 + j * P:1024 + (j + 1) * P],
                                     rhs=F["b2"][0:E0, :], start=False, stop=True)
                last.then_inc(s("wo0_done"), 1)
            if stop == "C":
                return

            turn_pairs("xn1", "zn")
            pe.wait_ge(s("xn1T_ready"), NS)
            pe.wait_ge(s("halo1_ready"), 1)
            pe.wait_ge(s("fold1_ready"), 1)
            with pe.Fori(0, NS) as i:
                pe.wait_ge(s("z_out"), i + 1)
                pe.wait_ge(s("xv_ready"), i + 1)
                for n in range(3):
                    for tap in range(K1):
                        last = t_.matmul(ps[n][:], lhsT=fold1[:, tap * 3 * P + n * P:tap * 3 * P + (n + 1) * P],
                                         rhs=znT[:, ds(i * SC + tap * P, SC)], start=tap == 0, stop=tap == K1 - 1)
                t_.matmul(ps[3][0:E1, :], lhsT=V["gateT"], rhs=tC[:, ds(i * SC, SC)],
                          start=True, stop=True).then_inc(s("z_done"), 1)
                pe.wait_ge(s("z_out"), i + 2)
                pe.wait_ge(s("gate1_in"), i + 1)
                pe.sem_inc(s("waits_apart"), 1)
                for j in range(ST):
                    last = t_.transpose(ps[4][:, j * E1:(j + 1) * E1],
                                        stage[0:E1, 3 * SC + j * P:3 * SC + (j + 1) * P], ident[0:E1, 0:E1])
                last.then_inc(s("gate1_turned"), 1)
            pe.sem_inc(s("axm_ready"), 1)
            pe.sem_inc(s("y1_done"), 1)
            pe.wait_ge(s("gate1_in"), NS + 1)
            pe.wait_ge(s("picks_ready"), 1)
            with pe.Fori(0, NS) as i:
                pe.wait_ge(s("axm_ready"), i + 1)
                pe.wait_ge(s("axs_ready"), i + 1)
                t_.matmul(ps[6][:], lhsT=V["loraAT"], rhs=tC[:, ds(i * SC, SC)],
                          start=True, stop=True).then_inc(s("ax_done"), 1)
                pe.wait_ge(s("pick_staged"), 2 * i + 2)
                for n in range(2):
                    for j in range(ST):
                        last = t_.transpose(ps[5 + 2 * n][:, j * P:(j + 1) * P],
                                            picks[:, n * SC + j * P:n * SC + (j + 1) * P], ident)
                last.then_inc(s("pick_turned"), 1)
                pe.wait_ge(s("axm_ready"), i + 2)
                for n in range(2):
                    for f in range(FS):
                        pe.wait_ge(s("h1_ready"), i * 2 * FS + n * FS + f + 1)
                        t_.matmul(ps[f][:], lhsT=V["wiT"][:, f * P:(f + 1) * P], rhs=tC[:, ds(i * SC, SC)],
                                  start=True, stop=False)
                        t_.matmul(ps[f][:], lhsT=V["loraBT"][:, f * P:(f + 1) * P], rhs=axm[n],
                                  start=False, stop=True).then_inc(s("h1_done"), 1)
                pe.wait_ge(s("ffn1_in"), i + 1)
                pe.wait_ge(s("hsum_ready"), i * FS + 2 * FS)
                for j in range(ST):
                    o = ps[4][:, j * P:(j + 1) * P]
                    t_.matmul(o, lhsT=pred[0:1, P:2 * P], rhs=pred[0:1, 0:P], start=True, stop=False)
                    for f in range(FS):
                        last = t_.matmul(o, lhsT=tK[:, f * SC + j * P:f * SC + (j + 1) * P],
                                         rhs=V["wo1T"][:, f * P:(f + 1) * P], start=False, stop=f == FS - 1)
                last.then_inc(s("y1_done"), 1)
            pe.sem_inc(s("yo_done"), 1)
            pe.wait_ge(s("ffn1_in"), NS + 1)
            with pe.Fori(0, NS) as i:
                pe.wait_ge(s("yT_staged"), i + 1)
                pe.wait_ge(s("result_ready"), i + 1)
                for j in range(ST):
                    last = t_.matmul(ps[0][:, j * P:(j + 1) * P], lhsT=stage[:, j * P:(j + 1) * P],
                                     rhs=V["outT"], start=True, stop=True)
                last.then_inc(s("yo_done"), 1)
                pe.wait_ge(s("zs_staged"), i + 1)
                for j in range(ST):
                    last = t_.transpose(ps[1][:, j * P:(j + 1) * P],
                                        stage[:, 3 * SC + j * P:3 * SC + (j + 1) * P], ident)
                last.then_inc(s("zm_turned"), 1)
                pe.wait_ge(s("zmT_ready"), i + 1)
                for f in range(3):
                    t_.matmul(ps[2 + f][0:FT, :], lhsT=V["l1T"][:, f * FT:(f + 1) * FT], rhs=stage[:, 2 * SC:3 * SC],
                              start=True, stop=True).then_inc(s("l1_done"), 1)
                    t_.matmul(ps[5 + f][0:FT, :], lhsT=V["l2T"][:, f * FT:(f + 1) * FT], rhs=stage[:, 2 * SC:3 * SC],
                              start=True, stop=True).then_inc(s("l2_done"), 1)
                pe.wait_ge(s("gated_ready"), i * 3 + 3)
                for j in range(ST):
                    for f in range(3):
                        last = t_.matmul(ps[0][:, j * P:(j + 1) * P], lhsT=tK[0:FT, f * SC + j * P:f * SC + (j + 1) * P],
                                         rhs=V["l3T"][0:FT, f * P:(f + 1) * P], start=f == 0, stop=f == 2)
                last.then_inc(s("mlp_done"), 1)

        @block.gpsimd
        def _(pool):
            ch = Count(pool, pool_steps)
            link = ch.link
            g = nc.gpsimd
            g.memset(small[:, 11 * T:11 * T + 1], 1e-5)
            g.memset(small[:, 11 * T + 1:11 * T + 2], 1e-6).then_inc(s("eps_set"), 1)
            if stop == "A2":
                return
            v4 = qv.rearrange("p (t n) -> p t n", t=T)[:, :, P:2 * P].rearrange("p t (h d) -> p t h d", d=HD)
            rk = tK[:, 3072 + T * H:4096].rearrange("p (t h) -> p t h", h=H).unsqueeze(3).broadcast_to([P, T, H, HD])
            pool.wait_ge(s("silu_done"), 1)
            pool.wait_ge(s("scales_ready"), 1)
            g.tensor_tensor(v4, v4, rk, ALU.mult).then_inc(s("v_scaled"), 1)
            if stop == "A4":
                return
            pool.wait_ge(s("prepared"), 1)
            pool.wait_ge(s("v_scaled"), 1)
            pool.sem_inc(s("out_done"), 2)
            prod = tK[:, 2048:4096]
            prod4 = prod.rearrange("p (h j k) -> p h j k", h=H, j=J)
            p8 = prod.rearrange("p (n k) -> p n k", k=HD)
            sum4 = stage[:, 0:1024].rearrange("p (n k) -> p n k", k=4)
            sum2 = stage[:, 1024:1536].rearrange("p (n k) -> p n k", k=2)
            with pool.Fori(0, NS) as i:
                ch.enter(i, 3 * ST)
                for t in range(ST):
                    state = R[(t + 1) % 2].rearrange("p (h j k) -> p h j k", h=H, j=J)
                    q = tDE[:, ds(i * 2 * SC + t * 2 * P, P)].rearrange("p (h k) -> p h k", k=HD)
                    pool.wait_ge(s("state_ready"), i * ST + t + 1)
                    link(g.tensor_tensor(prod4, state, q.unsqueeze(2).broadcast_to([P, H, J, HD]), ALU.mult))
                    link(g.tensor_tensor(sum4, p8[:, :, 0:4], p8[:, :, 4:8], ALU.add))
                    link(g.tensor_tensor(sum2, sum4[:, :, 0:2], sum4[:, :, 2:4], ALU.add))
                    pool.sem_inc(s("waits_apart"), 1)
                    o = tDE[:, ds(i * 2 * SC + t * 2 * P, 2 * P)]
                    g.tensor_tensor(o, sum2[:, :, 0], sum2[:, :, 1], ALU.add).then_inc(s("out_done"), 1)
            ch.leave(NS)
            if stop in ("B", "C"):
                return
            pool.sem_inc(s("hsum_ready"), FS)
            with pool.Fori(0, NS) as i:
                pool.wait_ge(s("y1_done"), i + 1)
                for f in range(FS):
                    pool.wait_ge(s("h1_ready"), i * 2 * FS + 2 * FS + f + 1)
                    g.tensor_tensor(tK[:, f * SC:(f + 1) * SC], tJ[:, f * SC:(f + 1) * SC],
                                    tJ[:, (FS + f) * SC:(FS + f + 1) * SC], ALU.add).then_inc(s("hsum_ready"), 1)


def kernel(**inputs):
    import numpy as np
    import concourse.bacc as bacc
    from concourse.bass_utils import run_bass_kernel_spmd as run

    a = {k: np.asarray(v) for k, v in inputs.items()}
    f32 = np.float32

    def rows(x, n=P):
        return np.broadcast_to(x.reshape(1, -1), (n, x.size))

    def padded(x, n=P):
        out = np.zeros((n,) + x.shape[1:], f32)
        out[:x.shape[0]] = x
        return out

    def col(x):
        return padded(x.reshape(-1, 1))

    p = np.arange(P)
    A, Fn, A1, F1 = "L0_attn_", "L0_ffn_", "L1_attn_", "L1_ffn_"
    fixed = dict(
        ident=np.eye(P, dtype=f32), headmask=(p[:, None] // HD == np.arange(H)[None]).astype(f32),
        headmean=(p[:, None] // HD == p[None] // HD).astype(f32) / HD,
        first=-(p % C == 0).astype(f32).reshape(P, 1), descend=rows(np.arange(E0, 0, -1).astype(f32)),
        woT=a[A + "Wo"].T, norm_w=np.tile(a[A + "norm_w"], H).reshape(P, 1),
        ln_g=col(a[Fn + "ln_g"]), ln_b=col(a[Fn + "ln_b"]),
        b1=a[Fn + "b1"].reshape(E0 * FS, P).T, b2=padded(a[Fn + "b2"]))
    qkv = ("q", "k", "v")
    early = dict(
        wqkvT=np.concatenate([a[A + "W" + n].T for n in qkv], 1),
        conv=rows(np.concatenate([a[A + f"w{n}_conv"][:, i] for i in range(K0) for n in qkv])),
        brow=rows(np.concatenate([a[A + "b" + n] for n in qkv])),
        wbrT=np.concatenate([a[A + "Wbeta"].T, a[Fn + "Wr"]], 1),
        taps=np.concatenate([a[A + f"w{n}_conv"] for n in qkv], 1),
        bqkv=np.stack([a[A + "b" + n] for n in qkv], 1),
        bconv=np.stack([a[A + f"b{n}_conv"] for n in qkv], 1),
        bbr=col(np.concatenate([a[A + "bbeta"], a[Fn + "br"]])))
    sw = a[A1 + "short_w"].reshape(3 * P, K1)
    last = dict(
        short=rows(np.concatenate([sw[:, i] for i in range(K1)])),
        wiT=a[F1 + "wi"].T, wo1T=a[F1 + "wo"].T.reshape(FS, P, P).transpose(1, 0, 2).reshape(P, FS * P),
        loraBT=a[F1 + "lora_B"].transpose(0, 2, 1).reshape(E1 * RK, F0))
    late = dict(
        bo=rows(a[A + "bo"]), inT=a[A1 + "in_proj_w"].T,
        shortb=a[A1 + "short_b"].reshape(3, P).T, poles=a[A1 + "log_poles"].reshape(P, NP1),
        res=a[A1 + "residues"], skip=col(a[A1 + "D_skip"]), outT=a[A1 + "out_proj_w"].T,
        pre_w=col(a[A1 + "pre_norm_w"]), post_w=col(a[A1 + "post_norm_w"]),
        l1T=a[A1 + "l1_w"].T, l2T=a[A1 + "l2_w"].T,
        l3T=padded(a[A1 + "l3_w"].T.reshape(3, FT, P).transpose(1, 0, 2).reshape(FT, 3 * P)),
        bi=a[F1 + "bi"].reshape(FS, P).T,
        loraAT=a[F1 + "lora_A"].reshape(E1 * RK, P).T,
        gateT=a[F1 + "gate_w"].T, gateb=col(a[F1 + "gate_b"]), bo1=rows(a[F1 + "bo"]))

    def packed(pack, parts):
        return np.ascontiguousarray(np.concatenate([parts[name].reshape(P, n) for name, n in pack], 1))

    arrays = {
        "x": np.ascontiguousarray(a[A + "x"].reshape(P, T * P)),
        "fixed": packed(FIXED, fixed), "early": packed(EARLY, early), "late": packed(LATE, late),
        "last": packed(LAST, last),
        "w1": np.ascontiguousarray(a[Fn + "W1"].transpose(1, 0, 2).reshape(P, E0 * F0)),
        "w2": np.ascontiguousarray(a[Fn + "W2"].reshape(E0, FS, P, P).transpose(2, 0, 1, 3).reshape(P, E0 * F0)),
    }
    nc = bacc.Bacc("TRN2", target_bir_lowering=False, num_devices=1)
    aps = [nc.dram_tensor(n, v.shape, mybir.dt.float32, kind="ExternalInput").ap() for n, v in arrays.items()]
    out = nc.dram_tensor("out", (P, T * P), mybir.dt.float32, kind="ExternalOutput").ap()
    two_layers(nc, *aps, out, stop=STOP)
    r = run(nc, [arrays], core_ids=[0])
    return r.results[0]["out"].reshape(B, L, D)


STOP = None
```

```python
import concourse.bass as bass
from concourse import mybir
from contextlib import ExitStack

B, L, D = 4, 1024, 128
P = 128
C = 32
T = L // C
N = B * L
H, HD = 16, 8
J = 2 * HD
K0, K1 = 4, 3
E0, F0 = 8, 512
FS = F0 // P
E1, RK = 8, 16
NP1 = 16
FF, FT = 336, 112
ST = 4
SC = ST * P
NS = T // ST
MASK_AT, WEIGH_AT = 5, 7
OUTS_AT = 4

FIXED = [("ident", P), ("headmask", H), ("headmean", 32), ("headspread", P), ("first", 1), ("descend", E0), ("woT", P),
         ("norm_w", 1), ("ln_g", 1), ("ln_b", 1), ("b1", E0 * FS), ("b2", P)]
EARLY = [("wqkvT", 3 * P), ("conv", K0 * 3 * P), ("brow", 3 * P), ("wbrT", H + E0), ("taps", 3 * K0),
         ("bqkv", 3), ("bconv", 3), ("bbr", 1)]
LATE = [("bo", P), ("inT", 3 * P), ("shortb", 3), ("poles", NP1), ("res", NP1), ("skip", 1),
        ("outT", P), ("pre_w", 1), ("post_w", 1), ("l1T", FF), ("l2T", FF), ("l3T", 3 * P),
        ("bi", FS), ("loraAT", P), ("gateT", E1), ("gateb", 1), ("bo1", P)]
LAST = [("short", K1 * 3 * P), ("wiT", F0), ("wo1T", FS * P), ("loraBT", F0)]


def width(pack):
    return sum(n for _, n in pack)


def columns(tile, pack):
    at, out = 0, {}
    for name, n in pack:
        out[name] = tile[:, at:at + n]
        at += n
    return out


class Count:

    def __init__(self, eng, sem):
        self.eng, self.sem, self.base, self.n = eng, sem, 0, 0

    def link(self, ins):
        ins.then_inc(self.sem, 1)
        self.n += 1
        self.eng.wait_ge(self.sem, self.base + self.n)

    def enter(self, i, per):
        self.outer, self.per = self.base + self.n, per
        self.base, self.n = self.outer + i * per, 0

    def leave(self, times):
        assert self.n == self.per, (self.n, self.per)
        self.base, self.n = self.outer + times * self.per, 0


def two_layers(nc, x_d, fixed_d, early_d, late_d, last_d, w1_d, w2_d, out_d, maps_d, states_d, stop=None):
    fp32 = mybir.dt.float32
    ALU = mybir.AluOpType
    ACT = mybir.ActivationFunctionType
    AX = mybir.AxisListType
    ds = bass.ds
    ctx = ExitStack()
    with ctx:
        def sb(name, cols):
            return ctx.enter_context(nc.sbuf_tensor(name, [P, cols], fp32))

        def sem(name):
            return ctx.enter_context(nc.semaphore(name))

        tA = sb("tA", N)
        tB = sb("tB", N)
        tC = sb("tC", N + (K0 - 1) * P)
        tDE = sb("tDE", 2 * N)
        tF = sb("tF", N)
        tG = sb("tG", N)
        tH = sb("tH", N)
        tI = sb("tI", N)
        tJ = sb("tJ", N)
        tK = sb("tK", N)
        wt = sb("wt", max(width(EARLY), width(LATE)))
        fx = sb("fx", width(FIXED))
        stage = sb("stage", 4 * SC)
        small = sb("small", 12 * T)
        brt = sb("brt", T * (H + E0))
        gates = sb("gates", 4 * T * E0)
        stats = sb("stats", 6 * T)
        pred = sb("pred", H * J)
        biasq = sb("biasq", 4)
        ps = [ctx.enter_context(nc.psum_tensor(f"ps{n}", [P, SC], fp32)) for n in range(8)]

        F = columns(fx, FIXED)
        W = columns(wt, EARLY)
        V = columns(wt, LATE)
        V.update(columns(tH[:, N - width(LAST):N], LAST))
        ident = F["ident"]

        x_in, fixed_in, early_in, late_in = sem("x_in"), sem("fixed_in"), sem("early_in"), sem("late_in")
        last_in = sem("last_in")
        maps_out, maps_in, states_out, states_in = sem("maps_out"), sem("maps_in"), sem("states_out"), sem("states_in")
        w1_in, w2_in, x_again, out_sent = sem("w1_in"), sem("w2_in"), sem("x_again"), sem("out_sent")
        dve_steps, act_steps, pool_steps = sem("dve_steps"), sem("act_steps"), sem("pool_steps")
        S = {}

        def s(name):
            if name not in S:
                S[name] = sem(name)
            return S[name]

        block = ctx.enter_context(nc.Block())

        xnT0 = tC[:, (K0 - 1) * P:]
        qv = tDE[:]
        k_tm, kb_tm = tF, tG
        fold0 = tK[:, 0:K0 * 3 * P]
        corr = tK[:, 1536:1536 + 3 * 384]
        mean, var, rstd, tmp1, tmp2 = (small[:, n * T:(n + 1) * T] for n in range(5))
        mask0 = gates[:, 0:T * E0]
        R = [tJ[:, 0:2048], tJ[:, 2048:4096]]

        znT, fold1 = tDE[:, 0:N + (K1 - 1) * P], tH[:, 0:K1 * 3 * P]
        scan = [tDE[:, 4352 + n * L:4352 + (n + 1) * L] for n in range(2)]
        picks = tDE[:, 6400:6400 + 2 * SC]
        axs = tK[:, 4 * SC:5 * SC]
        axm = [[stage[:, (2 * u + n) * SC:(2 * u + n + 1) * SC] for n in range(2)] for u in range(2)]
        m_prob = gates[:, 2 * T * E0:3 * T * E0]

        chainM, chainN = tC[:, 0:2048], tC[:, 2048:3072]
        chainS = tC[:, 3072:3072 + (C + 1) * 32]
        Sst = tK[:, 1024:2048]

        @block.sync
        def _(sp):
            sp.dma_start(tA[:], x_d).then_inc(x_in, 16)
            sp.dma_start(fx[:], fixed_d).then_inc(fixed_in, 16)
            sp.dma_start(wt[:, 0:width(EARLY)], early_d).then_inc(early_in, 16)
            sp.dma_start(tH[:], w1_d).then_inc(w1_in, 16)
            sp.dma_start(tI[:], w2_d).then_inc(w2_in, 16)
            if stop == "A2":
                sp.wait_ge(s("xnT_ready"), NS)
                sp.wait_ge(s("xeT_ready"), NS)
                sp.dma_start(out_d, tB[:]).then_inc(out_sent, 16)
                sp.wait_ge(out_sent, 16)
                return
            if stop == "A4":
                sp.wait_ge(s("prepared"), 1)
                sp.wait_ge(s("v_scaled"), 1)
                sp.dma_start(out_d, tG[:]).then_inc(out_sent, 16)
                sp.wait_ge(out_sent, 16)
                return
            sp.wait_ge(s("qkv_in"), NS + 1)
            sp.wait_ge(s("corrected"), 1)
            sp.dma_start(wt[:, 0:width(LATE)], late_d).then_inc(late_in, 16)
            sp.wait_ge(s("state_ready"), T)
            sp.dma_start(maps_d.rearrange("b c h n -> (b c) h n"),
                         R[0].rearrange("p (h n) -> p h n", h=H)).then_inc(maps_out, 16)
            sp.wait_ge(maps_out, 16)
            sp.wait_ge(s("y0_ready"), NS * E0 + 2)
            for half in range(2):
                for b in range(B):
                    p0 = half * 64 + b * H
                    sp.dma_start(chainM[p0:p0 + H, :].rearrange("h (c n) -> h c n", c=C),
                                 maps_d[b][:, :, 0:64].rearrange("c h n -> h c n")).then_inc(maps_in, 16)
                    n0 = 64 + half * 32
                    sp.dma_start(chainN[p0:p0 + H, :].rearrange("h (c n) -> h c n", c=C),
                                 maps_d[b][:, :, n0:n0 + 32].rearrange("c h n -> h c n")).then_inc(maps_in, 16)
            sp.dma_start(tI[:], x_d).then_inc(x_again, 16)
            sp.wait_ge(s("chained"), C)
            for half in range(2):
                for b in range(B):
                    p0 = half * 64 + b * H
                    sp.dma_start(states_d[b][:, :, half, :].rearrange("c h n -> h c n"),
                                 chainS[p0:p0 + H, 0:C * 32].rearrange("h (c n) -> h c n", c=C)
                                 ).then_inc(states_out, 16)
            sp.wait_ge(states_out, 16 * 2 * B)
            sp.dma_start(tK[:, 0:1024].rearrange("p (h n) -> p h n", h=H),
                         states_d.rearrange("b c h a n -> (b c) h (a n)")).then_inc(states_in, 16)
            if stop == "B":
                sp.wait_ge(s("y0_used"), NS * E0 + 2)
                sp.wait_ge(s("out_done"), T + 2)
                sp.dma_start(out_d, tDE[:, 0:N]).then_inc(out_sent, 16)
                sp.wait_ge(out_sent, 16)
                return
            if stop == "C":
                sp.wait_ge(s("x1_ready"), NS)
                sp.dma_start(out_d, tA[:]).then_inc(out_sent, 16)
                sp.wait_ge(out_sent, 16)
                return
            sp.wait_ge(s("inter_done"), NS + 2)
            sp.dma_start(tH[:, N - width(LAST):N], last_d).then_inc(last_in, 16)
            with sp.Fori(0, NS) as i:
                sp.wait_ge(s("result_ready"), i + 2)
                sp.dma_start(out_d[:, ds(i * SC, SC)], tA[:, ds(i * SC, SC)]).then_inc(out_sent, 16)
            sp.wait_ge(out_sent, 16 * NS)

        @block.vector
        def _(dve):
            ch = Count(dve, dve_steps)
            link = ch.link
            v = nc.vector

            def row_stats(x, mean_o, var_o):
                with dve.Fori(0, NS) as i:
                    for j in range(ST):
                        last = v.bn_stats(stats[:, ds(i * 6 * ST + 6 * j, 6)], x[:, ds(i * SC + j * P, P)])
                    ch.enter(i, 1)
                    link(last)
                ch.leave(NS)
                st = stats[:].rearrange("p (t s) -> p t s", s=6)
                link(v.tensor_tensor(mean_o, st[:, :, 1], st[:, :, 4], ALU.add))
                link(v.tensor_scalar(mean_o, mean_o, 0.5, None, ALU.mult))
                link(v.tensor_tensor(tmp1, st[:, :, 1], mean_o, ALU.subtract))
                link(v.tensor_tensor(tmp1, tmp1, tmp1, ALU.mult))
                link(v.tensor_tensor(tmp2, st[:, :, 2], st[:, :, 5], ALU.add))
                link(v.tensor_scalar(tmp2, tmp2, 1.0 / P, None, ALU.mult))
                return v.tensor_tensor(var_o, tmp1, tmp2, ALU.add)

            def normalise(x, y):
                with dve.Fori(0, NS) as i:
                    for j in range(ST):
                        c = i * SC + j * P
                        last = v.tensor_scalar(y[:, ds(c, P)], x[:, ds(c, P)], mean[:, ds(i * ST + j, 1)],
                                               rstd[:, ds(i * ST + j, 1)], ALU.subtract, ALU.mult)
                    ch.enter(i, 1)
                    link(last)
                ch.leave(NS)

            dve.wait_ge(x_in, 16)
            row_stats(tA, mean, var).then_inc(s("var_ready"), 1)
            dve.wait_ge(s("std_ready"), 1)
            link(v.reciprocal(rstd, rstd))
            normalise(tA, tA)
            row_stats(tA, mean, var).then_inc(s("var_ready"), 1)
            dve.wait_ge(early_in, 16)
            wb = W["wqkvT"].unsqueeze(1).broadcast_to([P, K0, 3 * P])
            v.tensor_tensor(fold0.rearrange("p (i n) -> p i n", i=K0), wb,
                            W["conv"].rearrange("p (i n) -> p i n", i=K0), ALU.mult).then_inc(s("fold0_ready"), 1)
            link(v.tensor_reduce(biasq[:, 0:3], W["taps"].rearrange("p (a i) -> p a i", i=K0), AX.X, ALU.add))
            link(v.tensor_tensor(biasq[:, 0:3], biasq[:, 0:3], W["bqkv"], ALU.mult))
            v.tensor_tensor(biasq[:, 0:3], biasq[:, 0:3], W["bconv"], ALU.add).then_inc(s("biasq_ready"), 1)
            cb = W["conv"].rearrange("p (i n) -> p i n", i=K0)
            cr = corr.rearrange("p (t n) -> p t n", t=3)
            link(v.tensor_tensor(cr, cb[:, 0:3, :], W["brow"].unsqueeze(1).broadcast_to([P, 3, 384]), ALU.mult))
            link(v.tensor_tensor(cr[:, 1, :], cr[:, 0, :], cr[:, 1, :], ALU.add))
            link(v.tensor_tensor(cr[:, 2, :], cr[:, 1, :], cr[:, 2, :], ALU.add))
            dve.wait_ge(s("std_ready"), 2)
            link(v.reciprocal(rstd, rstd))
            with dve.Fori(0, NS) as i:
                dve.wait_ge(s("xe_turned"), i + 1)
                for j in range(ST):
                    last = v.tensor_scalar(stage[:, SC + j * P:SC + (j + 1) * P], tA[:, ds(i * SC + j * P, P)],
                                           mean[:, ds(i * ST + j, 1)], rstd[:, ds(i * ST + j, 1)],
                                           ALU.subtract, ALU.mult)
                last.then_inc(s("xe_staged"), 1)
                dve.wait_ge(s("xe_turned"), i + 2)
                v.tensor_scalar(tB[:, ds(i * SC, SC)], ps[1][:], F["ln_g"], F["ln_b"],
                                ALU.mult, ALU.add).then_inc(s("xeT_ready"), 1)
            link(v.memset(tC[:, 0:(K0 - 1) * P], 0.0))
            dve.wait_ge(s("xnT_ready"), NS)
            halo = tC[:, 0:(K0 - 1) * P].rearrange("p (t b c) -> p t b c", b=B, c=C)
            src = xnT0[:, (T - K0 + 1) * P:T * P].rearrange("p (t b c) -> p t b c", b=B, c=C)
            for t in range(K0 - 1):
                last = v.tensor_copy(halo[:, t, :, 1:C], src[:, t, :, 0:C - 1])
            last.then_inc(s("halo0_ready"), 1)
            if stop == "A2":
                return

            dve.sem_inc(s("qkv_in"), 1)
            with dve.Fori(0, NS) as i:
                dve.wait_ge(s("qkv_turned"), i + 2)
                qvi = qv[:, ds(i * 2 * SC, 2 * SC)].rearrange("p (t n) -> p t n", t=ST)
                v.tensor_copy(qvi[:, :, 0:P], ps[4][:].rearrange("p (t n) -> p t n", t=ST))
                v.tensor_copy(k_tm[:, ds(i * SC, SC)], ps[5][:])
                v.tensor_copy(qvi[:, :, P:2 * P], ps[6][:].rearrange("p (t n) -> p t n", t=ST))
                v.tensor_copy(brt[:, ds(i * ST * (H + E0), ST * (H + E0))],
                              ps[7][:, 0:ST * (H + E0)]).then_inc(s("qkv_in"), 1)
            dve.wait_ge(s("qkv_in"), NS + 1)
            qvt = qv.rearrange("p (t n) -> p t n", t=T)
            kt = k_tm[:].rearrange("p (t n) -> p t n", t=T)
            for t in range(3):
                row = cr[:, 2 - t, :]
                for dst, o in ((qvt[:, t, 0:P], 0), (kt[:, t, :], P), (qvt[:, t, P:2 * P], 2 * P)):
                    last = v.scalar_tensor_tensor(out=dst, in0=row[:, o:o + P], scalar=F["first"], in1=dst,
                                                  op0=ALU.mult, op1=ALU.add)
            last.then_inc(s("corrected"), 1)
            dve.wait_ge(s("corrected"), 1)

            bt = brt[:].rearrange("p (t n) -> p t n", t=T)
            logit = bt[:, :, H:H + E0]
            m3 = [gates[:, n * T * E0:(n + 1) * T * E0].rearrange("p (t e) -> p t e", e=E0) for n in range(4)]

            def over_e(col):
                return col.unsqueeze(2).broadcast_to([P, T, E0])

            desc = F["descend"].unsqueeze(1).broadcast_to([P, T, E0])
            top = small[:, 5 * T:6 * T]
            link(v.tensor_reduce(top, logit, AX.X, ALU.max))
            v.tensor_tensor(m3[1], logit, over_e(top), ALU.subtract).then_inc(s("shifted0"), 1)
            link(v.tensor_tensor(m3[0], logit, over_e(top), ALU.is_equal))
            link(v.tensor_tensor(m3[0], m3[0], desc, ALU.mult))
            link(v.tensor_reduce(top, m3[0], AX.X, ALU.max))
            link(v.tensor_tensor(m3[0], m3[0], over_e(top), ALU.is_equal))
            dve.wait_ge(s("exp0_ready"), 1)
            link(v.tensor_reduce(top, m3[1], AX.X, ALU.add))
            link(v.reciprocal(top, top))
            v.tensor_tensor(m3[0], m3[0], over_e(top), ALU.mult).then_inc(s("mask0_ready"), 1)

            q2 = tJ[:].rearrange("p (n d) -> p n d", d=HD)
            norms = tK[:, 3072:4096]
            dve.wait_ge(s("q_squared"), 1)
            v.tensor_reduce(norms[:, 0:T * H], q2, AX.X, ALU.add).then_inc(s("q2_summed"), 1)
            dve.wait_ge(s("k_squared"), 1)
            v.tensor_reduce(norms[:, T * H:2 * T * H], q2, AX.X, ALU.add).then_inc(s("norms_summed"), 1)
            dve.wait_ge(s("norms_ready"), 1)
            link(v.tensor_scalar(norms, norms, 1e-6, None, ALU.add))
            v.reciprocal(norms, norms).then_inc(s("scales_ready"), 1)
            dve.wait_ge(s("scales_ready"), 1)

            def by_head(cols):
                return cols.rearrange("p (t h) -> p t h", h=H).unsqueeze(3).broadcast_to([P, T, H, HD])

            q4 = qvt[:, :, 0:P].rearrange("p t (h d) -> p t h d", d=HD)
            k4 = kt.rearrange("p t (h d) -> p t h d", d=HD)
            kb4 = kb_tm[:].rearrange("p (t h d) -> p t h d", h=H, d=HD)
            link(v.tensor_tensor(k4, k4, by_head(norms[:, T * H:2 * T * H]), ALU.mult))
            dve.wait_ge(s("beta_ready"), 1)
            v.tensor_tensor(kb4, k4, bt[:, :, 0:H].unsqueeze(3).broadcast_to([P, T, H, HD]), ALU.mult)
            link(v.tensor_tensor(q4, q4, by_head(norms[:, 0:T * H]), ALU.mult))
            link(v.memset(R[0], 0.0))
            link(v.memset(R[0].rearrange("p (h n) -> p h n", h=H)[:, :, 0:64:9], 1.0))
            v.memset(tA[:], 0.0).then_inc(s("prepared"), 1)
            dve.wait_ge(s("prepared"), 1)
            dve.wait_ge(s("v_scaled"), 1)
            if stop == "A4":
                return

            prod = tK[:, 0:2048]
            prod4 = prod.rearrange("p (h j k) -> p h j k", h=H, j=J)
            pr3 = pred[:].rearrange("p (h j) -> p h j", h=H)
            dve.sem_inc(s("y0_used"), 2)

            def heads(tile, col):
                return tile[:, ds(col, P)].rearrange("p (h k) -> p h k", k=HD).unsqueeze(2).broadcast_to([P, H, J, HD])

            with dve.Fori(0, NS) as i:
                ch.enter(i, 4 * ST)
                for e in range(E0):
                    t = e // 2
                    cur, nxt = R[t % 2], R[(t + 1) % 2]
                    cur4 = cur.rearrange("p (h j k) -> p h j k", h=H, j=J)
                    nxt4 = nxt.rearrange("p (h j k) -> p h j k", h=H, j=J)
                    if e % 2 == 0:
                        link(v.tensor_tensor(prod4, cur4, heads(k_tm, i * SC + t * P), ALU.mult))
                        link(v.tensor_reduce(pr3, prod4, AX.X, ALU.add))
                        link(v.tensor_tensor(pr3[:, :, HD:J], pr3[:, :, HD:J],
                                             qv[:, ds(i * 2 * SC + t * 2 * P + P, P)].rearrange(
                                                 "p (h k) -> p h k", k=HD), ALU.subtract))
                    else:
                        link(v.tensor_tensor(prod4, heads(kb_tm, i * SC + t * P),
                                             pr3.unsqueeze(3).broadcast_to([P, H, J, HD]), ALU.mult))
                        dve.wait_ge(s("out_done"), i * ST + t + 1)
                        v.tensor_tensor(nxt4, cur4, prod4, ALU.subtract).then_inc(s("state_ready"), 1)
                        dve.wait_ge(s("state_ready"), i * ST + t + 1)
                    dve.wait_ge(s("y0_ready"), i * E0 + e + 3)
                    dve.wait_ge(s("y0_used"), i * E0 + e + 2)
                    for j in range(ST):
                        yj = tA[:, ds(i * SC + j * P, P)]
                        last = v.scalar_tensor_tensor(out=yj, in0=ps[4 + e % 2][:, j * P:(j + 1) * P],
                                                      scalar=mask0[:, ds(i * ST * E0 + j * E0 + e, 1)],
                                                      in1=yj, op0=ALU.mult, op1=ALU.add)
                    last.then_inc(s("y0_used"), 1)
            ch.leave(NS)
            if stop == "B":
                return

            chain_prod = pred[:].rearrange("p (v k j) -> p v k j", v=HD // 2, k=HD)
            hm = F["headmask"]
            dve.wait_ge(maps_in, 16 * 4 * B)
            link(v.memset(chainS[:, 0:32], 0.0))
            for c in range(C):
                prev = chainS[:, c * 32:(c + 1) * 32].rearrange("p (v j) -> p v j", j=HD)
                nxt = chainS[:, (c + 1) * 32:(c + 2) * 32]
                mc = chainM[:, c * 64:(c + 1) * 64].rearrange("p (j k) -> p k j", k=HD)
                link(v.tensor_tensor(chain_prod, prev.unsqueeze(2).broadcast_to([P, HD // 2, HD, HD]),
                                     mc.unsqueeze(1).broadcast_to([P, HD // 2, HD, HD]), ALU.mult))
                link(v.tensor_reduce(nxt.rearrange("p (v k) -> p v k", k=HD), chain_prod, AX.X, ALU.add))
                v.tensor_tensor(nxt, nxt, chainN[:, c * 32:(c + 1) * 32], ALU.add).then_inc(s("chained"), 1)
                dve.wait_ge(s("chained"), c + 1)
            dve.wait_ge(states_in, 16)
            dve.wait_ge(s("out_done"), T + 2)
            v.tensor_copy(tK[:, 2048:3072].rearrange("p (v h k) -> p h v k", v=HD, h=H),
                          tK[:, 0:1024].rearrange("p (h v k) -> p h v k", h=H, v=HD)).then_inc(s("states_sorted"), 1)
            dve.wait_ge(s("states_turned"), 1)
            for n in range(2):
                last = v.tensor_copy(
                    Sst.rearrange("p (c b v) -> p v b c", c=C, b=B)[:, n * 4:(n + 1) * 4, :, :],
                    ps[2 + n][:].rearrange("p (v b c) -> p v b c", v=4, b=B))
            link(last)

            def by_chunk(tile):
                return tile[:].rearrange("p (t b c) -> p c b t", b=B, c=C)

            dve.sem_inc(s("oT_ready"), 2)

            def widen(n, u):
                dve.wait_ge(s("inter_done"), n + 1)
                v.tensor_tensor(
                    tH[:, u * 2048:(u + 1) * 2048].rearrange("p (n h v) -> p n h v", n=ST * B, h=H),
                    Sst[:, ds(n * ST * B * HD, ST * B * HD)].rearrange(
                        "p (n v) -> p n v", n=ST * B).unsqueeze(2).broadcast_to([P, ST * B, H, HD]),
                    hm.unsqueeze(1).unsqueeze(3).broadcast_to([P, ST * B, H, HD]),
                    ALU.mult).then_inc(s("state_wide"), 1)

            def add_own(n, u):
                dve.wait_ge(s("inter_done"), n + 3)
                v.tensor_tensor(
                    by_chunk(tB)[:, ds(n * ST, ST), :, :],
                    ps[u][:].rearrange("p (c b t) -> p c b t", c=ST, b=B),
                    by_chunk(tG)[:, ds(n * ST, ST), :, :], ALU.add).then_inc(s("oT_ready"), 1)

            dve.wait_ge(s("outs_in"), NS)
            widen(0, 0)
            with dve.Fori(0, NS // 2 - 1) as i:
                for u in range(2):
                    widen(i * 2 + u + 1, 1 - u)
                    add_own(i * 2 + u, u)
            widen(NS - 1, 1)
            add_own(NS - 2, 0)
            add_own(NS - 1, 1)
            for g in range(2):
                dve.wait_ge(s("oroot_ready"), g + 1)
                v.reciprocal(tK[:, 3072 + g * SC:3072 + (g + 1) * SC],
                             tK[:, 3072 + g * SC:3072 + (g + 1) * SC]).then_inc(s("oscale_ready"), 1)
            dve.wait_ge(s("x_biased"), 1)

            def scale_o(i):
                dve.wait_ge(s("spread_done"), i + 1)
                if i >= 2:
                    dve.wait_ge(s("wo0_done"), i - 1)
                v.scalar_tensor_tensor(out=stage[:, (i % 2) * SC:(i % 2 + 1) * SC], in0=tB[:, i * SC:(i + 1) * SC],
                                       scalar=F["norm_w"], in1=ps[2 + i % 2][:],
                                       op0=ALU.mult, op1=ALU.mult).then_inc(s("onT_ready"), 1)

            scale_o(0)
            for i in range(NS):
                if i + 1 < NS:
                    scale_o(i + 1)
                xi = tA[:, i * SC:(i + 1) * SC]
                dve.wait_ge(s("wo0_done"), i + 1)
                link(v.tensor_tensor(xi, ps[4 + i % 2][:], xi, ALU.add))
                v.tensor_tensor(xi, xi, tI[:, i * SC:(i + 1) * SC], ALU.add).then_inc(s("x1_ready"), 1)
            if stop == "C":
                return
            dve.wait_ge(s("x1_ready"), NS)
            row_stats(tA, mean, var).then_inc(s("var_ready"), 1)
            dve.wait_ge(s("std_ready"), 3)
            link(v.reciprocal(rstd, rstd))
            normalise(tA, tG)
            link(row_stats(tG, mean, var))
            link(v.tensor_tensor(mean, mean, mean, ALU.mult))
            v.tensor_tensor(var, var, mean, ALU.add).then_inc(s("var_ready"), 1)
            dve.wait_ge(last_in, 16)
            v.tensor_tensor(fold1.rearrange("p (i n) -> p i n", i=K1),
                            V["inT"].unsqueeze(1).broadcast_to([P, K1, 3 * P]),
                            V["short"].rearrange("p (i n) -> p i n", i=K1), ALU.mult).then_inc(s("fold1_ready"), 1)
            dve.wait_ge(s("std_ready"), 4)
            link(v.reciprocal(rstd, rstd))
            with dve.Fori(0, NS) as i:
                dve.wait_ge(s("zn_turned"), i + 1)
                v.tensor_tensor(stage[:, SC:2 * SC].rearrange("p (t n) -> p t n", t=ST),
                                tG[:, ds(i * SC, SC)].rearrange("p (t n) -> p t n", t=ST),
                                rstd[:, ds(i * ST, ST)].unsqueeze(2).broadcast_to([P, ST, P]),
                                ALU.mult).then_inc(s("zn_staged"), 1)
                dve.wait_ge(s("zn_turned"), i + 2)
                v.tensor_scalar(znT[:, ds((K1 - 1) * P + i * SC, SC)], ps[1][:], V["pre_w"], None,
                                ALU.mult).then_inc(s("znT_ready"), 1)
            link(v.memset(znT[:, 0:(K1 - 1) * P], 0.0))
            dve.wait_ge(s("znT_ready"), NS)
            halo1 = znT[:, 0:(K1 - 1) * P].rearrange("p (t b c) -> p t b c", b=B, c=C)
            src1 = znT[:, T * P:(T + K1 - 1) * P].rearrange("p (t b c) -> p t b c", b=B, c=C)
            for t in range(K1 - 1):
                last = v.tensor_copy(halo1[:, t, :, 1:C], src1[:, t, :, 0:C - 1])
            last.then_inc(s("halo1_ready"), 1)
            dve.sem_inc(s("xv_ready"), 2)
            dve.sem_inc(s("gate1_in"), 1)
            with dve.Fori(0, NS // 2) as m:
                for u in range(2):
                    i = 2 * m + u
                    dve.wait_ge(s("z_out"), i + 3)
                    v.scalar_tensor_tensor(
                        out=tF[:].rearrange("p (n t) -> p t n", t=T)[:, ds(i * ST, ST), :],
                        in0=ps[4 * u + 2][:].rearrange("p (t n) -> p t n", t=ST), scalar=V["shortb"][:, 2:3],
                        in1=stage[:, u * SC:(u + 1) * SC].rearrange("p (t n) -> p t n", t=ST),
                        op0=ALU.add, op1=ALU.mult).then_inc(s("xv_ready"), 1)
                    dve.wait_ge(s("gate1_turned"), i + 1)
                    v.tensor_copy(brt[:, ds(i * ST * E1, ST * E1)], ps[7][:, 0:ST * E1]).then_inc(s("gate1_in"), 1)
            dve.wait_ge(s("gate1_in"), NS + 1)
            lg = brt[:, 0:T * E1].rearrange("p (t e) -> p t e", e=E1)
            one, two, prob, work = m3
            link(v.tensor_reduce(top, lg, AX.X, ALU.max))
            v.tensor_tensor(prob, lg, over_e(top), ALU.subtract).then_inc(s("shifted1"), 1)
            dve.wait_ge(s("exp1_ready"), 1)
            link(v.tensor_reduce(top, prob, AX.X, ALU.add))
            link(v.reciprocal(top, top))
            link(v.tensor_tensor(prob, prob, over_e(top), ALU.mult))
            for n, pick in ((0, one), (1, two)):
                best = small[:, (6 + n) * T:(7 + n) * T]
                link(v.tensor_reduce(best, prob, AX.X, ALU.max))
                link(v.tensor_tensor(pick, prob, over_e(best), ALU.is_equal))
                link(v.tensor_tensor(pick, pick, desc, ALU.mult))
                link(v.tensor_reduce(top, pick, AX.X, ALU.max))
                link(v.tensor_tensor(pick, pick, over_e(top), ALU.is_equal))
                if n == 0:
                    link(v.scalar_tensor_tensor(out=prob, in0=pick, scalar=-4.0, in1=prob, op0=ALU.mult, op1=ALU.add))
            link(v.tensor_tensor(two, two, one, ALU.subtract))
            weight = small[:, 6 * T:7 * T]
            link(v.tensor_tensor(weight, weight, small[:, 7 * T:8 * T], ALU.add))
            v.memset(pred[0:1, P:2 * P], 1.0)
            v.tensor_scalar(pred[0:1, 0:P], V["bo1"][0:1, :], 2.0, None, ALU.mult).then_inc(s("picks_ready"), 1)
            dve.wait_ge(s("decay_ready"), 1)
            dve.wait_ge(s("xv_ready"), NS + 2)
            dve.sem_inc(s("ffn1_in"), 1)

            def mask_ranks(i, u):
                dve.wait_ge(s("pick_turned"), i + 2)
                dve.wait_ge(s("axs_ready"), i + 2)
                v.tensor_tensor(axm[u][0], ps[5][:], axs, ALU.mult)
                v.tensor_tensor(axm[u][1], ps[7][:], axs, ALU.mult).then_inc(s("axm_ready"), 1)

            def weigh(i):
                dve.wait_ge(s("y1_done"), i + 2)
                v.tensor_tensor(tI[:, ds(i * SC, SC)].rearrange("p (t n) -> p t n", t=ST),
                                ps[4][:].rearrange("p (t n) -> p t n", t=ST),
                                weight[:, ds(i * ST, ST)].unsqueeze(2).broadcast_to([P, ST, P]),
                                ALU.mult).then_inc(s("ffn1_in"), 1)

            def filter_batch(b, first=False, final=False):
                xb = tF[:, ds(b * L, L)]
                yb = tH[:, 0:L]
                link(v.tensor_scalar(yb, xb, V["skip"], None, ALU.mult))
                for n in range(NP1):
                    u, slot = n // 8, n % 8
                    if slot == MASK_AT and not (final and u == 1):
                        mask_ranks(2 * b + u + 1, 1 - u)
                    sn = scan[n % 2]
                    link(v.tensor_tensor_scan(sn, V["poles"][:, n:n + 1].broadcast_to([P, L]), xb, 0.0,
                                              ALU.mult, ALU.add))
                    link(v.scalar_tensor_tensor(out=yb, in0=sn, scalar=V["res"][:, n:n + 1], in1=yb,
                                                op0=ALU.mult, op1=ALU.add))
                    if slot == WEIGH_AT and not (first and u == 0):
                        weigh(2 * b + u - 1)
                x2b = tB[:].rearrange("p (t n) -> p t n", t=T)[:, :, ds(b * C, C)]
                v.tensor_tensor(x2b, x2b, yb.rearrange("p (c t) -> p t c", t=T), ALU.mult).then_inc(s("yT_ready"), 1)
                dve.wait_ge(s("yT_ready"), b + 1)

            mask_ranks(0, 0)
            filter_batch(0, first=True)
            with dve.Fori(0, B - 2) as m:
                ch.enter(m, 1 + NP1 + NP1)
                filter_batch(m + 1)
            ch.leave(B - 2)
            filter_batch(B - 1, final=True)
            weigh(NS - 1)
            ms = small[:, 8 * T:9 * T]
            dve.sem_inc(s("y_ready"), 2)
            with dve.Fori(0, NS // 2) as m:
                for u in range(2):
                    i = 2 * m + u
                    dve.wait_ge(s("yo_done"), i + 3)
                    v.tensor_tensor(tG[:, ds(i * SC, SC)], ps[u][:], tG[:, ds(i * SC, SC)],
                                    ALU.add).then_inc(s("y_ready"), 1)
                    dve.wait_ge(s("y_squared"), i + 1)
                    v.tensor_reduce(ms[:, ds(i * ST, ST)],
                                    stage[:, (2 + u) * SC:(3 + u) * SC].rearrange("p (t n) -> p t n", t=ST),
                                    AX.X, ALU.add).then_inc(s("ms_ready"), 1)
            dve.wait_ge(s("rms_ready"), 1)
            link(v.reciprocal(ms, ms))

            def scale_y(i, u):
                dve.wait_ge(s("zm_turned"), i + 1)
                v.tensor_tensor(stage[:, u * SC:(u + 1) * SC].rearrange("p (t n) -> p t n", t=ST),
                                tG[:, ds(i * SC, SC)].rearrange("p (t n) -> p t n", t=ST),
                                ms[:, ds(i * ST, ST)].unsqueeze(2).broadcast_to([P, ST, P]),
                                ALU.mult).then_inc(s("zs_staged"), 1)

            def gate_hidden(i, u):
                for f in range(3):
                    dve.wait_ge(s("gelu_ready"), i * 3 + f + 1)
                    dve.wait_ge(s("l2_done"), i * 3 + f + 1)
                    c = (3 * u + f) * SC
                    v.tensor_tensor(tK[0:FT, c:c + SC], tJ[0:FT, c:c + SC],
                                    ps[5 + f][0:FT, :], ALU.mult).then_inc(s("gated_ready"), 1)

            def finish(i):
                dve.wait_ge(s("mlp_done"), i + 1)
                dve.wait_ge(s("residual_ready"), i + 1)
                xi = tA[:, ds(i * SC, SC)]
                v.tensor_tensor(xi, xi, ps[0][:], ALU.add).then_inc(s("result_ready"), 1)

            dve.sem_inc(s("gated_ready"), 3)
            dve.sem_inc(s("result_ready"), 1)
            scale_y(0, 0)
            scale_y(1, 1)
            gate_hidden(0, 0)
            with dve.Fori(0, NS // 2 - 1) as m:
                for u in range(2):
                    scale_y(2 * m + u + 2, u)
                    gate_hidden(2 * m + u + 1, 1 - u)
                    finish(2 * m + u)
            gate_hidden(NS - 1, 1)
            finish(NS - 2)
            finish(NS - 1)

        @block.scalar
        def _(act):
            ch = Count(act, act_steps)
            link = ch.link
            a = nc.scalar

            def root(out, in_, eps, need, done):
                act.wait_ge(*need)
                a.activation(out, in_, ACT.Sqrt, bias=eps).then_inc(done, 1)

            eps5 = small[:, 11 * T:11 * T + 1]
            eps6 = small[:, 11 * T + 1:11 * T + 2]
            act.wait_ge(s("eps_set"), 1)
            root(rstd, var, eps5, (s("var_ready"), 1), s("std_ready"))
            root(rstd, var, eps5, (s("var_ready"), 2), s("std_ready"))
            act.wait_ge(s("var_ready"), 2)
            with act.Fori(0, NS) as i:
                act.wait_ge(s("xn_turned"), i + 1)
                a.activation(stage[:, 0:SC], tA[:, ds(i * SC, SC)], ACT.Copy).then_inc(s("xn_staged"), 1)
                act.wait_ge(s("xn_turned"), i + 2)
                a.activation(xnT0[:, ds(i * SC, SC)], ps[0][:], ACT.Copy).then_inc(s("xnT_ready"), 1)
            if stop == "A2":
                return
            act.wait_ge(s("biasq_ready"), 1)
            act.wait_ge(s("xe_turned"), NS + 1)
            act.wait_ge(s("xn_turned"), NS + 1)
            with act.Fori(0, NS) as i:
                act.wait_ge(s("qkv_turned"), i + 1)
                for n in range(3):
                    act.wait_ge(s("qkv_done"), i * 4 + n + 1)
                    a.activation(stage[:, n * SC:(n + 1) * SC], ps[n][:], ACT.Identity,
                                 bias=biasq[:, n:n + 1]).then_inc(s("qkv_staged"), 1)
                act.wait_ge(s("qkv_done"), i * 4 + 4)
                a.activation(stage[0:H + E0, 3 * SC:4 * SC], ps[3][0:H + E0, :], ACT.Identity,
                             bias=W["bbr"][0:H + E0, :]).then_inc(s("qkv_staged"), 1)
            qvt = qv.rearrange("p (t n) -> p t n", t=T)
            bt = brt[:].rearrange("p (t n) -> p t n", t=T)
            act.wait_ge(s("shifted0"), 1)
            g1 = gates[:, T * E0:2 * T * E0]
            a.activation(g1, g1, ACT.Exp).then_inc(s("exp0_ready"), 1)
            a.activation(bt[:, :, 0:H], bt[:, :, 0:H], ACT.Sigmoid).then_inc(s("beta_ready"), 1)
            a.activation(qvt[:, :, P:2 * P], qvt[:, :, P:2 * P], ACT.Silu).then_inc(s("silu_done"), 1)
            a.activation(tJ[:].rearrange("p (t n) -> p t n", t=T), qvt[:, :, 0:P],
                         ACT.Square).then_inc(s("q_squared"), 1)
            act.wait_ge(s("q2_summed"), 1)
            a.activation(tJ[:], k_tm[:], ACT.Square).then_inc(s("k_squared"), 1)
            act.wait_ge(s("norms_summed"), 1)
            a.activation(tK[:, 3072:4096], tK[:, 3072:4096], ACT.Sqrt).then_inc(s("norms_ready"), 1)
            if stop == "A4":
                return
            act.wait_ge(s("qkv_done"), 4 * NS)
            act.sem_inc(s("hid_ready"), FS)

            def hidden0(i, experts):
                for e in experts:
                    act.wait_ge(s("y0_ready"), i * E0 + e + 1)
                    for f in range(FS):
                        act.wait_ge(s("hid_done"), i * E0 * FS + e * FS + f + 1)
                        a.activation(tC[:, (e % 2) * 2048 + f * SC:(e % 2) * 2048 + (f + 1) * SC], ps[f][:],
                                     ACT.Relu, bias=F["b1"][:, e * FS + f:e * FS + f + 1]).then_inc(s("hid_ready"), 1)

            def outs_stage(i):
                act.wait_ge(s("out_done"), (i + 1) * ST + 2)
                act.wait_ge(s("outs_turned"), i + 1)
                sr = tDE[:, ds(i * 2 * SC, 2 * SC)].rearrange("p (th j) -> p th j", j=J)
                for n in range(2):
                    last = a.activation(stage[:, n * SC:(n + 1) * SC].rearrange("p (th k) -> p th k", k=HD),
                                        sr[:, :, n * HD:(n + 1) * HD], ACT.Copy)
                last.then_inc(s("outs_staged"), 1)

            def outs_take(i):
                act.wait_ge(s("outs_turned"), i + 2)
                a.activation(tF[:, ds(i * SC, SC)], ps[6][:], ACT.Copy)
                a.activation(tG[:, ds(i * SC, SC)], ps[7][:], ACT.Copy).then_inc(s("outs_in"), 1)

            hidden0(0, range(E0))
            with act.Fori(0, NS - 1) as i:
                hidden0(i + 1, range(OUTS_AT))
                outs_stage(i)
                hidden0(i + 1, range(OUTS_AT, OUTS_AT + 2))
                outs_take(i)
                hidden0(i + 1, range(OUTS_AT + 2, E0))
            outs_stage(NS - 1)
            outs_take(NS - 1)
            if stop == "B":
                return
            for i in range(NS):
                act.wait_ge(s("oT_ready"), NS + 2)
                if i >= 2:
                    act.wait_ge(s("o_meaned"), i - 1)
                a.activation(stage[:, (i % 2) * SC:(i % 2 + 1) * SC], tB[:, i * SC:(i + 1) * SC],
                             ACT.Square).then_inc(s("o_squared"), 1)
                act.wait_ge(s("mask_turned"), i + 1)
                a.activation(tF[0:E0, i * SC:(i + 1) * SC], ps[6 + i % 2][0:E0, :],
                             ACT.Copy).then_inc(s("maskT_ready"), 1)
                if i % 4 == 3:
                    g = i // 4
                    act.wait_ge(s("o_meaned"), i + 1)
                    a.activation(tK[:, 3072 + g * SC:3072 + (g + 1) * SC], ps[g][:], ACT.Sqrt,
                                 bias=eps6).then_inc(s("oroot_ready"), 1)
            if stop == "C":
                return
            root(rstd, var, eps5, (s("var_ready"), 3), s("std_ready"))
            root(rstd, var, eps6, (s("var_ready"), 4), s("std_ready"))
            a.activation(V["poles"], V["poles"], ACT.Exp).then_inc(s("decay_ready"), 1)
            act.wait_ge(s("wo0_done"), NS)
            with act.Fori(0, NS) as i:
                act.wait_ge(s("xn1_turned"), i + 1)
                a.activation(stage[:, 0:SC], tG[:, ds(i * SC, SC)], ACT.Copy).then_inc(s("xn1_staged"), 1)
                act.wait_ge(s("xn1_turned"), i + 2)
                a.activation(tC[:, ds(i * SC, SC)], ps[0][:], ACT.Copy).then_inc(s("xn1T_ready"), 1)
            act.wait_ge(s("zn_turned"), NS + 1)
            act.sem_inc(s("z_out"), 2)
            act.wait_ge(s("xn1_turned"), NS + 1)
            with act.Fori(0, NS // 2) as m:
                for u in range(2):
                    i = 2 * m + u
                    act.wait_ge(s("xv_ready"), i + 1)
                    act.wait_ge(s("z_done"), i + 1)
                    a.activation(tB[:, ds(i * SC, SC)], ps[4 * u][:], ACT.Identity, bias=V["shortb"][:, 0:1])
                    a.activation(stage[:, u * SC:(u + 1) * SC], ps[4 * u + 1][:], ACT.Identity,
                                 bias=V["shortb"][:, 1:2])
                    a.activation(stage[0:E1, (2 + u) * SC:(3 + u) * SC], ps[3][0:E1, :], ACT.Identity,
                                 bias=V["gateb"][0:E1, :]).then_inc(s("z_out"), 1)
            act.wait_ge(s("shifted1"), 1)
            a.activation(m_prob, m_prob, ACT.Exp).then_inc(s("exp1_ready"), 1)
            act.sem_inc(s("h1_ready"), FS)
            act.sem_inc(s("axs_ready"), 1)
            act.wait_ge(s("picks_ready"), 1)

            def spread_picks(i):
                act.wait_ge(s("pick_turned"), i + 1)
                for n in range(2):
                    last = a.activation(picks[:, n * SC:(n + 1) * SC].rearrange("p (te r) -> p te r", r=RK),
                                        gates[:, ds(n * T * E1 + i * ST * E1, ST * E1)].unsqueeze(2).broadcast_to(
                                            [P, ST * E1, RK]), ACT.Copy)
                last.then_inc(s("pick_staged"), 1)

            def take_ranks(i):
                act.wait_ge(s("ax_done"), i + 1)
                act.wait_ge(s("axm_ready"), i + 1)
                a.activation(axs, ps[6][:], ACT.Copy).then_inc(s("axs_ready"), 1)

            def hidden1(i, n):
                for f in range(FS):
                    act.wait_ge(s("h1_done"), i * 2 * FS + n * FS + f + 1)
                    act.wait_ge(s("hsum_ready"), i * FS + f + 1)
                    c = (n * FS + f) * SC
                    a.activation(tJ[:, c:c + SC], ps[f][:], ACT.Relu,
                                 bias=V["bi"][:, f:f + 1]).then_inc(s("h1_ready"), 1)

            act.sem_inc(s("pick_turned"), 1)
            act.sem_inc(s("axm_ready"), 1)
            spread_picks(0)
            take_ranks(0)
            with act.Fori(0, NS - 1) as i:
                spread_picks(i + 1)
                hidden1(i, 0)
                take_ranks(i + 1)
                hidden1(i, 1)
            for n in range(2):
                hidden1(NS - 1, n)
            act.wait_ge(s("yT_ready"), B)
            act.wait_ge(s("h1_done"), 2 * FS * NS)

            def stage_y(i, u):
                act.wait_ge(s("yo_done"), i + 1)
                a.activation(stage[:, u * SC:(u + 1) * SC], tB[:, ds(i * SC, SC)],
                             ACT.Copy).then_inc(s("yT_staged"), 1)

            def square_y(i, u):
                act.wait_ge(s("y_ready"), i + 3)
                act.wait_ge(s("ms_ready"), i + 1)
                a.activation(stage[:, (2 + u) * SC:(3 + u) * SC], tG[:, ds(i * SC, SC)],
                             ACT.Square).then_inc(s("y_squared"), 1)

            act.sem_inc(s("ms_ready"), 2)
            stage_y(0, 0)
            stage_y(1, 1)
            with act.Fori(0, NS // 2 - 1) as m:
                for u in range(2):
                    stage_y(2 * m + u + 2, u)
                    square_y(2 * m + u, u)
            square_y(NS - 2, 0)
            square_y(NS - 1, 1)
            act.wait_ge(s("ms_ready"), NS + 2)
            a.activation(small[:, 8 * T:9 * T], small[:, 8 * T:9 * T], ACT.Sqrt, bias=eps6,
                         scale=1.0 / P).then_inc(s("rms_ready"), 1)

            def take_zm(i, u):
                act.wait_ge(s("zm_turned"), i + 3)
                a.activation(stage[:, (2 + u) * SC:(3 + u) * SC], ps[1][:], ACT.Copy,
                             scale=V["post_w"]).then_inc(s("zmT_ready"), 1)

            def gelus(i, u):
                for f in range(3):
                    act.wait_ge(s("l1_done"), i * 3 + f + 1)
                    c = (3 * u + f) * SC
                    a.activation(tJ[0:FT, c:c + SC], ps[2 + f][0:FT, :],
                                 ACT.Gelu_apprx_tanh).then_inc(s("gelu_ready"), 1)

            take_zm(0, 0)
            with act.Fori(0, NS // 2 - 1) as m:
                for u in range(2):
                    gelus(2 * m + u, u)
                    take_zm(2 * m + u + 1, 1 - u)
            gelus(NS - 2, 0)
            take_zm(NS - 1, 1)
            gelus(NS - 1, 1)

        @block.tensor
        def _(pe):
            t_ = nc.tensor

            def turn_pairs(one, other):
                pe.sem_inc(s(one + "_turned"), 1)
                pe.sem_inc(s(other + "_turned"), 1)
                with pe.Fori(0, NS) as i:
                    for n, name in ((0, one), (1, other)):
                        pe.wait_ge(s(name + "_staged"), i + 1)
                        for j in range(ST):
                            c = n * SC + j * P
                            last = t_.transpose(ps[n][:, j * P:(j + 1) * P], stage[:, c:c + P], ident)
                        last.then_inc(s(name + "_turned"), 1)

            pe.wait_ge(fixed_in, 16)
            turn_pairs("xn", "xe")
            if stop == "A2":
                return

            pe.sem_inc(s("qkv_staged"), 4)
            pe.sem_inc(s("qkv_turned"), 1)
            pe.wait_ge(s("xnT_ready"), NS)
            pe.wait_ge(s("xeT_ready"), NS)
            pe.wait_ge(s("halo0_ready"), 1)
            pe.wait_ge(s("fold0_ready"), 1)

            def project0(i):
                for n in range(3):
                    pe.wait_ge(s("qkv_staged"), i * 4 + n + (2 if n == 2 else 1))
                    for tap in range(K0):
                        last = t_.matmul(ps[n][:], lhsT=fold0[:, tap * 3 * P + n * P:tap * 3 * P + (n + 1) * P],
                                         rhs=tC[:, ds(i * SC + tap * P, SC)], start=tap == 0, stop=tap == K0 - 1)
                    last.then_inc(s("qkv_done"), 1)
                t_.matmul(ps[3][0:H + E0, :], lhsT=W["wbrT"], rhs=tC[:, ds(i * SC + 3 * P, SC)],
                          start=True, stop=True).then_inc(s("qkv_done"), 1)

            def turn0(i):
                pe.wait_ge(s("qkv_staged"), i * 4 + 8)
                pe.wait_ge(s("qkv_in"), i + 1)
                for n in range(3):
                    for j in range(ST):
                        c = n * SC + j * P
                        t_.transpose(ps[4 + n][:, j * P:(j + 1) * P], stage[:, c:c + P], ident)
                for j in range(ST):
                    last = t_.transpose(ps[7][:, j * (H + E0):(j + 1) * (H + E0)],
                                        stage[0:H + E0, 3 * SC + j * P:3 * SC + (j + 1) * P],
                                        ident[0:H + E0, 0:H + E0])
                last.then_inc(s("qkv_turned"), 1)

            project0(0)
            with pe.Fori(0, NS - 1) as i:
                project0(i + 1)
                turn0(i)
            turn0(NS - 1)
            if stop == "A4":
                return

            pe.sem_inc(s("y0_ready"), 2)
            pe.wait_ge(w1_in, 16)
            pe.wait_ge(w2_in, 16)
            pe.wait_ge(s("qkv_in"), NS + 1)
            pe.wait_ge(s("qkv_staged"), 4 * NS + 4)

            def up(i, e):
                for f in range(FS):
                    pe.wait_ge(s("hid_ready"), i * E0 * FS + e * FS + f + 1)
                    t_.matmul(ps[f][:], lhsT=tH[:, (e * FS + f) * P:(e * FS + f + 1) * P],
                              rhs=tB[:, ds(i * SC, SC)], start=True, stop=True).then_inc(s("hid_done"), 1)

            def down(i, e):
                pe.wait_ge(s("y0_used"), i * E0 + e + 1)
                pe.wait_ge(s("hid_ready"), i * E0 * FS + e * FS + 2 * FS)
                for j in range(ST):
                    for f in range(FS):
                        c = (e % 2) * 2048 + f * SC + j * P
                        last = t_.matmul(ps[4 + e % 2][:, j * P:(j + 1) * P], lhsT=tC[:, c:c + P],
                                         rhs=tI[:, (e * FS + f) * P:(e * FS + f + 1) * P],
                                         start=f == 0, stop=f == FS - 1)
                last.then_inc(s("y0_ready"), 1)

            def experts0(i, after=None):
                for e in range(E0):
                    up(i, e)
                    if e:
                        down(i, e - 1)
                    if e == OUTS_AT and after is not None:
                        outs_turn(after)
                down(i, E0 - 1)

            def outs_turn(i):
                pe.wait_ge(s("outs_staged"), i + 1)
                for n in range(2):
                    for j in range(ST):
                        last = t_.transpose(ps[6 + n][:, j * P:(j + 1) * P],
                                            stage[:, n * SC + j * P:n * SC + (j + 1) * P], ident)
                last.then_inc(s("outs_turned"), 1)

            pe.sem_inc(s("outs_turned"), 1)
            experts0(0)
            with pe.Fori(0, NS - 1) as i:
                experts0(i + 1, i)
            outs_turn(NS - 1)
            if stop == "B":
                return

            pe.wait_ge(s("states_sorted"), 1)
            pe.wait_ge(s("hid_ready"), NS * E0 * FS + FS)
            for n in range(HD):
                last = t_.transpose(ps[2 + n // 4][:, (n % 4) * P:(n % 4 + 1) * P],
                                    tK[:, 2048 + n * P:2048 + (n + 1) * P], ident)
            last.then_inc(s("states_turned"), 1)
            pe.sem_inc(s("inter_done"), 2)
            pe.wait_ge(s("outs_in"), NS)
            qmt = tF[:].rearrange("p (t n) -> p n t", t=T)
            with pe.Fori(0, NS // 2) as i:
                for u in range(2):
                    pe.wait_ge(s("state_wide"), 2 * i + u + 1)
                    pe.wait_ge(s("oT_ready"), 2 * i + u + 1)
                    for a in range(ST):
                        for b in range(B):
                            n = a * B + b
                            last = t_.matmul(ps[u][:, n * T:(n + 1) * T],
                                             lhsT=tH[:, u * 2048 + n * P:u * 2048 + (n + 1) * P],
                                             rhs=qmt[:, ds((2 * i + u) * ST + a + b * C, 1), :],
                                             start=True, stop=True)
                    last.then_inc(s("inter_done"), 1)
            pe.wait_ge(s("oT_ready"), NS + 2)
            pe.wait_ge(s("inter_done"), NS + 2)
            pe.wait_ge(s("y0_used"), NS * E0 + 2)
            for i in range(NS):
                if i >= 2:
                    pe.wait_ge(s("maskT_ready"), i - 1)
                for j in range(ST):
                    t = i * ST + j
                    last = t_.transpose(ps[6 + i % 2][0:E0, j * P:(j + 1) * P], mask0[:, t * E0:(t + 1) * E0], ident)
                last.then_inc(s("mask_turned"), 1)
                pe.wait_ge(s("o_squared"), i + 1)
                k = 32 * (i % 4)
                t_.matmul(ps[i // 4][k:k + 32, :], lhsT=F["headmean"], rhs=stage[:, (i % 2) * SC:(i % 2 + 1) * SC],
                          start=True, stop=True).then_inc(s("o_meaned"), 1)

            def spread(i):
                k, g = 32 * (i % 4), i // 4
                pe.wait_ge(s("oscale_ready"), g + 1)
                if i >= 2:
                    pe.wait_ge(s("onT_ready"), i - 1)
                t_.matmul(ps[2 + i % 2][:], lhsT=F["headspread"][k:k + 32, :],
                          rhs=tK[k:k + 32, 3072 + g * SC:3072 + (g + 1) * SC],
                          start=True, stop=True).then_inc(s("spread_done"), 1)

            spread(0)
            for i in range(NS):
                if i + 1 < NS:
                    spread(i + 1)
                pe.wait_ge(s("onT_ready"), i + 1)
                pe.wait_ge(s("maskT_ready"), i + 1)
                if i >= 2:
                    pe.wait_ge(s("x1_ready"), i - 1)
                for j in range(ST):
                    c = (i % 2) * SC + j * P
                    o = ps[4 + i % 2][:, j * P:(j + 1) * P]
                    t_.matmul(o, lhsT=stage[:, c:c + P], rhs=F["woT"], start=True, stop=False)
                    last = t_.matmul(o, lhsT=tF[0:E0, i * SC + j * P:i * SC + (j + 1) * P],
                                     rhs=F["b2"][0:E0, :], start=False, stop=True)
                last.then_inc(s("wo0_done"), 1)
            if stop == "C":
                return
            turn_pairs("xn1", "zn")
            pe.wait_ge(s("xn1T_ready"), NS)
            pe.wait_ge(s("halo1_ready"), 1)
            pe.wait_ge(s("fold1_ready"), 1)

            def project1(i, u):
                pe.wait_ge(s("z_out"), i + 1)
                pe.wait_ge(s("xv_ready"), i + 1)
                for n in range(3):
                    for tap in range(K1):
                        last = t_.matmul(ps[4 * u + n][:],
                                         lhsT=fold1[:, tap * 3 * P + n * P:tap * 3 * P + (n + 1) * P],
                                         rhs=znT[:, ds(i * SC + tap * P, SC)], start=tap == 0, stop=tap == K1 - 1)
                pe.wait_ge(s("z_out"), i + 2)
                t_.matmul(ps[3][0:E1, :], lhsT=V["gateT"], rhs=tC[:, ds(i * SC, SC)],
                          start=True, stop=True).then_inc(s("z_done"), 1)

            def turn_logits(i, u):
                pe.wait_ge(s("z_out"), i + 3)
                pe.wait_ge(s("gate1_in"), i + 1)
                pe.sem_inc(s("waits_apart"), 1)
                for j in range(ST):
                    last = t_.transpose(ps[7][:, j * E1:(j + 1) * E1],
                                        stage[0:E1, (2 + u) * SC + j * P:(2 + u) * SC + (j + 1) * P],
                                        ident[0:E1, 0:E1])
                last.then_inc(s("gate1_turned"), 1)

            project1(0, 0)
            with pe.Fori(0, NS // 2 - 1) as m:
                for u in range(2):
                    project1(2 * m + u + 1, 1 - u)
                    turn_logits(2 * m + u, u)
            project1(NS - 1, 1)
            turn_logits(NS - 2, 0)
            turn_logits(NS - 1, 1)
            pe.sem_inc(s("y1_done"), 1)
            pe.wait_ge(s("gate1_in"), NS + 1)
            pe.wait_ge(s("xv_ready"), NS + 2)
            pe.wait_ge(s("picks_ready"), 1)

            def ranks(i):
                pe.wait_ge(s("axm_ready"), i + 1)
                pe.wait_ge(s("axs_ready"), i + 1)
                t_.matmul(ps[6][:], lhsT=V["loraAT"], rhs=tC[:, ds(i * SC, SC)],
                          start=True, stop=True).then_inc(s("ax_done"), 1)
                pe.wait_ge(s("pick_staged"), i + 1)
                for n in range(2):
                    for j in range(ST):
                        last = t_.transpose(ps[5 + 2 * n][:, j * P:(j + 1) * P],
                                            picks[:, n * SC + j * P:n * SC + (j + 1) * P], ident)
                last.then_inc(s("pick_turned"), 1)

            def first_pick(i, u):
                for f in range(FS):
                    pe.wait_ge(s("h1_ready"), i * 2 * FS + f + 1)
                    t_.matmul(ps[f][:], lhsT=V["wiT"][:, f * P:(f + 1) * P], rhs=tC[:, ds(i * SC, SC)],
                              start=True, stop=False)
                    if f == 0:
                        pe.wait_ge(s("axm_ready"), i + 2)
                    t_.matmul(ps[f][:], lhsT=V["loraBT"][:, f * P:(f + 1) * P], rhs=axm[u][0],
                              start=False, stop=True).then_inc(s("h1_done"), 1)

            def second_pick(i, u):
                for f in range(FS):
                    pe.wait_ge(s("h1_ready"), i * 2 * FS + FS + f + 1)
                    t_.matmul(ps[f][:], lhsT=V["loraBT"][:, f * P:(f + 1) * P], rhs=axm[u][1],
                              start=False, stop=True, skip_group_check=True).then_inc(s("h1_done"), 1)

            def down1(i):
                pe.wait_ge(s("ffn1_in"), i + 1)
                pe.wait_ge(s("hsum_ready"), i * FS + 2 * FS)
                for j in range(ST):
                    o = ps[4][:, j * P:(j + 1) * P]
                    t_.matmul(o, lhsT=pred[0:1, P:2 * P], rhs=pred[0:1, 0:P], start=True, stop=False)
                    for f in range(FS):
                        last = t_.matmul(o, lhsT=tK[:, f * SC + j * P:f * SC + (j + 1) * P],
                                         rhs=V["wo1T"][:, f * P:(f + 1) * P], start=False, stop=f == FS - 1)
                last.then_inc(s("y1_done"), 1)

            ranks(0)
            first_pick(0, 0)
            ranks(1)
            second_pick(0, 0)
            with pe.Fori(0, NS // 2 - 1) as m:
                for u in range(2):
                    i = 2 * m + u + 1
                    first_pick(i, 1 - u)
                    ranks(i + 1)
                    down1(i - 1)
                    second_pick(i, 1 - u)
            first_pick(NS - 1, 1)
            down1(NS - 2)
            second_pick(NS - 1, 1)
            down1(NS - 1)
            pe.sem_inc(s("yo_done"), 2)
            with pe.Fori(0, NS // 2) as m:
                for u in range(2):
                    i = 2 * m + u
                    pe.wait_ge(s("yT_staged"), i + 1)
                    pe.wait_ge(s("y_ready"), i + 1)
                    for j in range(ST):
                        last = t_.matmul(ps[u][:, j * P:(j + 1) * P],
                                         lhsT=stage[:, u * SC + j * P:u * SC + (j + 1) * P],
                                         rhs=V["outT"], start=True, stop=True)
                    last.then_inc(s("yo_done"), 1)

            def turn_zm(i, u):
                pe.wait_ge(s("zs_staged"), i + 1)
                pe.wait_ge(s("zmT_ready"), i + 1)
                pe.sem_inc(s("waits_apart"), 1)
                for j in range(ST):
                    last = t_.transpose(ps[1][:, j * P:(j + 1) * P],
                                        stage[:, u * SC + j * P:u * SC + (j + 1) * P], ident)
                last.then_inc(s("zm_turned"), 1)

            def mlp_hidden(i, u):
                pe.wait_ge(s("zmT_ready"), i + 2)
                zmT = stage[:, (2 + u) * SC:(3 + u) * SC]
                for f in range(3):
                    pe.wait_ge(s("gated_ready"), i * 3 + f + 1)
                    t_.matmul(ps[2 + f][0:FT, :], lhsT=V["l1T"][:, f * FT:(f + 1) * FT], rhs=zmT,
                              start=True, stop=True).then_inc(s("l1_done"), 1)
                    t_.matmul(ps[5 + f][0:FT, :], lhsT=V["l2T"][:, f * FT:(f + 1) * FT], rhs=zmT,
                              start=True, stop=True).then_inc(s("l2_done"), 1)

            def mlp_out(i, u):
                pe.wait_ge(s("gated_ready"), i * 3 + 6)
                pe.wait_ge(s("result_ready"), i + 1)
                for j in range(ST):
                    for f in range(3):
                        c = (3 * u + f) * SC + j * P
                        last = t_.matmul(ps[0][:, j * P:(j + 1) * P], lhsT=tK[0:FT, c:c + P],
                                         rhs=V["l3T"][0:FT, f * P:(f + 1) * P], start=f == 0, stop=f == 2)
                last.then_inc(s("mlp_done"), 1)

            pe.wait_ge(s("y_ready"), NS + 2)
            pe.sem_inc(s("zm_turned"), 2)
            pe.sem_inc(s("zmT_ready"), 1)
            turn_zm(0, 0)
            mlp_hidden(0, 0)
            turn_zm(1, 1)
            with pe.Fori(0, NS // 2 - 1) as m:
                for u in range(2):
                    mlp_hidden(2 * m + u + 1, 1 - u)
                    turn_zm(2 * m + u + 2, u)
                    mlp_out(2 * m + u, u)
            mlp_hidden(NS - 1, 1)
            mlp_out(NS - 2, 0)
            mlp_out(NS - 1, 1)

        @block.gpsimd
        def _(pool):
            ch = Count(pool, pool_steps)
            link = ch.link
            g = nc.gpsimd
            g.memset(small[:, 11 * T:11 * T + 1], 1e-5)
            g.memset(small[:, 11 * T + 1:11 * T + 2], 1e-6).then_inc(s("eps_set"), 1)
            if stop == "A2":
                return
            v4 = qv.rearrange("p (t n) -> p t n", t=T)[:, :, P:2 * P].rearrange("p t (h d) -> p t h d", d=HD)
            rk = tK[:, 3072 + T * H:4096].rearrange("p (t h) -> p t h", h=H).unsqueeze(3).broadcast_to([P, T, H, HD])
            pool.wait_ge(s("silu_done"), 1)
            pool.wait_ge(s("scales_ready"), 1)
            g.tensor_tensor(v4, v4, rk, ALU.mult).then_inc(s("v_scaled"), 1)
            if stop == "A4":
                return
            pool.wait_ge(s("prepared"), 1)
            pool.wait_ge(s("v_scaled"), 1)
            pool.sem_inc(s("out_done"), 2)
            prod = tK[:, 2048:4096]
            prod4 = prod.rearrange("p (h j k) -> p h j k", h=H, j=J)
            p8 = prod.rearrange("p (n k) -> p n k", k=HD)
            with pool.Fori(0, NS) as i:
                ch.enter(i, 3 * ST)
                for t in range(ST):
                    state = R[(t + 1) % 2].rearrange("p (h j k) -> p h j k", h=H, j=J)
                    q = tDE[:, ds(i * 2 * SC + t * 2 * P, P)].rearrange("p (h k) -> p h k", k=HD)
                    pool.wait_ge(s("state_ready"), i * ST + t + 1)
                    pool.wait_ge(s("out_done"), i * ST + t + 2)
                    link(g.tensor_tensor(prod4, state, q.unsqueeze(2).broadcast_to([P, H, J, HD]), ALU.mult))
                    link(g.tensor_tensor(p8[:, :, 0:4], p8[:, :, 0:4], p8[:, :, 4:8], ALU.add))
                    link(g.tensor_tensor(p8[:, :, 0:2], p8[:, :, 0:2], p8[:, :, 2:4], ALU.add))
                    pool.sem_inc(s("waits_apart"), 1)
                    o = tDE[:, ds(i * 2 * SC + t * 2 * P, 2 * P)]
                    g.tensor_tensor(o, p8[:, :, 0], p8[:, :, 1], ALU.add).then_inc(s("out_done"), 1)
            ch.leave(NS)
            if stop == "B":
                return
            pool.wait_ge(x_again, 16)
            pool.wait_ge(late_in, 16)
            x3 = tI[:].rearrange("p (t n) -> p t n", t=T)
            g.tensor_tensor(x3, x3, V["bo"].unsqueeze(1).broadcast_to([P, T, P]), ALU.add).then_inc(s("x_biased"), 1)
            if stop == "C":
                return
            pool.sem_inc(s("hsum_ready"), FS)
            with pool.Fori(0, NS) as i:
                pool.wait_ge(s("y1_done"), i + 1)
                for f in range(FS):
                    pool.wait_ge(s("h1_ready"), i * 2 * FS + 2 * FS + f + 1)
                    g.tensor_tensor(tK[:, f * SC:(f + 1) * SC], tJ[:, f * SC:(f + 1) * SC],
                                    tJ[:, (FS + f) * SC:(FS + f + 1) * SC], ALU.add).then_inc(s("hsum_ready"), 1)
            pool.wait_ge(s("ffn1_in"), NS + 1)
            link(g.tensor_tensor(tA[:], tA[:], tI[:], ALU.add))
            for i in range(NS):
                pool.wait_ge(s("y_ready"), i + 3)
                g.tensor_tensor(tA[:, i * SC:(i + 1) * SC], tA[:, i * SC:(i + 1) * SC],
                                tG[:, i * SC:(i + 1) * SC], ALU.add).then_inc(s("residual_ready"), 1)


def kernel(**inputs):
    import numpy as np
    import concourse.bacc as bacc
    from concourse.bass_utils import run_bass_kernel_spmd as run

    a = {k: np.asarray(v) for k, v in inputs.items()}
    f32 = np.float32

    def rows(x, n=P):
        return np.broadcast_to(x.reshape(1, -1), (n, x.size))

    def padded(x, n=P):
        out = np.zeros((n,) + x.shape[1:], f32)
        out[:x.shape[0]] = x
        return out

    def col(x):
        return padded(x.reshape(-1, 1))

    p = np.arange(P)
    A, Fn, A1, F1 = "L0_attn_", "L0_ffn_", "L1_attn_", "L1_ffn_"
    fixed = dict(
        ident=np.eye(P, dtype=f32), headmask=(p[:, None] // HD == np.arange(H)[None]).astype(f32),
        headmean=(p[:, None] // HD == np.arange(32)[None] % H).astype(f32) / HD,
        headspread=(p[:, None] % 32 == p[None] // HD).astype(f32),
        first=-(p % C == 0).astype(f32).reshape(P, 1), descend=rows(np.arange(E0, 0, -1).astype(f32)),
        woT=a[A + "Wo"].T, norm_w=np.tile(a[A + "norm_w"], H).reshape(P, 1),
        ln_g=col(a[Fn + "ln_g"]), ln_b=col(a[Fn + "ln_b"]),
        b1=a[Fn + "b1"].reshape(E0 * FS, P).T, b2=padded(a[Fn + "b2"]))
    qkv = ("q", "k", "v")
    early = dict(
        wqkvT=np.concatenate([a[A + "W" + n].T for n in qkv], 1),
        conv=rows(np.concatenate([a[A + f"w{n}_conv"][:, i] for i in range(K0) for n in qkv])),
        brow=rows(np.concatenate([a[A + "b" + n] for n in qkv])),
        wbrT=np.concatenate([a[A + "Wbeta"].T, a[Fn + "Wr"]], 1),
        taps=np.concatenate([a[A + f"w{n}_conv"] for n in qkv], 1),
        bqkv=np.stack([a[A + "b" + n] for n in qkv], 1),
        bconv=np.stack([a[A + f"b{n}_conv"] for n in qkv], 1),
        bbr=col(np.concatenate([a[A + "bbeta"], a[Fn + "br"]])))
    sw = a[A1 + "short_w"].reshape(3 * P, K1)
    last = dict(
        short=rows(np.concatenate([sw[:, i] for i in range(K1)])),
        wiT=a[F1 + "wi"].T, wo1T=a[F1 + "wo"].T.reshape(FS, P, P).transpose(1, 0, 2).reshape(P, FS * P),
        loraBT=a[F1 + "lora_B"].transpose(0, 2, 1).reshape(E1 * RK, F0))
    late = dict(
        bo=rows(a[A + "bo"]), inT=a[A1 + "in_proj_w"].T,
        shortb=a[A1 + "short_b"].reshape(3, P).T, poles=a[A1 + "log_poles"].reshape(P, NP1),
        res=a[A1 + "residues"], skip=col(a[A1 + "D_skip"]), outT=a[A1 + "out_proj_w"].T,
        pre_w=col(a[A1 + "pre_norm_w"]), post_w=col(a[A1 + "post_norm_w"]),
        l1T=a[A1 + "l1_w"].T, l2T=a[A1 + "l2_w"].T,
        l3T=padded(a[A1 + "l3_w"].T.reshape(3, FT, P).transpose(1, 0, 2).reshape(FT, 3 * P)),
        bi=a[F1 + "bi"].reshape(FS, P).T,
        loraAT=a[F1 + "lora_A"].reshape(E1 * RK, P).T,
        gateT=a[F1 + "gate_w"].T, gateb=col(a[F1 + "gate_b"]), bo1=rows(a[F1 + "bo"]))

    def packed(pack, parts):
        return np.ascontiguousarray(np.concatenate([parts[name].reshape(P, n) for name, n in pack], 1))

    arrays = {
        "x": np.ascontiguousarray(a[A + "x"].reshape(P, T * P)),
        "fixed": packed(FIXED, fixed), "early": packed(EARLY, early), "late": packed(LATE, late),
        "last": packed(LAST, last),
        "w1": np.ascontiguousarray(a[Fn + "W1"].transpose(1, 0, 2).reshape(P, E0 * F0)),
        "w2": np.ascontiguousarray(a[Fn + "W2"].reshape(E0, FS, P, P).transpose(2, 0, 1, 3).reshape(P, E0 * F0)),
    }
    nc = bacc.Bacc("TRN2", target_bir_lowering=False, num_devices=1)
    aps = [nc.dram_tensor(n, v.shape, mybir.dt.float32, kind="ExternalInput").ap() for n, v in arrays.items()]
    out = nc.dram_tensor("out", (P, T * P), mybir.dt.float32, kind="ExternalOutput").ap()
    maps = nc.dram_tensor("maps", (B, C, H, J * HD), mybir.dt.float32, kind="Internal").ap()
    states = nc.dram_tensor("states", (B, C, H, 2, HD * HD // 2), mybir.dt.float32, kind="Internal").ap()
    two_layers(nc, *aps, out, maps, states, stop=STOP)
    r = run(nc, [arrays], core_ids=[0])
    return r.results[0]["out"].reshape(B, L, D)


STOP = None
```

```python
import concourse.bass as bass
from concourse import mybir
from contextlib import ExitStack

B, L, D = 4, 1024, 128
P = 128
C = 32
T = L // C
N = B * L
H, HD = 16, 8
J = 2 * HD
K0, K1 = 4, 3
E0, F0 = 8, 512
FS = F0 // P
E1, RK = 8, 16
NP1 = 16
FF, FT = 336, 112
ST = 4
SC = ST * P
NS = T // ST
TURN_ORDER = [NS - 1] + list(range(NS - 1))
CHAIN_PER_EXPERT = 7
EARLY_LATE = 9
POOL_POLES = (1, 3, 5, 9, 11, 13)
DVE_POLES = [n for n in range(NP1) if n not in POOL_POLES]
MASK_AT = 5
GROUPS = [(0, 2), (2, 6)]
AHEAD = GROUPS[1][0]
BESIDE = GROUPS[1][1]
EB = E0 - 1
LATE_FROM = E0 + BESIDE * EB
LATE_PAIRS = [(i, 0) for i in range(1, 1 + BESIDE)] + [(NS - 1, e) for e in range(E0)]
LATE_UNITS = len(LATE_PAIRS)
OUTS_LATE = 1
OUTS_AT = 3
UNITS = NS * E0

FIXED = [("ident", P), ("headmask", H), ("headmean", 32), ("headspread", P), ("descend", E0), ("woT", P),
         ("norm_w", 1), ("ln_g", 1), ("ln_b", 1), ("b1", E0 * FS), ("b2", P)]
EARLY = [("wqkvT", 3 * P), ("conv", K0 * 3 * P), ("wbrT", H + E0), ("taps", 3 * K0),
         ("bqkv", 3), ("bconv", 3), ("bbr", 1)]
LATE = [("bo", P), ("inT", 3 * P), ("shortb", 3), ("poles", NP1), ("res", NP1), ("skip", 1),
        ("outT", P), ("pre_w", 1), ("post_w", 1), ("l1T", FF), ("l2T", FF), ("l3T", 3 * P),
        ("bi", FS), ("loraAT", P), ("gateT", E1), ("gateb", 1), ("bo1", P)]
LAST = [("short", K1 * 3 * P), ("wiT", F0), ("wo1T", FS * P), ("loraBT", F0)]


def width(pack):
    return sum(n for _, n in pack)


def columns(tile, pack):
    at, out = 0, {}
    for name, n in pack:
        out[name] = tile[:, at:at + n]
        at += n
    return out


class Count:

    def __init__(self, eng, sem):
        self.eng, self.sem, self.base, self.n = eng, sem, 0, 0

    def link(self, ins):
        ins.then_inc(self.sem, 1)
        self.n += 1
        self.eng.wait_ge(self.sem, self.base + self.n)

    def enter(self, i, per):
        self.outer, self.per = self.base + self.n, per
        self.base, self.n = self.outer + i * per, 0

    def leave(self, times):
        assert self.n == self.per, (self.n, self.per)
        self.base, self.n = self.outer + times * self.per, 0


def two_layers(nc, x_d, fixed_d, early_d, late_d, last_d, w1_d, w2_d, out_d, maps_d, states_d):
    fp32 = mybir.dt.float32
    ALU = mybir.AluOpType
    ACT = mybir.ActivationFunctionType
    AX = mybir.AxisListType
    ds = bass.ds
    ctx = ExitStack()
    with ctx:
        def sb(name, cols):
            return ctx.enter_context(nc.sbuf_tensor(name, [P, cols], fp32))

        def sem(name):
            return ctx.enter_context(nc.semaphore(name))

        tA = sb("tA", N)
        tB = sb("tB", N)
        tC = sb("tC", N + (K0 - 1) * P)
        tDE = sb("tDE", 2 * N)
        tF = sb("tF", N)
        tG = sb("tG", N)
        tH = sb("tH", N)
        tI = sb("tI", N)
        tJ = sb("tJ", N)
        tK = sb("tK", N)
        wt = sb("wt", max(width(EARLY), width(LATE)))
        fx = sb("fx", width(FIXED))
        stage = sb("stage", 4 * SC)
        small = sb("small", 12 * T)
        brt = sb("brt", T * (H + E0))
        gates = sb("gates", 4 * T * E0)
        stats = sb("stats", 6 * T)
        pred = sb("pred", H * J)
        biasq = sb("biasq", 3)
        missed = sb("missed", 9)
        ps = [ctx.enter_context(nc.psum_tensor(f"ps{n}", [P, SC], fp32)) for n in range(8)]

        F = columns(fx, FIXED)
        W = columns(wt, EARLY)
        V = columns(wt, LATE)
        V.update(columns(tH[:, N - width(LAST):N], LAST))
        ident = F["ident"]

        x_in = [sem(f"x_in{n}") for n in range(4)]
        fixed_in, early_in, late_in = sem("fixed_in"), sem("early_in"), sem("late_in")
        last_in = sem("last_in")
        maps_out, maps_in, states_out, states_in = sem("maps_out"), sem("maps_in"), sem("states_out"), sem("states_in")
        w1b_in = sem("w1b_in")
        w1_in, w2_in, x_again, out_sent = sem("w1_in"), sem("w2_in"), sem("x_again"), sem("out_sent")
        dve_steps, act_steps, pool_steps = sem("dve_steps"), sem("act_steps"), sem("pool_steps")
        S = {}

        def s(name):
            if name not in S:
                S[name] = sem(name)
            return S[name]

        block = ctx.enter_context(nc.Block())

        xnT0 = tC[:, (K0 - 1) * P:]
        qv = tDE[:]
        k_tm, kb_tm = tF, tG
        fold0 = tI[:, 0:K0 * 3 * P]
        mean, var, rstd, tmp1, tmp2 = (small[:, n * T:(n + 1) * T] for n in range(5))
        stages = [stage[:], tH[:, N - 4 * SC:N]]
        rstd2 = small[:, 9 * T:10 * T]
        mask0 = gates[:, 0:T * E0]
        R = [tJ[:, 0:2048], tJ[:, 2048:4096]]

        znT, fold1 = tDE[:, 0:N + (K1 - 1) * P], tH[:, 0:K1 * 3 * P]
        scan = [tDE[:, 4352 + n * L:4352 + (n + 1) * L] for n in range(2)]
        pool_scan = [tDE[:, n * L:(n + 1) * L] for n in range(len(POOL_POLES) // 2)]
        y_pool, y_dve = tDE[:, 3 * L:4 * L], tH[:, 0:L]
        picks = tDE[:, 6400:6400 + 2 * SC]
        axs = tK[:, 4 * SC:5 * SC]
        axm = [[stage[:, (2 * u + n) * SC:(2 * u + n + 1) * SC] for n in range(2)] for u in range(2)]
        m_prob = gates[:, 2 * T * E0:3 * T * E0]


        def squares(g):
            n = GROUPS[g][1] * SC
            c = GROUPS[g][0] * SC
            return tG[:, c:c + n], (tJ[:, 0:n], tA[:, SC:SC + n])[g]

        chainN, chainS, chainM = tJ[:, 0:1024], tJ[:, 1024:2048], tJ[:, 2048:4096]
        wide = [tDE[:, n * 2048:(n + 1) * 2048] for n in range(2)]
        o_sq = tJ
        maskT = tI[0:E0, :]
        x_res = tDE[:, N:2 * N]
        Sst = tK[:, 1024:2048]

        @block.sync
        def _(sp):
            for n in range(4):
                part = slice(n * 2 * SC, (n + 1) * 2 * SC)
                sp.dma_start(tA[:, part], x_d[:, part]).then_inc(x_in[n], 16)
            sp.dma_start(fx[:], fixed_d).then_inc(fixed_in, 16)
            sp.dma_start(wt[:, 0:width(EARLY)], early_d).then_inc(early_in, 16)
            sp.dma_start(tH[:, 0:N - 4 * SC], w1_d[:, 0:N - 4 * SC]).then_inc(w1_in, 16)
            sp.wait_ge(s("qkv_done"), 4 * NS)
            sp.dma_start(tI[:], w2_d).then_inc(w2_in, 16)
            sp.wait_ge(s("qkv_turned"), NS + 2)
            sp.dma_start(tH[:, N - 4 * SC:N], w1_d[:, N - 4 * SC:N]).then_inc(w1b_in, 16)
            sp.wait_ge(s("corrected"), 1)
            sp.dma_start(wt[:, 0:width(LATE)], late_d).then_inc(late_in, 16)
            sp.wait_ge(s("state_ready"), T)
            sp.dma_start(maps_d.rearrange("b c h n -> (b c) h n"),
                         R[0].rearrange("p (h n) -> p h n", h=H)).then_inc(maps_out, 16)
            sp.wait_ge(maps_out, 16)
            sp.wait_ge(s("out_done"), T + 2)
            for half in range(2):
                for b in range(B):
                    p0 = half * 64 + b * H
                    sp.dma_start(chainM[p0:p0 + H, :].rearrange("h (c n) -> h c n", c=C),
                                 maps_d[b][:, :, 0:64].rearrange("c h n -> h c n")).then_inc(maps_in, 16)
                    n0 = 64 + half * 32
                    sp.dma_start(chainN[p0:p0 + H, :].rearrange("h (c n) -> h c n", c=C),
                                 maps_d[b][:, :, n0:n0 + 32].rearrange("c h n -> h c n")).then_inc(maps_in, 16)
            sp.wait_ge(s("outs_staged"), NS)
            sp.dma_start(x_res, x_d).then_inc(x_again, 16)
            sp.wait_ge(s("chained"), C - 1)
            for half in range(2):
                for b in range(B):
                    p0 = half * 64 + b * H
                    sp.dma_start(states_d[b][:, :, half, :].rearrange("c h n -> h c n"),
                                 chainS[p0:p0 + H, 0:C * 32].rearrange("h (c n) -> h c n", c=C)
                                 ).then_inc(states_out, 16)
            sp.wait_ge(states_out, 16 * 2 * B)
            sp.dma_start(tK[:, 0:1024].rearrange("p (h n) -> p h n", h=H),
                         states_d.rearrange("b c h a n -> (b c) h (a n)")).then_inc(states_in, 16)
            sp.wait_ge(s("y0_ready"), UNITS + 2)
            sp.dma_start(tH[:, N - width(LAST):N], last_d).then_inc(last_in, 16)
            with sp.Fori(0, NS) as i:
                sp.wait_ge(s("result_ready"), i + 2)
                sp.dma_start(out_d[:, ds(i * SC, SC)], tA[:, ds(i * SC, SC)]).then_inc(out_sent, 16)
            sp.wait_ge(out_sent, 16 * NS)

        @block.vector
        def _(dve):
            ch = Count(dve, dve_steps)
            link = ch.link
            v = nc.vector

            def token_stats(i, x):
                for t in range(i * ST, (i + 1) * ST):
                    last = v.bn_stats(stats[:, 6 * t:6 * t + 6], x[:, t * P:(t + 1) * P])
                return last

            def mean_var():
                st = stats[:].rearrange("p (t s) -> p t s", s=6)
                link(v.tensor_tensor(mean, st[:, :, 1], st[:, :, 4], ALU.add))
                link(v.tensor_scalar(mean, mean, 0.5, None, ALU.mult))
                link(v.tensor_tensor(tmp1, st[:, :, 1], mean, ALU.subtract))
                link(v.tensor_tensor(tmp1, tmp1, tmp1, ALU.mult))
                link(v.tensor_tensor(tmp2, st[:, :, 2], st[:, :, 5], ALU.add))
                link(v.tensor_scalar(tmp2, tmp2, 1.0 / P, None, ALU.mult))
                v.tensor_tensor(var, tmp1, tmp2, ALU.add).then_inc(s("var_ready"), 1)

            def normalise(i, x, y):
                for t in range(i * ST, (i + 1) * ST):
                    last = v.tensor_scalar(y[:, t * P:(t + 1) * P], x[:, t * P:(t + 1) * P], mean[:, t:t + 1],
                                           rstd[:, t:t + 1], ALU.subtract, ALU.mult)
                return last

            def second_var():
                link(v.reciprocal(rstd, rstd))
                link(v.tensor_tensor(tmp1, rstd, rstd, ALU.mult))
                v.tensor_tensor(var, var, tmp1, ALU.mult).then_inc(s("var_ready"), 1)

            for i in range(NS):
                if i % 2 == 0:
                    dve.wait_ge(x_in[i // 2], 16)
                last = token_stats(i, tA)
            link(last)
            mean_var()
            dve.wait_ge(early_in, 16)
            v.tensor_tensor(fold0.rearrange("p (i n) -> p i n", i=K0),
                            W["wqkvT"].unsqueeze(1).broadcast_to([P, K0, 3 * P]),
                            W["conv"].rearrange("p (i n) -> p i n", i=K0), ALU.mult).then_inc(s("fold0_ready"), 1)
            dve.wait_ge(s("std_ready"), 1)
            second_var()
            halo = tC[:, 0:(K0 - 1) * P].rearrange("p (t b c) -> p t b c", b=B, c=C)
            link(v.memset(tC[:, 0:(K0 - 1) * P], 0.0))
            for n, i in enumerate(TURN_ORDER):
                normalise(i, tA, tA).then_inc(s("xn_ready"), 1)
                if n == 2:
                    dve.wait_ge(s("xnT_ready"), 1)
                    src = xnT0[:, (T - K0 + 1) * P:T * P].rearrange("p (t b c) -> p t b c", b=B, c=C)
                    for t in range(K0 - 1):
                        last = v.tensor_copy(halo[:, t, :, 1:C], src[:, t, :, 0:C - 1])
                    last.then_inc(s("halo0_ready"), 1)
            taps = W["taps"].rearrange("p (a i) -> p a i", i=K0)
            link(v.tensor_reduce(biasq[:], taps, AX.X, ALU.add))
            link(v.tensor_tensor(biasq[:], biasq[:], W["bqkv"], ALU.mult))
            v.tensor_tensor(biasq[:], biasq[:], W["bconv"], ALU.add).then_inc(s("biasq_ready"), 1)
            link(v.tensor_copy(missed[:, 6:9], taps[:, :, 0]))
            link(v.tensor_tensor(missed[:, 3:6], missed[:, 6:9], taps[:, :, 1], ALU.add))
            link(v.tensor_tensor(missed[:, 0:3], missed[:, 3:6], taps[:, :, 2], ALU.add))
            m_ta = missed[:].rearrange("p (t a) -> p t a", a=3)
            link(v.tensor_tensor(m_ta, m_ta, W["bqkv"].unsqueeze(1).broadcast_to([P, 3, 3]), ALU.mult))
            dve.wait_ge(s("std_ready"), 2)
            link(v.reciprocal(rstd2, rstd2))
            dve.wait_ge(s("xn_ready"), NS)
            dve.wait_ge(s("xn_turned"), NS)
            x3 = tA[:].rearrange("p (t n) -> p t n", t=T)
            v.tensor_tensor(x3, x3, rstd2.unsqueeze(2).broadcast_to([P, T, P]), ALU.mult).then_inc(s("xe_ready"), 1)
            dve.wait_ge(fixed_in, 16)
            v.tensor_scalar(F["woT"], F["woT"], F["norm_w"], None, ALU.mult)
            dve.wait_ge(s("qkv_staged"), 4 + 3)
            for n in range(3):
                first = stages[0][:, n * SC:n * SC + 3 * P].rearrange("p (t b c) -> p t b c", b=B, c=C)[:, :, :, 0]
                last = v.tensor_tensor(first, first, m_ta[:, :, n].unsqueeze(2).broadcast_to([P, 3, B]), ALU.subtract)
            last.then_inc(s("corrected"), 1)

            qvt = qv.rearrange("p (t n) -> p t n", t=T)
            kt = k_tm[:].rearrange("p (t n) -> p t n", t=T)
            bt = brt[:].rearrange("p (t n) -> p t n", t=T)
            m3 = [gates[:, n * T * E0:(n + 1) * T * E0].rearrange("p (t e) -> p t e", e=E0) for n in range(4)]
            desc = F["descend"].unsqueeze(1).broadcast_to([P, T, E0])
            top = small[:, 5 * T:6 * T]

            def over_e(col):
                return col.unsqueeze(2).broadcast_to([P, col.shape[1], E0])

            def prepare(g):
                t0, n = GROUPS[g][0] * ST, GROUPS[g][1] * ST
                tt = slice(t0, t0 + n)
                logit, tp, m0, m1 = bt[:, tt, H:H + E0], top[:, tt], m3[0][:, tt], m3[1][:, tt]
                dve.wait_ge(s("qkv_in"), 1 + GROUPS[g][0] + GROUPS[g][1])
                link(v.tensor_reduce(tp, logit, AX.X, ALU.max))
                v.tensor_tensor(m1, logit, over_e(tp), ALU.subtract).then_inc(s("shifted0"), 1)
                link(v.tensor_tensor(m0, logit, over_e(tp), ALU.is_equal))
                link(v.tensor_tensor(m0, m0, desc[:, 0:n], ALU.mult))
                link(v.tensor_reduce(tp, m0, AX.X, ALU.max))
                link(v.tensor_tensor(m0, m0, over_e(tp), ALU.is_equal))
                norms, (q2, k2) = tK[:, 0:2 * n * H], squares(g)
                dve.wait_ge(s("squared"), 2 * g + 1)
                v.tensor_reduce(norms[:, 0:n * H], q2.rearrange("p (n d) -> p n d", d=HD), AX.X, ALU.add)
                dve.wait_ge(s("squared"), 2 * g + 2)
                v.tensor_reduce(norms[:, n * H:2 * n * H], k2.rearrange("p (n d) -> p n d", d=HD), AX.X,
                                ALU.add).then_inc(s("norms_summed"), 1)
                if g == 1:
                    add_expert(0, 4, 4, 0)
                    add_expert(0, 5, 5, 1)
                dve.wait_ge(s("exp0_ready"), g + 1)
                link(v.tensor_reduce(tp, m1, AX.X, ALU.add))
                link(v.reciprocal(tp, tp))
                link(v.tensor_tensor(m0, m0, over_e(tp), ALU.mult))
                dve.wait_ge(s("norms_ready"), g + 1)
                link(v.tensor_scalar(norms, norms, 1e-6, None, ALU.add))
                v.reciprocal(norms, norms).then_inc(s("scales_ready"), 1)
                dve.wait_ge(s("scales_ready"), g + 1)

                def by_head(cols):
                    return cols.rearrange("p (t h) -> p t h", h=H).unsqueeze(3).broadcast_to([P, n, H, HD])

                q4 = qvt[:, tt, 0:P].rearrange("p t (h d) -> p t h d", d=HD)
                k4 = kt[:, tt].rearrange("p t (h d) -> p t h d", d=HD)
                kb4 = kb_tm[:].rearrange("p (t h d) -> p t h d", h=H, d=HD)[:, tt]
                link(v.tensor_tensor(k4, k4, by_head(norms[:, n * H:2 * n * H]), ALU.mult))
                dve.wait_ge(s("beta_ready"), g + 1)
                v.tensor_tensor(kb4, k4, bt[:, tt, 0:H].unsqueeze(3).broadcast_to([P, n, H, HD]), ALU.mult)
                last = v.tensor_tensor(q4, q4, by_head(norms[:, 0:n * H]), ALU.mult)
                if g == 0:
                    link(last)
                    link(v.memset(R[0], 0.0))
                    last = v.memset(R[0].rearrange("p (h n) -> p h n", h=H)[:, :, 0:64:9], 1.0)
                last.then_inc(s("prepared"), 1)
                if g == 1:
                    add_expert(0, 6, 6, 0)
                    add_expert(0, 7, 7, 1)
                dve.wait_ge(s("prepared"), g + 1)
                dve.wait_ge(s("v_scaled"), g + 1)

            prod = tK[:, 0:2048]
            prod4 = prod.rearrange("p (h j k) -> p h j k", h=H, j=J)
            pr3 = pred[:].rearrange("p (h j) -> p h j", h=H)
            dve.sem_inc(s("y0_used"), 2)

            def heads(tile, col):
                return tile[:, ds(col, P)].rearrange("p (h k) -> p h k", k=HD).unsqueeze(2).broadcast_to([P, H, J, HD])

            def add_expert(i, e, unit, bank, first=False):
                dve.wait_ge(s("y0_ready"), unit + 3)
                dve.wait_ge(s("y0_used"), unit + 2)
                for j in range(ST):
                    yj = tA[:, ds(i * SC + j * P, P)]
                    y, m = ps[4 + bank][:, j * P:(j + 1) * P], mask0[:, ds(i * ST * E0 + j * E0 + e, 1)]
                    if first:
                        last = v.tensor_scalar(yj, y, m, None, ALU.mult)
                    else:
                        last = v.scalar_tensor_tensor(out=yj, in0=y, scalar=m, in1=yj, op0=ALU.mult, op1=ALU.add)
                last.then_inc(s("y0_used"), 1)

            def delta_tokens(i, sums):
                for half in range(2 * ST):
                    t = half // 2
                    cur, nxt = R[t % 2], R[(t + 1) % 2]
                    cur4 = cur.rearrange("p (h j k) -> p h j k", h=H, j=J)
                    nxt4 = nxt.rearrange("p (h j k) -> p h j k", h=H, j=J)
                    if half % 2 == 0:
                        link(v.tensor_tensor(prod4, cur4, heads(k_tm, i * SC + t * P), ALU.mult))
                        link(v.tensor_reduce(pr3, prod4, AX.X, ALU.add))
                        link(v.tensor_tensor(pr3[:, :, HD:J], pr3[:, :, HD:J],
                                             qv[:, ds(i * 2 * SC + t * 2 * P + P, P)].rearrange(
                                                 "p (h k) -> p h k", k=HD), ALU.subtract))
                    else:
                        link(v.tensor_tensor(prod4, heads(kb_tm, i * SC + t * P),
                                             pr3.unsqueeze(3).broadcast_to([P, H, J, HD]), ALU.mult))
                        dve.wait_ge(s("out_done"), i * ST + t + 1)
                        v.tensor_tensor(nxt4, cur4, prod4, ALU.subtract).then_inc(s("state_ready"), 1)
                        dve.wait_ge(s("state_ready"), i * ST + t + 1)
                    if sums[half] is not None:
                        add_expert(*sums[half])

            prepare(0)
            delta_tokens(0, [None] * (2 * ST))
            delta_tokens(1, [None] * ST + [(0, e, e, e % 2, e == 0) for e in range(ST)])
            prepare(1)
            with dve.Fori(0, BESIDE // 2) as m:
                ch.enter(m, 2 * 4 * ST)
                for w in range(2):
                    i = 2 * m + w
                    delta_tokens(i + AHEAD, [None] + [(i + 1, e, i * EB + E0 + e - 1, (w + e - 1) % 2, e == 1)
                                                      for e in range(1, E0)])
            ch.leave(BESIDE // 2)

            chain_prod = pred[:].rearrange("p (v k j) -> p v k j", v=HD // 2, k=HD)
            hm = F["headmask"]

            def late_expert(n):
                i, e = LATE_PAIRS[n]
                add_expert(i, e, LATE_FROM + n, (LATE_FROM + n) % 2, i == NS - 1 and e == 0)

            for n in range(3):
                late_expert(n)
            dve.wait_ge(maps_in, 16 * 4 * B)
            v.memset(chainS[:, 0:32], 0.0)
            v.tensor_copy(chainS[:, 32:64], chainN[:, 0:32]).then_inc(s("chained"), 1)
            dve.wait_ge(s("chained"), 1)
            for c in range(1, C - 1):
                prev = chainS[:, c * 32:(c + 1) * 32].rearrange("p (v j) -> p v j", j=HD)
                nxt = chainS[:, (c + 1) * 32:(c + 2) * 32]
                mc = chainM[:, c * 64:(c + 1) * 64].rearrange("p (j k) -> p k j", k=HD)
                link(v.tensor_tensor(chain_prod, prev.unsqueeze(2).broadcast_to([P, HD // 2, HD, HD]),
                                     mc.unsqueeze(1).broadcast_to([P, HD // 2, HD, HD]), ALU.mult))
                link(v.tensor_reduce(nxt.rearrange("p (v k) -> p v k", k=HD), chain_prod, AX.X, ALU.add))
                v.tensor_tensor(nxt, nxt, chainN[:, c * 32:(c + 1) * 32], ALU.add).then_inc(s("chained"), 1)
                dve.wait_ge(s("chained"), c + 1)
                if c % CHAIN_PER_EXPERT == 0:
                    late_expert(2 + c // CHAIN_PER_EXPERT)
            for n in range(3 + (C - 2) // CHAIN_PER_EXPERT, EARLY_LATE):
                late_expert(n)
            dve.wait_ge(states_in, 16)
            dve.wait_ge(s("out_done"), T + 2)
            v.tensor_copy(tK[:, 2048:3072].rearrange("p (v h k) -> p h v k", v=HD, h=H),
                          tK[:, 0:1024].rearrange("p (h v k) -> p h v k", h=H, v=HD)).then_inc(s("states_sorted"), 1)
            late_expert(EARLY_LATE)
            dve.wait_ge(s("states_turned"), 1)
            for n in range(2):
                last = v.tensor_copy(
                    Sst.rearrange("p (c b v) -> p v b c", c=C, b=B)[:, n * 4:(n + 1) * 4, :, :],
                    ps[6 + n][:].rearrange("p (v b c) -> p v b c", v=4, b=B))
            link(last)

            def by_chunk(tile):
                return tile[:].rearrange("p (t b c) -> p c b t", b=B, c=C)

            dve.sem_inc(s("oT_ready"), 2)

            def widen(n, u):
                dve.wait_ge(s("inter_done"), n + 1)
                v.tensor_tensor(
                    wide[u].rearrange("p (n h v) -> p n h v", n=ST * B, h=H),
                    Sst[:, ds(n * ST * B * HD, ST * B * HD)].rearrange(
                        "p (n v) -> p n v", n=ST * B).unsqueeze(2).broadcast_to([P, ST * B, H, HD]),
                    hm.unsqueeze(1).unsqueeze(3).broadcast_to([P, ST * B, H, HD]),
                    ALU.mult).then_inc(s("state_wide"), 1)

            def add_own(n, u):
                dve.wait_ge(s("inter_done"), n + 3)
                v.tensor_tensor(
                    by_chunk(tG)[:, ds(n * ST, ST), :, :],
                    ps[6 + u][:].rearrange("p (c b t) -> p c b t", c=ST, b=B),
                    by_chunk(tG)[:, ds(n * ST, ST), :, :], ALU.add).then_inc(s("oT_ready"), 1)

            dve.wait_ge(s("outs_in"), NS)
            widen(0, 0)
            def invert_roots(g):
                dve.wait_ge(s("oroot_ready"), g + 1)
                r = tK[:, 3072 + g * SC:3072 + (g + 1) * SC]
                v.reciprocal(r, r).then_inc(s("oscale_ready"), 1)

            def scale_o(n):
                dve.wait_ge(s("spread_done"), n + 1)
                o = by_chunk(tG)[:, n * ST:(n + 1) * ST, :, :]
                v.tensor_tensor(o, o, ps[2 + n % 2][:].rearrange("p (c b t) -> p c b t", c=ST, b=B),
                                ALU.mult).then_inc(s("onT_ready"), 1)

            for n in range(NS):
                if n + 1 < NS:
                    widen(n + 1, (n + 1) % 2)
                add_own(n, n % 2)
                if EARLY_LATE + 1 + n < LATE_UNITS:
                    late_expert(EARLY_LATE + 1 + n)
                if n == 5:
                    invert_roots(0)
                elif n >= 6:
                    scale_o(2 * n - 12)
                    scale_o(2 * n - 11)
            invert_roots(1)
            for n in range(4, NS):
                scale_o(n)
            dve.wait_ge(s("x_biased"), 1)
            for i in range(NS):
                xi = tA[:, i * SC:(i + 1) * SC]
                dve.wait_ge(s("wo0_done"), i + 1)
                link(v.tensor_tensor(xi, ps[4 + i % 4][:], xi, ALU.add))
                v.tensor_tensor(xi, xi, x_res[:, i * SC:(i + 1) * SC], ALU.add).then_inc(s("x1_ready"), 1)
                if i == NS // 2:
                    dve.wait_ge(last_in, 16)
                    v.tensor_tensor(fold1.rearrange("p (i n) -> p i n", i=K1),
                                    V["inT"].unsqueeze(1).broadcast_to([P, K1, 3 * P]),
                                    V["short"].rearrange("p (i n) -> p i n", i=K1),
                                    ALU.mult).then_inc(s("fold1_ready"), 1)
                dve.wait_ge(s("x1_ready"), i + 1)
                last = token_stats(i, tA)
            link(last)
            mean_var()
            dve.wait_ge(s("std_ready"), 3)
            second_var()
            link(v.memset(znT[:, 0:(K1 - 1) * P], 0.0))
            halo1 = znT[:, 0:(K1 - 1) * P].rearrange("p (t b c) -> p t b c", b=B, c=C)
            src1 = znT[:, T * P:(T + K1 - 1) * P].rearrange("p (t b c) -> p t b c", b=B, c=C)

            def scale_xn1(n):
                i = TURN_ORDER[n]
                dve.wait_ge(s("xn1_ready"), n + 1)
                v.tensor_tensor(tK[:, i * SC:(i + 1) * SC].rearrange("p (t n) -> p t n", t=ST),
                                tG[:, i * SC:(i + 1) * SC].rearrange("p (t n) -> p t n", t=ST),
                                rstd2[:, i * ST:(i + 1) * ST].unsqueeze(2).broadcast_to([P, ST, P]),
                                ALU.mult).then_inc(s("zn_ready"), 1)

            for n, i in enumerate(TURN_ORDER):
                normalise(i, tA, tG).then_inc(s("xn1_ready"), 1)
                if n == 1:
                    dve.wait_ge(s("std_ready"), 4)
                    link(v.reciprocal(rstd2, rstd2))
                if n >= 1:
                    scale_xn1(n - 1)
                if n == 4:
                    dve.wait_ge(s("znT_ready"), 1)
                    for t in range(K1 - 1):
                        last = v.tensor_copy(halo1[:, t, :, 1:C], src1[:, t, :, 0:C - 1])
                    last.then_inc(s("halo1_ready"), 1)
            scale_xn1(NS - 1)
            dve.sem_inc(s("xv_ready"), 2)
            dve.sem_inc(s("gate1_in"), 1)
            with dve.Fori(0, NS // 2) as m:
                for u in range(2):
                    i = 2 * m + u
                    dve.wait_ge(s("z_out"), i + 3)
                    v.scalar_tensor_tensor(
                        out=tF[:].rearrange("p (n t) -> p t n", t=T)[:, ds(i * ST, ST), :],
                        in0=ps[4 * u + 1][:].rearrange("p (t n) -> p t n", t=ST), scalar=V["shortb"][:, 2:3],
                        in1=stage[:, u * SC:(u + 1) * SC].rearrange("p (t n) -> p t n", t=ST),
                        op0=ALU.add, op1=ALU.mult).then_inc(s("xv_ready"), 1)
                    dve.wait_ge(s("gate1_turned"), i + 1)
                    v.tensor_copy(brt[:, ds(i * ST * E1, ST * E1)], ps[7][:, 0:ST * E1]).then_inc(s("gate1_in"), 1)
            dve.wait_ge(s("gate1_in"), NS + 1)
            lg = brt[:, 0:T * E1].rearrange("p (t e) -> p t e", e=E1)
            one, two, prob, work = m3
            link(v.tensor_reduce(top, lg, AX.X, ALU.max))
            v.tensor_tensor(prob, lg, over_e(top), ALU.subtract).then_inc(s("shifted1"), 1)
            dve.wait_ge(s("exp1_ready"), 1)
            link(v.tensor_reduce(top, prob, AX.X, ALU.add))
            link(v.reciprocal(top, top))
            link(v.tensor_tensor(prob, prob, over_e(top), ALU.mult))
            for n, pick in ((0, one), (1, two)):
                best = small[:, (6 + n) * T:(7 + n) * T]
                link(v.tensor_reduce(best, prob, AX.X, ALU.max))
                link(v.tensor_tensor(pick, prob, over_e(best), ALU.is_equal))
                link(v.tensor_tensor(pick, pick, desc, ALU.mult))
                link(v.tensor_reduce(top, pick, AX.X, ALU.max))
                link(v.tensor_tensor(pick, pick, over_e(top), ALU.is_equal))
                if n == 0:
                    link(v.scalar_tensor_tensor(out=prob, in0=pick, scalar=-4.0, in1=prob, op0=ALU.mult, op1=ALU.add))
            link(v.tensor_tensor(two, two, one, ALU.subtract))
            weight = small[:, 6 * T:7 * T]
            link(v.tensor_tensor(weight, weight, small[:, 7 * T:8 * T], ALU.add))
            v.tensor_scalar(V["bo1"], V["bo1"], 2.0, None, ALU.mult).then_inc(s("picks_ready"), 1)
            dve.wait_ge(s("decay_ready"), 1)
            dve.wait_ge(s("xv_ready"), NS + 2)
            dve.sem_inc(s("ffn1_in"), 1)

            def mask_ranks(i, u):
                dve.wait_ge(s("pick_turned"), i + 2)
                dve.wait_ge(s("axs_ready"), i + 2)
                v.tensor_tensor(axm[u][0], ps[5][:], axs, ALU.mult)
                v.tensor_tensor(axm[u][1], ps[7][:], axs, ALU.mult).then_inc(s("axm_ready"), 1)

            def sum_pole(b, q):
                res = V["res"][:, DVE_POLES[q]:DVE_POLES[q] + 1]
                if q == 0:
                    dve.wait_ge(s("y_taken"), b + 1)
                    link(v.tensor_scalar(y_dve, scan[0], res, None, ALU.mult))
                elif q < len(DVE_POLES) - 1:
                    link(v.scalar_tensor_tensor(out=y_dve, in0=scan[q % 2], scalar=res, in1=y_dve,
                                                op0=ALU.mult, op1=ALU.add))
                else:
                    v.scalar_tensor_tensor(out=y_dve, in0=scan[q % 2], scalar=res, in1=y_dve,
                                           op0=ALU.mult, op1=ALU.add).then_inc(s("y_dve_ready"), 1)
                    dve.wait_ge(s("y_dve_ready"), b + 1)

            def filter_batch(b, final=False):
                xb = tF[:, ds(b * L, L)]
                for n in range(NP1):
                    u, slot = n // 8, n % 8
                    if slot == MASK_AT and not (final and u == 1):
                        mask_ranks(2 * b + u + 1, 1 - u)
                    pole = V["poles"][:, n:n + 1].broadcast_to([P, L])
                    if n in POOL_POLES:
                        k = POOL_POLES.index(n)
                        dve.wait_ge(s("pole_added"), b * len(POOL_POLES) + k + 1)
                        v.tensor_tensor_scan(pool_scan[k % len(pool_scan)], pole, xb, 0.0,
                                             ALU.mult, ALU.add).then_inc(s("pole_scanned"), 1)
                    else:
                        q = DVE_POLES.index(n)
                        link(v.tensor_tensor_scan(scan[q % 2], pole, xb, 0.0, ALU.mult, ALU.add))
                        if q >= 1:
                            sum_pole(b, q - 1)
                sum_pole(b, len(DVE_POLES) - 1)

            dve.sem_inc(s("pole_added"), len(pool_scan))
            dve.sem_inc(s("y_taken"), 1)
            mask_ranks(0, 0)
            filter_batch(0)
            with dve.Fori(0, B - 2) as m:
                ch.enter(m, 2 * (NP1 - len(POOL_POLES)) - 1)
                filter_batch(m + 1)
            ch.leave(B - 2)
            filter_batch(B - 1, final=True)
            dve.wait_ge(s("pole_added"), B * len(POOL_POLES) + len(pool_scan))
            dve.wait_ge(s("x2_ready"), NS + 2)
            link(v.tensor_tensor(y_dve, y_dve, y_pool, ALU.add))
            x2b = tB[:].rearrange("p (t n) -> p t n", t=T)[:, :, (B - 1) * C:B * C]
            v.tensor_tensor(x2b, x2b, y_dve.rearrange("p (c t) -> p t c", t=T), ALU.mult).then_inc(s("yT_ready"), 1)
            ms = small[:, 8 * T:9 * T]
            for i in range(NS + 1):
                if i < NS:
                    dve.wait_ge(s("yo_done"), i + 1)
                    y = tG[:, i * SC:(i + 1) * SC]
                    v.tensor_tensor(y, ps[i % 4][:], y, ALU.add).then_inc(s("y_ready"), 1)
                if i >= 1:
                    dve.wait_ge(s("y_squared"), i)
                    v.tensor_reduce(ms[:, (i - 1) * ST:i * ST],
                                    tK[:, (i - 1) * SC:i * SC].rearrange("p (t n) -> p t n", t=ST),
                                    AX.X, ALU.add).then_inc(s("ms_ready"), 1)
            dve.wait_ge(s("rms_ready"), 1)
            link(v.reciprocal(ms, ms))

            def scale_y(i, u):
                dve.wait_ge(s("zm_turned"), i + 1)
                v.tensor_tensor(stage[:, u * SC:(u + 1) * SC].rearrange("p (t n) -> p t n", t=ST),
                                tG[:, ds(i * SC, SC)].rearrange("p (t n) -> p t n", t=ST),
                                ms[:, ds(i * ST, ST)].unsqueeze(2).broadcast_to([P, ST, P]),
                                ALU.mult).then_inc(s("zs_staged"), 1)

            def gate_hidden(i, u):
                for f in range(3):
                    dve.wait_ge(s("gelu_ready"), i * 3 + f + 1)
                    dve.wait_ge(s("l2_done"), i * 3 + f + 1)
                    c = (3 * u + f) * SC
                    v.tensor_tensor(tK[0:FT, c:c + SC], tJ[0:FT, c:c + SC],
                                    ps[5 + f][0:FT, :], ALU.mult).then_inc(s("gated_ready"), 1)

            def finish(i):
                dve.wait_ge(s("mlp_done"), i + 1)
                dve.wait_ge(s("residual_ready"), i + 1)
                xi = tA[:, ds(i * SC, SC)]
                v.tensor_tensor(xi, xi, ps[0][:], ALU.add).then_inc(s("result_ready"), 1)

            dve.sem_inc(s("gated_ready"), 3)
            dve.sem_inc(s("result_ready"), 1)
            scale_y(0, 0)
            scale_y(1, 1)
            gate_hidden(0, 0)
            with dve.Fori(0, NS // 2 - 1) as m:
                for u in range(2):
                    scale_y(2 * m + u + 2, u)
                    gate_hidden(2 * m + u + 1, 1 - u)
                    finish(2 * m + u)
            gate_hidden(NS - 1, 1)
            finish(NS - 2)
            finish(NS - 1)

        @block.scalar
        def _(act):
            ch = Count(act, act_steps)
            link = ch.link
            a = nc.scalar

            def root(out, in_, eps, need, done):
                act.wait_ge(*need)
                a.activation(out, in_, ACT.Sqrt, bias=eps).then_inc(done, 1)

            eps5 = small[:, 11 * T:11 * T + 1]
            eps6 = small[:, 11 * T + 1:11 * T + 2]
            act.wait_ge(s("eps_set"), 1)
            root(rstd, var, eps5, (s("var_ready"), 1), s("std_ready"))
            root(rstd2, var, eps5, (s("var_ready"), 2), s("std_ready"))
            for n, i in enumerate(TURN_ORDER):
                act.wait_ge(s("xn_turned"), n + 1)
                a.activation(xnT0[:, i * SC:(i + 1) * SC], ps[4 + n % 4][:], ACT.Copy).then_inc(s("xnT_ready"), 1)
            act.wait_ge(s("biasq_ready"), 1)
            act.sem_inc(s("qkv_in"), 1)

            def stage_qkv(i, u):
                act.wait_ge(s("qkv_turned"), i + 1)
                for n in range(3):
                    act.wait_ge(s("qkv_done"), i * 4 + n + 1)
                    a.activation(stages[u][:, n * SC:(n + 1) * SC], ps[n][:], ACT.Identity,
                                 bias=biasq[:, n:n + 1]).then_inc(s("qkv_staged"), 1)
                act.wait_ge(s("qkv_done"), i * 4 + 4)
                a.activation(stages[u][0:H + E0, 3 * SC:4 * SC], ps[3][0:H + E0, :], ACT.Identity,
                             bias=W["bbr"][0:H + E0, :]).then_inc(s("qkv_staged"), 1)

            def take_qkv(i):
                act.wait_ge(s("qkv_turned"), i + 3)
                qvi = qv[:, ds(i * 2 * SC, 2 * SC)].rearrange("p (t n) -> p t n", t=ST)
                a.activation(qvi[:, :, 0:P], ps[4][:].rearrange("p (t n) -> p t n", t=ST), ACT.Copy)
                a.activation(k_tm[:, ds(i * SC, SC)], ps[5][:], ACT.Copy)
                a.activation(brt[:, ds(i * ST * (H + E0), ST * (H + E0))], ps[7][:, 0:ST * (H + E0)], ACT.Copy)
                a.activation(qvi[:, :, P:2 * P], ps[6][:].rearrange("p (t n) -> p t n", t=ST),
                             ACT.Silu).then_inc(s("qkv_in"), 1)

            qvt = qv.rearrange("p (t n) -> p t n", t=T)
            bt = brt[:].rearrange("p (t n) -> p t n", t=T)

            def square_qk(g):
                t0, n = GROUPS[g][0] * ST, GROUPS[g][1] * ST
                q2, k2 = squares(g)
                act.wait_ge(s("qkv_in"), 1 + GROUPS[g][0] + GROUPS[g][1])
                a.activation(q2.rearrange("p (t n) -> p t n", t=n), qvt[:, t0:t0 + n, 0:P],
                             ACT.Square).then_inc(s("squared"), 1)
                a.activation(k2, k_tm[:, t0 * P:(t0 + n) * P], ACT.Square).then_inc(s("squared"), 1)

            def gates_and_norms(g):
                t0, n = GROUPS[g][0] * ST, GROUPS[g][1] * ST
                act.wait_ge(s("norms_summed"), g + 1)
                a.activation(tK[:, 0:2 * n * H], tK[:, 0:2 * n * H], ACT.Sqrt).then_inc(s("norms_ready"), 1)
                act.wait_ge(s("shifted0"), g + 1)
                g1 = gates[:, T * E0 + t0 * E0:T * E0 + (t0 + n) * E0]
                a.activation(g1, g1, ACT.Exp).then_inc(s("exp0_ready"), 1)
                b1 = bt[:, t0:t0 + n, 0:H]
                a.activation(b1, b1, ACT.Sigmoid).then_inc(s("beta_ready"), 1)

            for i in range(NS):
                act.wait_ge(s("xe_turned"), i + 1)
                a.activation(tB[:, i * SC:(i + 1) * SC], ps[4 + i % 4][:], ACT.Identity, bias=F["ln_b"],
                             scale=F["ln_g"]).then_inc(s("xeT_ready"), 1)
                if i == 3:
                    stage_qkv(0, 0)
            for i in range(AHEAD):
                stage_qkv(i + 1, 1 - i % 2)
                take_qkv(i)
            square_qk(0)
            gates_and_norms(0)
            with act.Fori(0, (NS - AHEAD) // 2 - 1) as m:
                for u in range(2):
                    stage_qkv(AHEAD + 2 * m + u + 1, 1 - u)
                    take_qkv(AHEAD + 2 * m + u)
            stage_qkv(NS - 1, 1)
            take_qkv(NS - 2)
            take_qkv(NS - 1)
            act.sem_inc(s("hid_ready"), FS)

            def hidden0(e, unit, buf):
                act.wait_ge(s("y0_ready"), unit + 1)
                for f in range(FS):
                    act.wait_ge(s("hid_done"), unit * FS + f + 1)
                    a.activation(tC[:, buf * 2048 + f * SC:buf * 2048 + (f + 1) * SC], ps[f][:],
                                 ACT.Relu, bias=F["b1"][:, e * FS + f:e * FS + f + 1]).then_inc(s("hid_ready"), 1)

            def outs_stage(i):
                act.wait_ge(s("out_done"), (i + 1) * ST + 2)
                act.wait_ge(s("outs_turned"), i + 1)
                sr = tDE[:, ds(i * 2 * SC, 2 * SC)].rearrange("p (th j) -> p th j", j=J)
                for n in range(2):
                    last = a.activation(stage[:, n * SC:(n + 1) * SC].rearrange("p (th k) -> p th k", k=HD),
                                        sr[:, :, n * HD:(n + 1) * HD], ACT.Copy)
                last.then_inc(s("outs_staged"), 1)

            def outs_take(i):
                act.wait_ge(s("outs_turned"), i + 2)
                a.activation(tF[:, ds(i * SC, SC)], ps[6][:], ACT.Copy)
                a.activation(tG[:, ds(i * SC, SC)], ps[7][:], ACT.Copy).then_inc(s("outs_in"), 1)

            outs_stage(0)
            for e in range(E0):
                hidden0(e, e, e % 2)
                if e == 0:
                    square_qk(1)
                elif e == 1:
                    outs_take(0)
                elif e == 4:
                    gates_and_norms(1)
            with act.Fori(0, BESIDE // 2) as m:
                for w in range(2):
                    i = 2 * m + w
                    for e in range(1, E0):
                        hidden0(e, i * EB + E0 + e - 1, (w + e - 1) % 2)
                        if e == OUTS_AT:
                            outs_stage(i + 1)
                        elif e == OUTS_AT + 2:
                            outs_take(i + 1)
            for n, (_, e) in enumerate(LATE_PAIRS):
                hidden0(e, LATE_FROM + n, (LATE_FROM + n) % 2)
                if n == OUTS_LATE:
                    outs_stage(NS - 1)
                elif n == OUTS_LATE + 2:
                    outs_take(NS - 1)
            def square_o(n):
                act.wait_ge(s("oT_ready"), n + 3)
                act.wait_ge(s("states_turned"), 1)
                a.activation(o_sq[:, n * SC:(n + 1) * SC].rearrange("p (c b t) -> p c b t", c=ST, b=B),
                             tG[:].rearrange("p (t b c) -> p c b t", b=B, c=C)[:, n * ST:(n + 1) * ST, :, :],
                             ACT.Square).then_inc(s("o_squared"), 1)

            def take_mask(i):
                act.wait_ge(s("mask_turned"), i + 1)
                a.activation(maskT[:, i * SC:(i + 1) * SC], ps[4 + i % 2][0:E0, :],
                             ACT.Copy).then_inc(s("maskT_ready"), 1)

            def roots(g):
                act.wait_ge(s("o_meaned"), 4 * g + 4)
                a.activation(tK[:, 3072 + g * SC:3072 + (g + 1) * SC], ps[g][:], ACT.Sqrt,
                             bias=eps6).then_inc(s("oroot_ready"), 1)

            act.wait_ge(s("y0_ready"), UNITS + 2)
            for n in range(NS):
                square_o(n)
                if n >= 3 and n < NS - 1:
                    take_mask(2 * n - 6)
                    take_mask(2 * n - 5)
                if n % 4 == 3:
                    roots(n // 4)
            root(rstd, var, eps5, (s("var_ready"), 3), s("std_ready"))
            root(rstd2, var, eps6, (s("var_ready"), 4), s("std_ready"))
            a.activation(V["poles"], V["poles"], ACT.Exp).then_inc(s("decay_ready"), 1)
            act.wait_ge(s("wo0_done"), NS)
            for n in range(NS + 1):
                if n < NS:
                    i = TURN_ORDER[n]
                    act.wait_ge(s("xn1_turned"), n + 1)
                    a.activation(tC[:, i * SC:(i + 1) * SC], ps[4 + n % 2][:], ACT.Copy).then_inc(s("xn1T_ready"), 1)
                if n >= 1:
                    i = TURN_ORDER[n - 1]
                    act.wait_ge(s("zn_turned"), n)
                    a.activation(znT[:, (K1 - 1 + i * ST) * P:(K1 - 1 + (i + 1) * ST) * P], ps[6 + (n - 1) % 2][:],
                                 ACT.Copy, scale=V["pre_w"]).then_inc(s("znT_ready"), 1)
            act.sem_inc(s("z_out"), 2)
            with act.Fori(0, NS // 2) as m:
                for u in range(2):
                    i = 2 * m + u
                    act.wait_ge(s("xv_ready"), i + 1)
                    act.wait_ge(s("z_done"), i + 1)
                    a.activation(stage[:, u * SC:(u + 1) * SC], ps[4 * u][:], ACT.Identity,
                                 bias=V["shortb"][:, 1:2])
                    a.activation(stage[0:E1, (2 + u) * SC:(3 + u) * SC], ps[3][0:E1, :], ACT.Identity,
                                 bias=V["gateb"][0:E1, :]).then_inc(s("z_out"), 1)
            act.wait_ge(s("shifted1"), 1)
            a.activation(m_prob, m_prob, ACT.Exp).then_inc(s("exp1_ready"), 1)
            with act.Fori(0, NS // 2) as m:
                for u in range(2):
                    act.wait_ge(s("x2_done"), 2 * m + u + 1)
                    a.activation(tB[:, ds((2 * m + u) * SC, SC)], ps[4 * u + 2][:], ACT.Identity,
                                 bias=V["shortb"][:, 0:1]).then_inc(s("x2_ready"), 1)
            act.sem_inc(s("h1_ready"), FS)
            act.sem_inc(s("axs_ready"), 1)
            act.wait_ge(s("picks_ready"), 1)

            def spread_picks(i):
                act.wait_ge(s("pick_turned"), i + 1)
                for n in range(2):
                    last = a.activation(picks[:, n * SC:(n + 1) * SC].rearrange("p (te r) -> p te r", r=RK),
                                        gates[:, ds(n * T * E1 + i * ST * E1, ST * E1)].unsqueeze(2).broadcast_to(
                                            [P, ST * E1, RK]), ACT.Copy)
                last.then_inc(s("pick_staged"), 1)

            def take_ranks(i):
                act.wait_ge(s("ax_done"), i + 1)
                act.wait_ge(s("axm_ready"), i + 1)
                a.activation(axs, ps[6][:], ACT.Copy).then_inc(s("axs_ready"), 1)

            def hidden1(i, n):
                for f in range(FS):
                    act.wait_ge(s("h1_done"), i * 2 * FS + n * FS + f + 1)
                    act.wait_ge(s("hsum_ready"), i * FS + f + 1)
                    c = (n * FS + f) * SC
                    a.activation(tJ[:, c:c + SC], ps[f][:], ACT.Relu,
                                 bias=V["bi"][:, f:f + 1]).then_inc(s("h1_ready"), 1)

            def scale_pole(i, u, k):
                n = POOL_POLES[u * len(pool_scan) + k]
                act.wait_ge(s("pole_scanned"), i * len(pool_scan) + k + 1)
                a.activation(pool_scan[k], pool_scan[k], ACT.Copy,
                             scale=V["res"][:, n:n + 1]).then_inc(s("pole_scaled"), 1)

            def start_filter(b):
                act.wait_ge(s("yT_ready"), b + 1)
                a.activation(y_pool, tF[:, ds(b * L, L)], ACT.Copy, scale=V["skip"]).then_inc(s("skip_ready"), 1)

            weight = small[:, 6 * T:7 * T]

            def weigh(i):
                act.wait_ge(s("y1_done"), i + 2)
                act.wait_ge(s("bias_added"), 1)
                for j in range(ST):
                    last = a.activation(tI[:, ds(i * SC + j * P, P)], ps[4][:, j * P:(j + 1) * P], ACT.Copy,
                                        scale=weight[:, ds(i * ST + j, 1)])
                last.then_inc(s("ffn1_in"), 1)

            def ffn_step(i, u, b, first=False, last=False):
                if not first:
                    weigh(i - 2)
                if not last:
                    spread_picks(i + 1)
                if not last:
                    take_ranks(i + 1)
                hidden1(i, 0)
                if u == 0:
                    start_filter(b)
                scale_pole(i, u, 0)
                scale_pole(i, u, 1)
                if last:
                    scale_pole(i, u, 2)
                hidden1(i, 1)
                if not last:
                    scale_pole(i, u, 2)

            act.sem_inc(s("pick_turned"), 1)
            act.sem_inc(s("axm_ready"), 1)
            act.sem_inc(s("yT_ready"), 1)
            act.wait_ge(s("xv_ready"), NS + 2)
            spread_picks(0)
            take_ranks(0)
            ffn_step(0, 0, 0, first=True)
            ffn_step(1, 1, 0, first=True)
            with act.Fori(0, B - 2) as b:
                ffn_step(2 * b + 2, 0, b + 1)
                ffn_step(2 * b + 3, 1, b + 1)
            ffn_step(NS - 2, 0, B - 1)
            ffn_step(NS - 1, 1, B - 1, last=True)
            weigh(NS - 2)
            weigh(NS - 1)
            for i in range(NS):
                act.wait_ge(s("y_ready"), i + 1)
                a.activation(tK[:, i * SC:(i + 1) * SC], tG[:, i * SC:(i + 1) * SC],
                             ACT.Square).then_inc(s("y_squared"), 1)
            act.wait_ge(s("ms_ready"), NS)
            a.activation(small[:, 8 * T:9 * T], small[:, 8 * T:9 * T], ACT.Sqrt, bias=eps6,
                         scale=1.0 / P).then_inc(s("rms_ready"), 1)

            def take_zm(i, u):
                act.wait_ge(s("zm_turned"), i + 3)
                a.activation(stage[:, (2 + u) * SC:(3 + u) * SC], ps[1][:], ACT.Copy,
                             scale=V["post_w"]).then_inc(s("zmT_ready"), 1)

            def gelus(i, u):
                for f in range(3):
                    act.wait_ge(s("l1_done"), i * 3 + f + 1)
                    c = (3 * u + f) * SC
                    a.activation(tJ[0:FT, c:c + SC], ps[2 + f][0:FT, :],
                                 ACT.Gelu_apprx_tanh).then_inc(s("gelu_ready"), 1)

            take_zm(0, 0)
            with act.Fori(0, NS // 2 - 1) as m:
                for u in range(2):
                    gelus(2 * m + u, u)
                    take_zm(2 * m + u + 1, 1 - u)
            gelus(NS - 2, 0)
            take_zm(NS - 1, 1)
            gelus(NS - 1, 1)

        @block.tensor
        def _(pe):
            t_ = nc.tensor

            pe.wait_ge(fixed_in, 16)
            for n, i in enumerate(TURN_ORDER):
                pe.wait_ge(s("xn_ready"), n + 1)
                if n >= 4:
                    pe.wait_ge(s("xnT_ready"), n - 3)
                for t in range(i * ST, (i + 1) * ST):
                    last = t_.transpose(ps[4 + n % 4][:, (t % ST) * P:(t % ST + 1) * P], tA[:, t * P:(t + 1) * P], ident)
                last.then_inc(s("xn_turned"), 1)

            pe.sem_inc(s("qkv_staged"), 4)
            pe.sem_inc(s("qkv_turned"), 2)
            pe.wait_ge(s("xnT_ready"), NS)
            pe.wait_ge(s("halo0_ready"), 1)
            pe.wait_ge(s("fold0_ready"), 1)

            def project0(i):
                for n in range(3):
                    pe.wait_ge(s("qkv_staged"), i * 4 + n + (2 if n == 2 else 1))
                    for tap in range(K0):
                        last = t_.matmul(ps[n][:], lhsT=fold0[:, tap * 3 * P + n * P:tap * 3 * P + (n + 1) * P],
                                         rhs=tC[:, ds(i * SC + tap * P, SC)], start=tap == 0, stop=tap == K0 - 1)
                    last.then_inc(s("qkv_done"), 1)
                t_.matmul(ps[3][0:H + E0, :], lhsT=W["wbrT"], rhs=tC[:, ds(i * SC + 3 * P, SC)],
                          start=True, stop=True).then_inc(s("qkv_done"), 1)

            def turn0(i, u):
                pe.wait_ge(s("qkv_staged"), i * 4 + 8)
                pe.wait_ge(s("qkv_in"), i + 1)
                pe.wait_ge(s("corrected"), 1)
                for n in range(3):
                    for j in range(ST):
                        c = n * SC + j * P
                        t_.transpose(ps[4 + n][:, j * P:(j + 1) * P], stages[u][:, c:c + P], ident)
                for j in range(ST):
                    last = t_.transpose(ps[7][:, j * (H + E0):(j + 1) * (H + E0)],
                                        stages[u][0:H + E0, 3 * SC + j * P:3 * SC + (j + 1) * P],
                                        ident[0:H + E0, 0:H + E0])
                last.then_inc(s("qkv_turned"), 1)

            project0(0)
            pe.wait_ge(s("xe_ready"), 1)
            pe.wait_ge(s("xnT_ready"), NS)
            for i in range(NS):
                if i >= 4:
                    pe.wait_ge(s("xeT_ready"), i - 3)
                for t in range(i * ST, (i + 1) * ST):
                    last = t_.transpose(ps[4 + i % 4][:, (t % ST) * P:(t % ST + 1) * P],
                                        tA[:, t * P:(t + 1) * P], ident)
                last.then_inc(s("xe_turned"), 1)
            pe.wait_ge(s("xeT_ready"), NS)
            with pe.Fori(0, NS // 2 - 1) as m:
                for u in range(2):
                    project0(2 * m + u + 1)
                    turn0(2 * m + u, u)
            project0(NS - 1)
            turn0(NS - 2, 0)
            turn0(NS - 1, 1)
            pe.wait_ge(s("qkv_staged"), 4 * NS + 4)

            pe.sem_inc(s("y0_ready"), 2)
            pe.wait_ge(w1_in, 16)
            pe.wait_ge(s("qkv_in"), NS + 1)
            pe.wait_ge(s("xeT_ready"), NS)

            def up(i, e, unit):
                for f in range(FS):
                    pe.wait_ge(s("hid_ready"), unit * FS + f + 1)
                    t_.matmul(ps[f][:], lhsT=tH[:, (e * FS + f) * P:(e * FS + f + 1) * P],
                              rhs=tB[:, ds(i * SC, SC)], start=True, stop=True).then_inc(s("hid_done"), 1)

            def down(e, unit, buf):
                pe.wait_ge(s("y0_used"), unit + 1)
                pe.wait_ge(s("hid_ready"), unit * FS + 2 * FS)
                for j in range(ST):
                    for f in range(FS):
                        c = buf * 2048 + f * SC + j * P
                        last = t_.matmul(ps[4 + buf][:, j * P:(j + 1) * P], lhsT=tC[:, c:c + P],
                                         rhs=tI[:, (e * FS + f) * P:(e * FS + f + 1) * P],
                                         start=f == 0, stop=f == FS - 1)
                last.then_inc(s("y0_ready"), 1)

            def outs_turn(i):
                pe.wait_ge(s("outs_staged"), i + 1)
                for n in range(2):
                    for j in range(ST):
                        last = t_.transpose(ps[6 + n][:, j * P:(j + 1) * P],
                                            stage[:, n * SC + j * P:n * SC + (j + 1) * P], ident)
                last.then_inc(s("outs_turned"), 1)

            pe.sem_inc(s("outs_turned"), 1)
            for e in range(E0):
                up(0, e, e)
                if e == 0:
                    outs_turn(0)
                    pe.wait_ge(w2_in, 16)
                else:
                    down(e - 1, e - 1, (e - 1) % 2)
                if e == 2:
                    pe.wait_ge(w1b_in, 16)
            with pe.Fori(0, BESIDE // 2) as m:
                for w in range(2):
                    i = 2 * m + w
                    for e in range(1, E0):
                        unit = i * EB + E0 + e - 1
                        up(i + 1, e, unit)
                        down(e - 1 if e > 1 else E0 - 1, unit - 1, (w + e) % 2)
                        if e == OUTS_AT + 1:
                            outs_turn(i + 1)

            def late(n):
                unit = LATE_FROM + n
                if n < LATE_UNITS:
                    up(*LATE_PAIRS[n], unit)
                if n <= LATE_UNITS:
                    down(LATE_PAIRS[n - 1][1] if n else E0 - 1, unit - 1, (unit - 1) % 2)

            for n in range(EARLY_LATE + 2):
                late(n)
                if n == OUTS_LATE + 1:
                    outs_turn(NS - 1)
            pe.wait_ge(s("states_sorted"), 1)
            pe.wait_ge(s("outs_in"), NS)
            for n in range(HD):
                last = t_.transpose(ps[6 + n // 4][:, (n % 4) * P:(n % 4 + 1) * P],
                                    tK[:, 2048 + n * P:2048 + (n + 1) * P], ident)
            last.then_inc(s("states_turned"), 1)
            qmt = tF[:].rearrange("p (t n) -> p n t", t=T)

            def inter(n):
                u = n % 2
                pe.wait_ge(s("state_wide"), n + 1)
                pe.wait_ge(s("oT_ready"), n + 1)
                for a in range(ST):
                    for b in range(B):
                        k = a * B + b
                        last = t_.matmul(ps[6 + u][:, k * T:(k + 1) * T], lhsT=wide[u][:, k * P:(k + 1) * P],
                                         rhs=qmt[:, n * ST + a + b * C, :], start=True, stop=True)
                last.then_inc(s("inter_done"), 1)

            pe.sem_inc(s("inter_done"), 2)

            def turn_mask(i):
                if i >= 2:
                    pe.wait_ge(s("maskT_ready"), i - 1)
                for j in range(ST):
                    t = i * ST + j
                    last = t_.transpose(ps[4 + i % 2][0:E0, j * P:(j + 1) * P], mask0[:, t * E0:(t + 1) * E0], ident)
                last.then_inc(s("mask_turned"), 1)

            def mean(n):
                pe.wait_ge(s("o_squared"), n + 1)
                k = 32 * (n % 4)
                t_.matmul(ps[n // 4][k:k + 32, :], lhsT=F["headmean"], rhs=o_sq[:, n * SC:(n + 1) * SC],
                          start=True, stop=True).then_inc(s("o_meaned"), 1)

            def spread(n):
                k, g = 32 * (n % 4), n // 4
                pe.wait_ge(s("oscale_ready"), g + 1)
                if n >= 2:
                    pe.wait_ge(s("onT_ready"), n - 1)
                t_.matmul(ps[2 + n % 2][:], lhsT=F["headspread"][k:k + 32, :],
                          rhs=tK[k:k + 32, 3072 + g * SC:3072 + (g + 1) * SC],
                          start=True, stop=True).then_inc(s("spread_done"), 1)

            for n in range(NS):
                late(EARLY_LATE + 2 + n)
                inter(n)
                if n == 4:
                    pe.wait_ge(s("y0_used"), UNITS + 2)
                    pe.wait_ge(s("hid_ready"), UNITS * FS + FS)
                    for k in range(3):
                        mean(k)
                if n >= 4:
                    mean(n - 1)
                    turn_mask(2 * n - 8)
                    turn_mask(2 * n - 7)
                if n >= 6:
                    spread(2 * n - 12)
                    spread(2 * n - 11)
            mean(NS - 1)
            for n in range(4, NS):
                spread(n)
            pe.wait_ge(s("onT_ready"), NS)
            pe.wait_ge(s("oT_ready"), NS + 2)
            pe.wait_ge(s("maskT_ready"), NS)
            for i in range(NS):
                if i >= 4:
                    pe.wait_ge(s("x1_ready"), i - 3)
                for t in range(i * ST, (i + 1) * ST):
                    o = ps[4 + i % 4][:, (t % ST) * P:(t % ST + 1) * P]
                    t_.matmul(o, lhsT=tG[:, t * P:(t + 1) * P], rhs=F["woT"], start=True, stop=False)
                    last = t_.matmul(o, lhsT=maskT[:, t * P:(t + 1) * P], rhs=F["b2"][0:E0, :],
                                     start=False, stop=True)
                last.then_inc(s("wo0_done"), 1)
            for n in range(NS + 1):
                if n < NS:
                    i = TURN_ORDER[n]
                    pe.wait_ge(s("xn1_ready"), n + 1)
                    if n >= 2:
                        pe.wait_ge(s("xn1T_ready"), n - 1)
                    for t in range(i * ST, (i + 1) * ST):
                        last = t_.transpose(ps[4 + n % 2][:, (t % ST) * P:(t % ST + 1) * P],
                                            tG[:, t * P:(t + 1) * P], ident)
                    last.then_inc(s("xn1_turned"), 1)
                if n >= 1:
                    i = TURN_ORDER[n - 1]
                    pe.wait_ge(s("zn_ready"), n)
                    if n >= 3:
                        pe.wait_ge(s("znT_ready"), n - 2)
                    for t in range(i * ST, (i + 1) * ST):
                        last = t_.transpose(ps[6 + (n - 1) % 2][:, (t % ST) * P:(t % ST + 1) * P],
                                            tK[:, t * P:(t + 1) * P], ident)
                    last.then_inc(s("zn_turned"), 1)
            pe.wait_ge(s("znT_ready"), 2)
            pe.wait_ge(s("xn1T_ready"), 2)
            pe.wait_ge(s("halo1_ready"), 1)
            pe.wait_ge(s("fold1_ready"), 1)
            def project1(i, u):
                pe.wait_ge(s("z_out"), i + 1)
                pe.wait_ge(s("xv_ready"), i + 1)
                for n in range(2):
                    for tap in range(K1):
                        c = (tap * 3 + 1 + n) * P
                        t_.matmul(ps[4 * u + n][:], lhsT=fold1[:, c:c + P],
                                  rhs=znT[:, ds(i * SC + tap * P, SC)], start=tap == 0, stop=tap == K1 - 1)
                pe.wait_ge(s("z_out"), i + 2)
                t_.matmul(ps[3][0:E1, :], lhsT=V["gateT"], rhs=tC[:, ds(i * SC, SC)],
                          start=True, stop=True).then_inc(s("z_done"), 1)

            def turn_logits(i, u):
                pe.wait_ge(s("z_out"), i + 3)
                pe.wait_ge(s("gate1_in"), i + 1)
                pe.sem_inc(s("waits_apart"), 1)
                for j in range(ST):
                    last = t_.transpose(ps[7][:, j * E1:(j + 1) * E1],
                                        stage[0:E1, (2 + u) * SC + j * P:(2 + u) * SC + (j + 1) * P],
                                        ident[0:E1, 0:E1])
                last.then_inc(s("gate1_turned"), 1)

            project1(0, 0)
            pe.wait_ge(s("znT_ready"), NS)
            pe.wait_ge(s("xn1T_ready"), NS)
            with pe.Fori(0, NS // 2 - 1) as m:
                for u in range(2):
                    project1(2 * m + u + 1, 1 - u)
                    turn_logits(2 * m + u, u)
            project1(NS - 1, 1)
            turn_logits(NS - 2, 0)
            turn_logits(NS - 1, 1)
            pe.sem_inc(s("x2_ready"), 2)
            with pe.Fori(0, NS // 2) as m:
                for u in range(2):
                    i = 2 * m + u
                    pe.wait_ge(s("x2_ready"), i + 1)
                    for tap in range(K1):
                        last = t_.matmul(ps[4 * u + 2][:], lhsT=fold1[:, tap * 3 * P:tap * 3 * P + P],
                                         rhs=znT[:, ds(i * SC + tap * P, SC)], start=tap == 0, stop=tap == K1 - 1)
                    last.then_inc(s("x2_done"), 1)
            pe.sem_inc(s("y1_done"), 1)
            pe.wait_ge(s("gate1_in"), NS + 1)
            pe.wait_ge(s("xv_ready"), NS + 2)
            pe.wait_ge(s("x2_ready"), NS + 2)
            pe.wait_ge(s("picks_ready"), 1)

            def ranks(i):
                pe.wait_ge(s("axm_ready"), i + 1)
                pe.wait_ge(s("axs_ready"), i + 1)
                t_.matmul(ps[6][:], lhsT=V["loraAT"], rhs=tC[:, ds(i * SC, SC)],
                          start=True, stop=True).then_inc(s("ax_done"), 1)
                pe.wait_ge(s("pick_staged"), i + 1)
                for n in range(2):
                    for j in range(ST):
                        last = t_.transpose(ps[5 + 2 * n][:, j * P:(j + 1) * P],
                                            picks[:, n * SC + j * P:n * SC + (j + 1) * P], ident)
                last.then_inc(s("pick_turned"), 1)

            def first_pick(i, u, ahead=True):
                for f in range(FS):
                    pe.wait_ge(s("h1_ready"), i * 2 * FS + f + 1)
                    t_.matmul(ps[f][:], lhsT=V["wiT"][:, f * P:(f + 1) * P], rhs=tC[:, ds(i * SC, SC)],
                              start=True, stop=False)
                pe.wait_ge(s("axm_ready"), i + 2)
                if ahead:
                    ranks(i + 1)
                for f in range(FS):
                    t_.matmul(ps[f][:], lhsT=V["loraBT"][:, f * P:(f + 1) * P], rhs=axm[u][0],
                              start=False, stop=True).then_inc(s("h1_done"), 1)

            def second_pick(i, u):
                for f in range(FS):
                    pe.wait_ge(s("h1_ready"), i * 2 * FS + FS + f + 1)
                    t_.matmul(ps[f][:], lhsT=V["loraBT"][:, f * P:(f + 1) * P], rhs=axm[u][1],
                              start=False, stop=True, skip_group_check=True).then_inc(s("h1_done"), 1)

            def down1(i, sums):
                pe.wait_ge(s("ffn1_in"), i + 1)
                pe.wait_ge(s("hsum_ready"), i * FS + 2 * FS)
                for j in range(ST):
                    o = ps[4][:, j * P:(j + 1) * P]
                    for f in range(FS):
                        last = t_.matmul(o, lhsT=sums[:, f * SC + j * P:f * SC + (j + 1) * P],
                                         rhs=V["wo1T"][:, f * P:(f + 1) * P], start=f == 0, stop=f == FS - 1)
                last.then_inc(s("y1_done"), 1)

            ranks(0)
            first_pick(0, 0)
            second_pick(0, 0)
            with pe.Fori(0, NS // 2 - 1) as m:
                for u in range(2):
                    i = 2 * m + u + 1
                    first_pick(i, 1 - u)
                    second_pick(i, 1 - u)
                    down1(i - 1, tK)
            first_pick(NS - 1, 1, ahead=False)
            second_pick(NS - 1, 1)
            down1(NS - 2, tK)
            down1(NS - 1, tJ)
            pe.wait_ge(s("yT_ready"), B + 1)
            pe.wait_ge(s("h1_ready"), NS * 2 * FS + FS)
            for i in range(NS):
                if i >= 4:
                    pe.wait_ge(s("y_ready"), i - 3)
                for t in range(i * ST, (i + 1) * ST):
                    last = t_.matmul(ps[i % 4][:, (t % ST) * P:(t % ST + 1) * P], lhsT=tB[:, t * P:(t + 1) * P],
                                     rhs=V["outT"], start=True, stop=True)
                last.then_inc(s("yo_done"), 1)

            def turn_zm(i, u):
                pe.wait_ge(s("zs_staged"), i + 1)
                pe.wait_ge(s("zmT_ready"), i + 1)
                pe.sem_inc(s("waits_apart"), 1)
                for j in range(ST):
                    last = t_.transpose(ps[1][:, j * P:(j + 1) * P],
                                        stage[:, u * SC + j * P:u * SC + (j + 1) * P], ident)
                last.then_inc(s("zm_turned"), 1)

            def mlp_hidden(i, u):
                pe.wait_ge(s("zmT_ready"), i + 2)
                zmT = stage[:, (2 + u) * SC:(3 + u) * SC]
                for f in range(3):
                    pe.wait_ge(s("gated_ready"), i * 3 + f + 1)
                    t_.matmul(ps[2 + f][0:FT, :], lhsT=V["l1T"][:, f * FT:(f + 1) * FT], rhs=zmT,
                              start=True, stop=True).then_inc(s("l1_done"), 1)
                    t_.matmul(ps[5 + f][0:FT, :], lhsT=V["l2T"][:, f * FT:(f + 1) * FT], rhs=zmT,
                              start=True, stop=True).then_inc(s("l2_done"), 1)

            def mlp_out(i, u):
                pe.wait_ge(s("gated_ready"), i * 3 + 6)
                pe.wait_ge(s("result_ready"), i + 1)
                for j in range(ST):
                    for f in range(3):
                        c = (3 * u + f) * SC + j * P
                        last = t_.matmul(ps[0][:, j * P:(j + 1) * P], lhsT=tK[0:FT, c:c + P],
                                         rhs=V["l3T"][0:FT, f * P:(f + 1) * P], start=f == 0, stop=f == 2)
                last.then_inc(s("mlp_done"), 1)

            pe.wait_ge(s("y_ready"), NS)
            pe.sem_inc(s("zm_turned"), 2)
            pe.sem_inc(s("zmT_ready"), 1)
            turn_zm(0, 0)
            mlp_hidden(0, 0)
            turn_zm(1, 1)
            with pe.Fori(0, NS // 2 - 1) as m:
                for u in range(2):
                    mlp_hidden(2 * m + u + 1, 1 - u)
                    turn_zm(2 * m + u + 2, u)
                    mlp_out(2 * m + u, u)
            mlp_hidden(NS - 1, 1)
            mlp_out(NS - 2, 0)
            mlp_out(NS - 1, 1)

        @block.gpsimd
        def _(pool):
            ch = Count(pool, pool_steps)
            link = ch.link
            g = nc.gpsimd
            g.memset(small[:, 11 * T:11 * T + 1], 1e-5)
            g.memset(small[:, 11 * T + 1:11 * T + 2], 1e-6).then_inc(s("eps_set"), 1)
            pool.sem_inc(s("out_done"), 2)
            prod = tK[:, 2048:4096]
            prod4 = prod.rearrange("p (h j k) -> p h j k", h=H, j=J)
            p8 = prod.rearrange("p (n k) -> p n k", k=HD)

            def outputs(i):
                for t in range(ST):
                    state = R[(t + 1) % 2].rearrange("p (h j k) -> p h j k", h=H, j=J)
                    q = tDE[:, ds(i * 2 * SC + t * 2 * P, P)].rearrange("p (h k) -> p h k", k=HD)
                    pool.wait_ge(s("state_ready"), i * ST + t + 1)
                    pool.wait_ge(s("out_done"), i * ST + t + 2)
                    link(g.tensor_tensor(prod4, state, q.unsqueeze(2).broadcast_to([P, H, J, HD]), ALU.mult))
                    link(g.tensor_tensor(p8[:, :, 0:4], p8[:, :, 0:4], p8[:, :, 4:8], ALU.add))
                    link(g.tensor_tensor(p8[:, :, 0:2], p8[:, :, 0:2], p8[:, :, 2:4], ALU.add))
                    pool.sem_inc(s("waits_apart"), 1)
                    o = tDE[:, ds(i * 2 * SC + t * 2 * P, 2 * P)]
                    g.tensor_tensor(o, p8[:, :, 0], p8[:, :, 1], ALU.add).then_inc(s("out_done"), 1)

            for n, (first, steps) in enumerate(GROUPS):
                tokens = slice(first * ST, (first + steps) * ST)
                v4 = qv.rearrange("p (t n) -> p t n", t=T)[:, tokens, P:2 * P].rearrange("p t (h d) -> p t h d", d=HD)
                rk = tK[:, steps * ST * H:2 * steps * ST * H].rearrange("p (t h) -> p t h", h=H)
                pool.wait_ge(s("scales_ready"), n + 1)
                g.tensor_tensor(v4, v4, rk.unsqueeze(3).broadcast_to([P, steps * ST, H, HD]),
                                ALU.mult).then_inc(s("v_scaled"), 1)
                pool.wait_ge(s("prepared"), n + 1)
                pool.wait_ge(s("v_scaled"), n + 1)
                with pool.Fori(0, steps) as i:
                    ch.enter(i, 3 * ST)
                    outputs(i + first)
                ch.leave(steps)
            pool.wait_ge(x_again, 16)
            pool.wait_ge(late_in, 16)
            x3 = x_res.rearrange("p (t n) -> p t n", t=T)
            g.tensor_tensor(x3, x3, V["bo"].unsqueeze(1).broadcast_to([P, T, P]), ALU.add).then_inc(s("x_biased"), 1)
            pool.wait_ge(s("picks_ready"), 1)
            t3 = tI[:].rearrange("p (t n) -> p t n", t=T)
            weight = small[:, 6 * T:7 * T].unsqueeze(2).broadcast_to([P, T, P])
            link(g.tensor_tensor(t3, weight, V["bo1"].unsqueeze(1).broadcast_to([P, T, P]), ALU.mult))
            link(g.tensor_tensor(tA[:], tA[:], tI[:], ALU.add))
            pool.sem_inc(s("bias_added"), 1)
            pool.sem_inc(s("hsum_ready"), FS)
            pool.wait_ge(s("xv_ready"), NS + 2)
            pool.wait_ge(s("decay_ready"), 1)
            half = len(POOL_POLES) // 2

            def add_poles(b, u):
                for k in range(half):
                    pool.wait_ge(s("pole_scaled"), b * 2 * half + u * half + k + 1)
                    pool.wait_ge(s("skip_ready"), b + 1)
                    link(g.tensor_tensor(y_pool, y_pool, pool_scan[k], ALU.add))
                    pool.sem_inc(s("pole_added"), 1)

            def add_hidden(i, to):
                pool.wait_ge(s("y1_done"), i + 1)
                for f in range(FS):
                    pool.wait_ge(s("h1_ready"), i * 2 * FS + 2 * FS + f + 1)
                    g.tensor_tensor(to[:, f * SC:(f + 1) * SC], tJ[:, f * SC:(f + 1) * SC],
                                    tJ[:, (FS + f) * SC:(FS + f + 1) * SC], ALU.add).then_inc(s("hsum_ready"), 1)

            with pool.Fori(0, B - 1) as b:
                ch.enter(b, 1 + len(POOL_POLES))
                add_poles(b, 0)
                add_hidden(2 * b, tK)
                add_poles(b, 1)
                pool.wait_ge(s("y_dve_ready"), b + 1)
                link(g.tensor_tensor(y_pool, y_pool, y_dve, ALU.add))
                pool.sem_inc(s("y_taken"), 1)
                pool.wait_ge(s("x2_ready"), NS + 2)
                x2b = tB[:].rearrange("p (t n) -> p t n", t=T)[:, :, ds(b * C, C)]
                g.tensor_tensor(x2b, x2b, y_pool.rearrange("p (c t) -> p t c", t=T),
                                ALU.mult).then_inc(s("yT_ready"), 1)
                pool.wait_ge(s("yT_ready"), b + 2)
                add_hidden(2 * b + 1, tK)
            ch.leave(B - 1)
            add_poles(B - 1, 0)
            add_hidden(NS - 2, tK)
            add_poles(B - 1, 1)
            for f in range(FS):
                pool.wait_ge(s("h1_ready"), (NS - 1) * 2 * FS + 2 * FS + f + 1)
                g.tensor_tensor(tJ[:, f * SC:(f + 1) * SC], tJ[:, f * SC:(f + 1) * SC],
                                tJ[:, (FS + f) * SC:(FS + f + 1) * SC], ALU.add).then_inc(s("hsum_ready"), 1)
            pool.wait_ge(s("ffn1_in"), NS + 1)
            link(g.tensor_tensor(tA[:], tA[:], tI[:], ALU.add))
            for i in range(NS):
                pool.wait_ge(s("y_ready"), i + 1)
                g.tensor_tensor(tA[:, i * SC:(i + 1) * SC], tA[:, i * SC:(i + 1) * SC],
                                tG[:, i * SC:(i + 1) * SC], ALU.add).then_inc(s("residual_ready"), 1)


def kernel(**inputs):
    import numpy as np
    import concourse.bacc as bacc
    from concourse.bass_utils import run_bass_kernel_spmd as run

    a = {k: np.asarray(v) for k, v in inputs.items()}
    f32 = np.float32

    def rows(x, n=P):
        return np.broadcast_to(x.reshape(1, -1), (n, x.size))

    def padded(x, n=P):
        out = np.zeros((n,) + x.shape[1:], f32)
        out[:x.shape[0]] = x
        return out

    def col(x):
        return padded(x.reshape(-1, 1))

    p = np.arange(P)
    A, Fn, A1, F1 = "L0_attn_", "L0_ffn_", "L1_attn_", "L1_ffn_"
    fixed = dict(
        ident=np.eye(P, dtype=f32), headmask=(p[:, None] // HD == np.arange(H)[None]).astype(f32),
        headmean=(p[:, None] // HD == np.arange(32)[None] % H).astype(f32) / HD,
        headspread=(p[:, None] % 32 == p[None] // HD).astype(f32),
        descend=rows(np.arange(E0, 0, -1).astype(f32)),
        woT=a[A + "Wo"].T, norm_w=np.tile(a[A + "norm_w"], H).reshape(P, 1),
        ln_g=col(a[Fn + "ln_g"]), ln_b=col(a[Fn + "ln_b"]),
        b1=a[Fn + "b1"].reshape(E0 * FS, P).T, b2=padded(a[Fn + "b2"]))
    qkv = ("q", "k", "v")
    early = dict(
        wqkvT=np.concatenate([a[A + "W" + n].T for n in qkv], 1),
        conv=rows(np.concatenate([a[A + f"w{n}_conv"][:, i] for i in range(K0) for n in qkv])),
        wbrT=np.concatenate([a[A + "Wbeta"].T, a[Fn + "Wr"]], 1),
        taps=np.concatenate([a[A + f"w{n}_conv"] for n in qkv], 1),
        bqkv=np.stack([a[A + "b" + n] for n in qkv], 1),
        bconv=np.stack([a[A + f"b{n}_conv"] for n in qkv], 1),
        bbr=col(np.concatenate([a[A + "bbeta"], a[Fn + "br"]])))
    sw = a[A1 + "short_w"].reshape(3 * P, K1)
    last = dict(
        short=rows(np.concatenate([sw[:, i] for i in range(K1)])),
        wiT=a[F1 + "wi"].T, wo1T=a[F1 + "wo"].T.reshape(FS, P, P).transpose(1, 0, 2).reshape(P, FS * P),
        loraBT=a[F1 + "lora_B"].transpose(0, 2, 1).reshape(E1 * RK, F0))
    late = dict(
        bo=rows(a[A + "bo"]), inT=a[A1 + "in_proj_w"].T,
        shortb=a[A1 + "short_b"].reshape(3, P).T, poles=a[A1 + "log_poles"].reshape(P, NP1),
        res=a[A1 + "residues"], skip=col(a[A1 + "D_skip"]), outT=a[A1 + "out_proj_w"].T,
        pre_w=col(a[A1 + "pre_norm_w"]), post_w=col(a[A1 + "post_norm_w"]),
        l1T=a[A1 + "l1_w"].T, l2T=a[A1 + "l2_w"].T,
        l3T=padded(a[A1 + "l3_w"].T.reshape(3, FT, P).transpose(1, 0, 2).reshape(FT, 3 * P)),
        bi=a[F1 + "bi"].reshape(FS, P).T,
        loraAT=a[F1 + "lora_A"].reshape(E1 * RK, P).T,
        gateT=a[F1 + "gate_w"].T, gateb=col(a[F1 + "gate_b"]), bo1=rows(a[F1 + "bo"]))

    def packed(pack, parts):
        return np.ascontiguousarray(np.concatenate([parts[name].reshape(P, n) for name, n in pack], 1))

    arrays = {
        "x": np.ascontiguousarray(a[A + "x"].reshape(P, T * P)),
        "fixed": packed(FIXED, fixed), "early": packed(EARLY, early), "late": packed(LATE, late),
        "last": packed(LAST, last),
        "w1": np.ascontiguousarray(a[Fn + "W1"].transpose(1, 0, 2).reshape(P, E0 * F0)),
        "w2": np.ascontiguousarray(a[Fn + "W2"].reshape(E0, FS, P, P).transpose(2, 0, 1, 3).reshape(P, E0 * F0)),
    }
    nc = bacc.Bacc("TRN2", target_bir_lowering=False, num_devices=1)
    aps = [nc.dram_tensor(n, v.shape, mybir.dt.float32, kind="ExternalInput").ap() for n, v in arrays.items()]
    out = nc.dram_tensor("out", (P, T * P), mybir.dt.float32, kind="ExternalOutput").ap()
    maps = nc.dram_tensor("maps", (B, C, H, J * HD), mybir.dt.float32, kind="Internal").ap()
    states = nc.dram_tensor("states", (B, C, H, 2, HD * HD // 2), mybir.dt.float32, kind="Internal").ap()
    two_layers(nc, *aps, out, maps, states)
    r = run(nc, [arrays], core_ids=[0])
    return r.results[0]["out"].reshape(B, L, D)
```
